# Optimizing a Trainium2 kernel written in Bass

```python
import numpy as np
import jax
import jax.numpy as jnp

def _softmax(x, axis=-1):
    return jax.nn.softmax(x, axis=axis)

def _gelu(x):
    return jax.nn.gelu(x, approximate=True)

def _silu(x):
    return jax.nn.silu(x)

def _sigmoid(x):
    return jax.nn.sigmoid(x)

def _layernorm(x, axis=-1, eps=1e-05):
    m = jnp.mean(x, axis=axis, keepdims=True)
    v = jnp.var(x, axis=axis, keepdims=True)
    return (x - m) / jnp.sqrt(v + eps)

def _scatter_add(tgt, idx, src, axis=0):
    return tgt.at[idx].add(src)

def _segment_sum(src, seg, n):
    return jax.ops.segment_sum(src, seg, n)
kernel_name = 'mk_gnn_preln_d4_gnn_r32_72e0b2'

def setup_inputs(seed: int=0):
    np.random.seed(seed)
    _w = jnp.asarray

    def _rec_inputs():
        import jax
        import jax.numpy as jnp
        _gk = jax.random.key(seed)
        x = -0.000202 + 1 * jax.random.normal(jax.random.fold_in(_gk, 1), (3125, 128), jnp.float32)
        _s = jax.random.randint(jax.random.fold_in(_gk, 2), (25000,), 0, 3125, jnp.int32)
        _d = jax.random.randint(jax.random.fold_in(_gk, 3), (25000,), 0, 3125, jnp.int32)
        _loop = jnp.arange(3125, dtype=jnp.int32)
        src = jnp.concatenate([_s, _d, _loop])
        dst = jnp.concatenate([_d, _s, _loop])
        _o = jnp.argsort(dst, stable=True)
        src = src[_o]
        dst = dst[_o]
        edge_attr_64 = 0.000189758 + 1.00013 * jax.random.normal(jax.random.fold_in(_gk, 11), (53125, 64), jnp.float32)
        edge_type_20 = jax.random.randint(jax.random.fold_in(_gk, 13), (53125,), 0, 20, jnp.int32)
        edge_weight = jax.random.uniform(jax.random.fold_in(_gk, 14), (53125,), jnp.float32, 0.0, 0.999998)
        return (x, src, dst, edge_attr_64, edge_type_20, edge_weight)
    x, src, dst, edge_attr_64, edge_type_20, edge_weight = _rec_inputs()

    def _L0_gnn_setup():
        import jax, jax.numpy as jnp
        import numpy as np
        NUM_NODES = 50000
        NUM_EDGES = 25000
        INPUT_DIM = 128
        HIDDEN_DIM = 128
        PE_DIM = 64
        key = jax.random.key(seed)
        ks = jax.random.split(key, 12)
        x = jax.random.normal(ks[0], (NUM_NODES, INPUT_DIM), dtype=jnp.float32)
        edge_index = jax.random.randint(ks[1], (2, NUM_EDGES), 0, NUM_NODES, dtype=jnp.int64)
        edge_pe = jax.random.normal(ks[2], (NUM_EDGES, PE_DIM), dtype=jnp.float32)
        s1 = 1.0 / np.sqrt(INPUT_DIM + PE_DIM)
        W1 = jax.random.uniform(ks[3], (INPUT_DIM + PE_DIM, HIDDEN_DIM), minval=-s1, maxval=s1)
        b1 = jax.random.uniform(ks[4], (HIDDEN_DIM,), minval=-s1, maxval=s1)
        s2 = 1.0 / np.sqrt(HIDDEN_DIM)
        W2 = jax.random.uniform(ks[5], (HIDDEN_DIM, HIDDEN_DIM), minval=-s2, maxval=s2)
        b2 = jax.random.uniform(ks[6], (HIDDEN_DIM,), minval=-s2, maxval=s2)
        s3 = 1.0 / np.sqrt(INPUT_DIM + HIDDEN_DIM)
        U1 = jax.random.uniform(ks[7], (INPUT_DIM + HIDDEN_DIM, HIDDEN_DIM), minval=-s3, maxval=s3)
        c1 = jax.random.uniform(ks[8], (HIDDEN_DIM,), minval=-s3, maxval=s3)
        U2 = jax.random.uniform(ks[9], (HIDDEN_DIM, INPUT_DIM), minval=-s2, maxval=s2)
        c2 = jax.random.uniform(ks[10], (INPUT_DIM,), minval=-s2, maxval=s2)
        return {'x': x, 'edge_pe': edge_pe, 'W1': W1, 'b1': b1, 'W2': W2, 'b2': b2, 'U1': U1, 'c1': c1, 'U2': U2, 'c2': c2, 'edge_index': edge_index}
    _L0_gnn_all = _L0_gnn_setup()
    _L0_gnn_in = {k: v for k, v in _L0_gnn_all.items() if k in ('W1', 'b1', 'W2', 'b2', 'U1', 'c1', 'U2', 'c2')}
    del _L0_gnn_all

    def _L1_gnn_setup():
        import jax, jax.numpy as jnp
        import numpy as np
        N = 50000
        E = 25000
        NFEAT = 128
        NOUT = 128
        EPS = 1e-05
        key = jax.random.key(seed)
        ks = jax.random.split(key, 6)
        x = jax.random.normal(ks[0], (N, NFEAT), dtype=jnp.float32)
        edge_index = jax.random.randint(ks[1], (2, E), 0, N)
        edge_weight = jax.random.uniform(ks[2], (E,), dtype=jnp.float32)
        W = jax.random.normal(ks[3], (NFEAT, NOUT), dtype=jnp.float32) / np.sqrt(NFEAT).astype(np.float32)
        b = jnp.zeros((NOUT,), jnp.float32)
        bn_gamma = jnp.ones((NOUT,), jnp.float32)
        bn_beta = jnp.zeros((NOUT,), jnp.float32)
        ln_gamma = jnp.ones((NOUT,), jnp.float32)
        ln_beta = jnp.zeros((NOUT,), jnp.float32)
        return {'x': x, 'edge_index': edge_index, 'edge_weight': edge_weight, 'W': W, 'b': b, 'bn_gamma': bn_gamma, 'bn_beta': bn_beta, 'ln_gamma': ln_gamma, 'ln_beta': ln_beta}
    _L1_gnn_all = _L1_gnn_setup()
    _L1_gnn_in = {k: v for k, v in _L1_gnn_all.items() if k in ('W', 'b', 'bn_gamma', 'bn_beta', 'ln_gamma', 'ln_beta')}
    del _L1_gnn_all

    def _L2_gnn_setup():
        import jax, jax.numpy as jnp
        import numpy as np
        N_NODES = 3125
        N_EDGES = 18750
        N_RELATIONS = 20
        EMBED_DIM = 128
        N_HOPS = 3
        EPS = 1e-12

        def _l2_normalize(x):
            norm = jnp.sqrt(jnp.sum(x * x, axis=1, keepdims=True))
            return x / jnp.maximum(norm, EPS)
        key = jax.random.key(seed)
        k1, k2, k3, k4 = jax.random.split(key, 4)
        ego_embed = jax.random.normal(k1, (N_NODES, EMBED_DIM), dtype=jnp.float32)
        edge_index = jax.random.randint(k2, (2, N_EDGES), 0, N_NODES, dtype=jnp.int64)
        edge_type = jax.random.randint(k3, (N_EDGES,), 0, N_RELATIONS, dtype=jnp.int64)
        relation_embed = jax.random.normal(k4, (N_RELATIONS, EMBED_DIM), dtype=jnp.float32)
        return {'ego_embed': ego_embed, 'edge_index': edge_index, 'edge_type': edge_type, 'relation_embed': relation_embed, 'dropout': 0}
    _L2_gnn_all = _L2_gnn_setup()
    _L2_gnn_in = {k: v for k, v in _L2_gnn_all.items() if k in ('relation_embed',)}
    del _L2_gnn_all

    def _L3_gnn_setup():
        import jax, jax.numpy as jnp
        import numpy as np
        N_NODES = 50000
        EMBED_DIM = 128
        NUM_HEADS = 8
        N_EDGES = 25000
        key = jax.random.key(seed)
        k1, k2, k3, k4 = jax.random.split(key, 4)
        node_states = jax.random.normal(k1, (N_NODES, EMBED_DIM), dtype=jnp.float32)
        edges = jax.random.randint(k2, (2, N_EDGES), 0, N_NODES, dtype=jnp.int64)
        fan_in, fan_out = (EMBED_DIM, 3 * EMBED_DIM)
        g = 1.0 / np.sqrt(2.0) * np.sqrt(6.0 / (fan_in + fan_out))
        qkv_w = jax.random.uniform(k3, (3 * EMBED_DIM, EMBED_DIM), dtype=jnp.float32, minval=-g, maxval=g)
        qkv_b = jnp.zeros((3 * EMBED_DIM,), dtype=jnp.float32)
        g2 = np.sqrt(6.0 / (2 * EMBED_DIM))
        out_w = jax.random.uniform(k4, (EMBED_DIM, EMBED_DIM), dtype=jnp.float32, minval=-g2, maxval=g2)
        out_b = jnp.zeros((EMBED_DIM,), dtype=jnp.float32)
        return {'node_states': node_states, 'edges': edges, 'qkv_w': qkv_w, 'qkv_b': qkv_b, 'out_w': out_w, 'out_b': out_b}
    _L3_gnn_all = _L3_gnn_setup()
    _L3_gnn_in = {k: v for k, v in _L3_gnn_all.items() if k in ('qkv_w', 'qkv_b', 'out_w', 'out_b')}
    del _L3_gnn_all
    return {'x': x, 'src': src, 'dst': dst, 'edge_attr_64': edge_attr_64, 'edge_type_20': edge_type_20, 'edge_weight': edge_weight, 'L0_gnn_W1': _L0_gnn_in['W1'], 'L0_gnn_b1': _L0_gnn_in['b1'], 'L0_gnn_W2': _L0_gnn_in['W2'], 'L0_gnn_b2': _L0_gnn_in['b2'], 'L0_gnn_U1': _L0_gnn_in['U1'], 'L0_gnn_c1': _L0_gnn_in['c1'], 'L0_gnn_U2': _L0_gnn_in['U2'], 'L0_gnn_c2': _L0_gnn_in['c2'], 'L1_gnn_W': _L1_gnn_in['W'], 'L1_gnn_b': _L1_gnn_in['b'], 'L1_gnn_bn_gamma': _L1_gnn_in['bn_gamma'], 'L1_gnn_bn_beta': _L1_gnn_in['bn_beta'], 'L1_gnn_ln_gamma': _L1_gnn_in['ln_gamma'], 'L1_gnn_ln_beta': _L1_gnn_in['ln_beta'], 'L2_gnn_relation_embed': _L2_gnn_in['relation_embed'], 'L3_gnn_qkv_w': _L3_gnn_in['qkv_w'], 'L3_gnn_qkv_b': _L3_gnn_in['qkv_b'], 'L3_gnn_out_w': _L3_gnn_in['out_w'], 'L3_gnn_out_b': _L3_gnn_in['out_b']}

def reference(x, src, dst, edge_attr_64, edge_type_20, edge_weight, L0_gnn_W1, L0_gnn_b1, L0_gnn_W2, L0_gnn_b2, L0_gnn_U1, L0_gnn_c1, L0_gnn_U2, L0_gnn_c2, L1_gnn_W, L1_gnn_b, L1_gnn_bn_gamma, L1_gnn_bn_beta, L1_gnn_ln_gamma, L1_gnn_ln_beta, L2_gnn_relation_embed, L3_gnn_qkv_w, L3_gnn_qkv_b, L3_gnn_out_w, L3_gnn_out_b):
    import jax
    import jax.numpy as jnp

    def _L0_gnn_ref(x, edge_pe, W1, b1, W2, b2, U1, c1, U2, c2, edge_index):
        import jax, jax.numpy as jnp
        import numpy as np
        NUM_NODES = 50000
        NUM_EDGES = 25000
        INPUT_DIM = 128
        HIDDEN_DIM = 128
        PE_DIM = 64
        src, dst = (edge_index[0], edge_index[1])
        msg_in = jnp.concatenate([x[src], edge_pe], axis=-1)
        h = jax.nn.relu(msg_in @ W1 + b1)
        messages = h @ W2 + b2
        aggregated = jax.ops.segment_sum(messages, dst, num_segments=x.shape[0])
        upd_in = jnp.concatenate([x, aggregated], axis=-1)
        u = jax.nn.relu(upd_in @ U1 + c1)
        return u @ U2 + c2

    def _L1_gnn_ref(x, edge_index, edge_weight, W, b, bn_gamma, bn_beta, ln_gamma, ln_beta):
        import jax, jax.numpy as jnp
        import numpy as np
        N = 50000
        E = 25000
        NFEAT = 128
        NOUT = 128
        EPS = 1e-05
        n = x.shape[0]
        row, col = (edge_index[0], edge_index[1])
        loop = jnp.arange(n)
        row = jnp.concatenate([row, loop])
        col = jnp.concatenate([col, loop])
        ew = jnp.concatenate([edge_weight, jnp.ones((n,), x.dtype)])
        deg = jax.ops.segment_sum(ew, col, num_segments=n)
        dinv = jnp.where(deg > 0, jax.lax.rsqrt(deg), 0.0)
        norm = dinv[row] * ew * dinv[col]
        h = x @ W
        msg = h[row] * norm[:, None]
        out = jax.ops.segment_sum(msg, col, num_segments=n) + b
        out = jax.nn.elu(out)
        mu = out.mean(axis=0)
        var = out.var(axis=0)
        out = (out - mu) * jax.lax.rsqrt(var + EPS) * bn_gamma + bn_beta
        m = out.mean(axis=-1, keepdims=True)
        v = out.var(axis=-1, keepdims=True)
        out = (out - m) * jax.lax.rsqrt(v + EPS) * ln_gamma + ln_beta
        return out

    def _L2_gnn_ref(ego_embed, edge_index, edge_type, relation_embed, dropout):
        import jax, jax.numpy as jnp
        import numpy as np
        N_NODES = 3125
        N_EDGES = 18750
        N_RELATIONS = 20
        EMBED_DIM = 128
        N_HOPS = 3
        EPS = 1e-12

        def _l2_normalize(x):
            norm = jnp.sqrt(jnp.sum(x * x, axis=1, keepdims=True))
            return x / jnp.maximum(norm, EPS)
        n_nodes = ego_embed.shape[0]
        head = edge_index[0]
        tail = edge_index[1]
        cnt = jax.ops.segment_sum(jnp.ones(edge_type.shape, dtype=ego_embed.dtype), head, num_segments=n_nodes)
        denom = jnp.maximum(cnt, 1.0)[:, None]
        res = ego_embed
        x = ego_embed
        for _ in range(N_HOPS):
            msg = x[tail] * relation_embed[edge_type]
            agg = jax.ops.segment_sum(msg, head, num_segments=n_nodes)
            x = agg / denom
            x = _l2_normalize(x)
            res = res + x
        return res

    def _L3_gnn_ref(node_states, edges, qkv_w, qkv_b, out_w, out_b):
        import jax, jax.numpy as jnp
        import numpy as np
        N_NODES = 50000
        EMBED_DIM = 128
        NUM_HEADS = 8
        N_EDGES = 25000
        N, E = node_states.shape
        H = NUM_HEADS
        hd = E // H
        src = edges[0]
        tgt = edges[1]
        qkv = node_states @ qkv_w.T + qkv_b
        q, k, v = jnp.split(qkv, 3, axis=1)
        qe = q[tgt]
        ke = k[src]
        ve = v[src]
        scores = (qe * ke).reshape(-1, H, hd).sum(-1) * float(hd) ** (-0.5)
        smax = jax.ops.segment_max(scores, tgt, num_segments=N)
        ex = jnp.exp(scores - smax[tgt])
        denom = jax.ops.segment_sum(ex, tgt, num_segments=N)
        w = ex / denom[tgt]
        msg = (ve.reshape(-1, H, hd) * w[:, :, None]).reshape(-1, E)
        attn_out = jax.ops.segment_sum(msg, tgt, num_segments=N)
        return attn_out @ out_w.T + out_b
    edge_index = jnp.stack([src, dst])
    h = jnp.maximum(_layernorm(x, axis=-1), 0.0)
    x = x + _L0_gnn_ref(h, edge_attr_64, L0_gnn_W1, L0_gnn_b1, L0_gnn_W2, L0_gnn_b2, L0_gnn_U1, L0_gnn_c1, L0_gnn_U2, L0_gnn_c2, edge_index)
    h = jnp.maximum(_layernorm(x, axis=-1), 0.0)
    x = x + _L1_gnn_ref(h, edge_index, edge_weight, L1_gnn_W, L1_gnn_b, L1_gnn_bn_gamma, L1_gnn_bn_beta, L1_gnn_ln_gamma, L1_gnn_ln_beta)
    h = jnp.maximum(_layernorm(x, axis=-1), 0.0)
    x = x + _L2_gnn_ref(h, edge_index, edge_type_20, L2_gnn_relation_embed, 0)
    h = jnp.maximum(_layernorm(x, axis=-1), 0.0)
    x = x + _L3_gnn_ref(h, edge_index, L3_gnn_qkv_w, L3_gnn_qkv_b, L3_gnn_out_w, L3_gnn_out_b)
    return x

_drawn_inputs = setup_inputs


def setup_inputs(seed=0):
    import zlib

    import numpy as np

    out = dict(_drawn_inputs(seed))
    spreads = {'L1_gnn_b': (0.0, 0.729),
     'L1_gnn_bn_gamma': (1.0, 0.2),
     'L1_gnn_bn_beta': (0.0, 0.1),
     'L1_gnn_ln_gamma': (1.0, 0.2),
     'L1_gnn_ln_beta': (0.0, 0.1),
     'L3_gnn_qkv_b': (0.0, 0.1),
     'L3_gnn_out_b': (0.0, 0.1)}
    factors = {'L0_gnn_c1': 3.919}
    for name, (base, spread) in spreads.items():
        noise = np.random.default_rng([zlib.crc32(name.encode()), seed]).standard_normal(out[name].shape)
        drawn = base * np.exp(spread * noise) if base else spread * noise
        out[name] = jnp.asarray(drawn.astype(out[name].dtype))
    for name, factor in factors.items():
        out[name] = (out[name] * factor).astype(out[name].dtype)
    return out
```

```python
from contextlib import ExitStack, contextmanager

import concourse.bass as bass
from concourse import mybir

F32 = mybir.dt.float32
BF16 = mybir.dt.bfloat16
I32 = mybir.dt.int32
ALU = mybir.AluOpType
ACT = mybir.ActivationFunctionType
AX = mybir.AxisListType

P = 128
BIG = 1.0e30
PART = 2
PARTS = 4
PITCH = 136
ROW = 68


def program(nc, x_in, src, dst, attr, etype, eweight, W1, b1, W2, b2, U1, c1, U2, c2, gW, gb, bn_g, bn_b,
            ln_g, ln_b, rel, qkv_w, qkv_b, out_w, out_b, out):
    N, D = x_in.shape
    E, A = attr.shape
    NREL = rel.shape[0]
    WN = 125
    NW = N // WN
    EJ = E // WN
    HEADS = 8
    HD = D // HEADS
    PER_TURN = PART * PARTS
    T = -(-((E + NW * (P - 1)) // P) // PER_TURN) * PER_TURN
    TURNS = T // PER_TURN
    NQ = T // PART
    assert N == NW * WN and E == EJ * WN and D == 128 and A == 64 and NW % 5 == 0

    dst_rows = nc.dram_tensor("dst_rows", (P * T, ROW), F32, kind="Internal").ap()
    src_rows = nc.dram_tensor("src_rows", (P * T, 4), F32, kind="Internal").ap()
    win_tab = nc.dram_tensor("win_tab", (2, T), I32, kind="Internal").ap()
    tables = [nc.dram_tensor(f"table{i}", (N, D), F32, kind="Internal").ap() for i in range(7)]
    tab_p, tab_h, tab_x0, tab_x1, tab_x2, tab_k, tab_v = tables

    by_window = lambda ap: ap.rearrange("(w p) d -> p w d", p=WN)
    by_lane = lambda ap: ap.rearrange("(l t) c -> l t c", l=P)

    outer = ExitStack()

    def keep(name, shape, dt=F32):
        return outer.enter_context(nc.sbuf_tensor(name, shape, dt))

    @contextmanager
    def stage(title):
        snap = nc.snapshot_sems()
        ctx = ExitStack()
        with ctx:
            def sb(name, shape, dt=F32):
                return ctx.enter_context(nc.sbuf_tensor(f"{title}_{name}", shape, dt))
            yield sb, lambda name: nc.alloc_semaphore(f"{title}_{name}")
        nc.clear_and_free_semaphores(nc.allocated_since(snap))
        nc.all_engine_barrier()

    def pipeline(eng, steps):
        furthest = max(ahead for ahead, _ in steps)
        peeled = -(-furthest // PARTS)

        def straight(parts):
            for at in parts:
                for ahead, f in steps:
                    if 0 <= at + ahead < NQ:
                        f((at + ahead) // PARTS, (at + ahead) % PARTS)
        straight(range(-furthest, 0))
        with eng.Fori(0, TURNS - peeled) as g:
            for p in range(PARTS):
                for ahead, f in steps:
                    f(g + (p + ahead) // PARTS, (p + ahead) % PARTS)
        straight(range((TURNS - peeled) * PARTS, NQ))

    def split_parts(link, x, out3, part_f, rest):
        v = nc.vector
        b = [slice(32 * i, 32 * i + 32) for i in range(3)]
        link(v.tensor_copy(out3[:, :], x))
        link(v.tensor_copy(part_f, out3[:, :]))
        link(v.tensor_tensor(rest, x, part_f, ALU.subtract))
        for i in (1, 2):
            link(v.tensor_copy(out3[b[i], :], rest[b[i], :]))
        link(v.tensor_copy(part_f[b[2], :], out3[b[2], :]))
        link(v.tensor_tensor(rest[b[2], :], rest[b[2], :], part_f[b[2], :], ALU.subtract))
        link(v.tensor_copy(out3[b[2], :], rest[b[2], :]))

    class Chain:
        def __init__(self, eng, sem):
            self.eng, self.sem, self.n = eng, sem, 0

        def __call__(self, ins):
            self.n += 1
            ins.then_inc(self.sem, 1)
            self.eng.wait_ge(self.sem, self.n)

    with outer:
        PS = outer.enter_context(nc.psum_tensor("PS", [P, 8 * 512], F32))

        def bank(b, parts, cols, at=0):
            return PS[0:parts, b * 512 + at:b * 512 + at + cols]

        def banks(b, stride, n, parts, cols):
            return PS[0:parts, b * 512:b * 512 + n * stride].rearrange("p (i c) -> p i c", c=stride)[:, :, 0:cols]

        X = keep("X", [WN, NW, D])
        H = keep("H", [WN, NW, D])
        acc = keep("acc", [WN, 2, NW * PITCH])
        accw = [acc[:, k, :].rearrange("p (w c) -> p w c", c=PITCH) for k in range(2)]
        aux = keep("aux", [WN, NW, D])
        ident = keep("ident", [P, P])
        ones = keep("ones", [P, P])
        ones_b = keep("ones_b", [P, P], BF16)
        ident_b = keep("ident_b", [P, P], BF16)
        ident128 = keep("ident128", [P, P], BF16)
        lane_diag = keep("lane_diag", [P, P], BF16)
        lane = keep("lane", [P, 1])
        iota = keep("iota", [P, P])
        iota1 = keep("iota1", [P, P])
        dmeta = keep("dmeta", [P, T + PER_TURN, 4])
        smeta = keep("smeta", [P, T + PER_TURN, 4])
        tmeta = keep("tmeta", [P, T + PER_TURN, 2])
        index = keep("index", [P, T + PER_TURN], I32)
        off_d = keep("off_d", [1, T], I32)
        off_s = keep("off_s", [1, T], I32)
        stat = keep("stat", [WN, 16, NW])
        cnt_d, deg, dinv, denom = (stat[:, i, :] for i in range(4))
        W1a = keep("W1a", [D, D])
        W1b = keep("W1b", [A, D])
        W2s = keep("W2s", [D, D])
        U1a = keep("U1a", [D, D])
        U1b = keep("U1b", [D, D])
        U2s = keep("U2s", [D, D])
        gWs = keep("gWs", [D, D])
        relS = keep("relS", [96, D], BF16)
        qkvT = keep("qkvT", [D, 3 * D])
        outT = keep("outT", [D, D])
        rows1 = keep("rows1", [1, 3, D])
        c1col = keep("c1col", [D, 1])
        vecs = keep("vecs", [WN, 6, D])
        qkvb = keep("qkvb", [1, 3 * D])

        with stage("places") as (sb, sem):
            raw = sb("raw", [P, 4, D])
            relraw = sb("relraw", [96, D])
            relpart = sb("relpart", [96, 2, D])
            keys = sb("keys", [WN, 3, EJ], I32)
            wts = sb("wts", [WN, EJ])
            zeros = sb("zeros", [P, PER_TURN * ROW])
            lower = sb("lower", [P, P])
            wcol = sb("wcol", [WN, NW])
            TQ = T // 4
            tcol = sb("tcol", [TQ, 4])
            onehot = sb("onehot", [WN, NW, EJ], BF16)
            cum = sb("cum", [WN, NW * EJ])
            cumw = cum[:, :].rearrange("p (w j) -> p w j", j=EJ)
            kf = H[:, :, :].rearrange("p w d -> p (w d)")[:, 0:5 * EJ].rearrange("p (i j) -> p i j", i=5)
            ki = sb("ki", [WN, EJ], I32)
            place = sb("place", [WN, 2, EJ], I32)
            small = sb("small", [WN, 10, NW])
            smalli = sb("smalli", [WN, 2, NW], I32)
            wcmp = sb("wcmp", [TQ, 4, NW])
            wval = sb("wval", [TQ, 4])
            wvali = sb("wvali", [TQ, 2, 4], I32)
            meta = sb("meta", [WN, EJ, 8])
            RING = 17
            HALF = [(0, 9), (9, 8)]
            CHUNKS = EJ // RING
            assert CHUNKS * RING == EJ and TQ <= P
            rowbuf = sb("rowbuf", [WN, RING, ROW])
            smallbuf = sb("smallbuf", [WN, RING, 4])
            placebuf = sb("placebuf", [WN, 2, RING], I32)

            loaded, zero_ready, zeroed = sem("loaded"), sem("zero_ready"), sem("zeroed")
            const_made, consts = sem("const_made"), sem("consts")
            weights_in, turned, turned_out = sem("weights_in"), sem("turned"), sem("turned_out")
            counted, summed = sem("counted"), sem("summed")
            wins, wins_out, wins_in = sem("wins"), sem("wins_out"), sem("wins_in")
            dve_link, placed = sem("dve_link"), sem("placed")
            attr_in = [sem(f"attr_in{h}") for h in range(2)]
            scattered = [sem(f"scattered{h}") for h in range(2)]
            staged, staged_seen = sem("staged"), sem("staged_seen")
            smeta_in = sem("smeta_in")

            with nc.Block() as block:
                @block.sync
                def _(sp):
                    sp.wait_ge(zero_ready, 1)
                    for i, a in enumerate((dst, src, etype)):
                        sp.dma_start(keys[:, i, :], a.rearrange("(p j) -> p j", p=WN)).then_inc(loaded, 16)
                    sp.dma_start(wts[:, :], eweight.rearrange("(p j) -> p j", p=WN)).then_inc(loaded, 16)
                    sp.wait_ge(zero_ready, 1)
                    z = zeros[:, :].unsqueeze(1).broadcast_to([P, TURNS, PER_TURN * ROW])
                    sp.dma_start(dst_rows.rearrange("(l g t) c -> l g (t c)", l=P, t=PER_TURN), z).then_inc(zeroed, 16)
                    z = zeros[:, 0:PER_TURN * 4].unsqueeze(1).broadcast_to([P, TURNS, PER_TURN * 4])
                    sp.dma_start(src_rows.rearrange("(l g t) c -> l g (t c)", l=P, t=PER_TURN), z).then_inc(zeroed, 16)
                    plain = [(X[:, :, :], by_window(x_in)), (W1a[:, :], W1[0:D, :]), (W1b[:, :], W1[D:D + A, :]),
                             (W2s[:, :], W2), (U1a[:, :], U1[0:D, :]), (U1b[:, :], U1[D:2 * D, :]), (U2s[:, :], U2),
                             (gWs[:, :], gW), (raw[:, 3, :], out_w),
                             (rows1[:, 0, :], b2.unsqueeze(0)), (rows1[:, 1, :], c2.unsqueeze(0)),
                             (rows1[:, 2, :], b1.unsqueeze(0)), (qkvb[:, :], qkv_b.unsqueeze(0)),
                             (c1col[:, :], c1.unsqueeze(1)),
                             (raw[:, 0:3, :], qkv_w.rearrange("(i p) d -> p i d", p=P))]
                    plain += [(relraw[32 * i:32 * i + NREL, :], rel) for i in range(3)]
                    plain += [(vecs[:, i, :], a.partition_broadcast(WN)) for i, a in enumerate((gb, bn_g, bn_b, ln_g, ln_b, out_b))]
                    for o, a in plain:
                        sp.dma_start(o, a).then_inc(weights_in, 16)
                    sp.wait_ge(wins, 2)
                    for i in range(2):
                        sp.dma_start(win_tab[i].rearrange("(p q) -> p q", q=4), wvali[:, i, :]).then_inc(wins_out, 16)
                    sp.wait_ge(wins_out, 32)
                    for i, o in enumerate((off_d, off_s)):
                        sp.dma_start(o[:, :], win_tab[i:i + 1, :]).then_inc(wins_in, 16)
                    sp.wait_ge(wins_in, 32)
                    at = attr.rearrange("(p j) a -> p j a", p=WN)

                    def load(c):
                        for h, (lo, n) in enumerate(HALF):
                            if not isinstance(c, int):
                                sp.wait_ge(scattered[h], c * (32 * n))
                            sp.dma_start(rowbuf[:, lo:lo + n, 0:A], at[:, bass.ds(c * RING + lo, n), :]).then_inc(attr_in[h], 16)
                    load(0)
                    with sp.Fori(1, CHUNKS) as c:
                        load(c)
                    for h, (lo, n) in enumerate(HALF):
                        sp.wait_ge(scattered[h], 32 * n * CHUNKS)
                    sp.dma_start(smeta[:, 0:T, :], by_lane(src_rows)).then_inc(smeta_in, 16)
                    sp.wait_ge(smeta_in, 16)
                    sp.wait_ge(weights_in, 16 * len(plain))

                @block.gpsimd
                def _(pool):
                    pool.memset(ones[:, :], 1.0).then_inc(const_made, 1)
                    for t in (iota, iota1):
                        pool.iota(t[:, :], [[1, P]], base=0 if t is iota else 1, channel_multiplier=0,
                                  allow_small_or_imprecise_dtypes=True).then_inc(const_made, 1)
                    pool.iota(wcol[:, :], [[1, NW]], base=0, channel_multiplier=0,
                              allow_small_or_imprecise_dtypes=True).then_inc(const_made, 1)
                    pool.iota(tcol[:, :], [[1, 4]], base=0, channel_multiplier=4,
                              allow_small_or_imprecise_dtypes=True).then_inc(const_made, 1)
                    pool.iota(lane[:, :], [[0, 1]], base=0, channel_multiplier=1,
                              allow_small_or_imprecise_dtypes=True).then_inc(const_made, 1)
                    pool.wait_ge(const_made, 6)
                    pool.affine_select(out=ident[:, :], in_=ones[:, :], compare_op=ALU.is_equal, fill=0.0, base=0,
                                       pattern=[[-1, P]], channel_multiplier=1).then_inc(consts, 1)
                    pool.affine_select(out=lower[:, :], in_=ones[:, :], compare_op=ALU.is_gt, fill=0.0, base=0,
                                       pattern=[[1, P]], channel_multiplier=-1).then_inc(consts, 1)
                    pool.wait_ge(zeroed, 32)

                    def send(c):
                        for h, (lo, n) in enumerate(HALF):
                            pool.wait_ge(staged, c * 2 + (h + 1))
                            pool.sem_inc(staged_seen, 1)
                            pool.wait_ge(attr_in[h], c * 16 + 16)
                            pool.sem_inc(staged_seen, 1)
                            for j in range(lo, lo + n):
                                for i, (rows, buf) in enumerate(((dst_rows, rowbuf), (src_rows, smallbuf))):
                                    pool.indirect_dma_start(
                                        out=rows, in_=buf[:, j, :], in_offset=None,
                                        out_offset=bass.IndirectOffsetOnAxis(ap=placebuf[:, i, j:j + 1], axis=0)
                                    ).then_inc(scattered[h], 16)
                    with pool.Fori(0, CHUNKS) as c:
                        send(c)

                @block.scalar
                def _(act):
                    act.wait_ge(turned, 1)
                    act.copy(qkvT[:, :], bank(0, P, 3 * D)).then_inc(turned_out, 1)
                    act.copy(outT[:, :], bank(1, P, D)).then_inc(turned_out, 1)
                    act.wait_ge(placed, 1)

                    def put(c):
                        for h, (lo, n) in enumerate(HALF):
                            if not isinstance(c, int):
                                act.wait_ge(scattered[h], c * (32 * n))
                            j = bass.ds(c * RING + lo, n)
                            act.copy(rowbuf[:, lo:lo + n, A:ROW], meta[:, j, 0:4])
                            act.copy(smallbuf[:, lo:lo + n, :], meta[:, j, 4:8])
                            act.copy(placebuf[:, :, lo:lo + n], place[:, :, j]).then_inc(staged, 1)
                    put(0)
                    with act.Fori(1, CHUNKS) as c:
                        put(c)

                @block.tensor
                def _(pe):
                    pe.wait_ge(consts, 2)
                    pe.wait_ge(weights_in, 16 * 24)
                    for i in range(3):
                        nc.tensor.transpose(bank(0, P, D, i * D), raw[:, i, :], ident[:, :])
                    nc.tensor.transpose(bank(1, P, D), raw[:, 3, :], ident[:, :]).then_inc(turned, 1)
                    for k in range(2):
                        pe.wait_ge(counted, k + 1)
                        nc.tensor.matmul(bank(2 + k, WN, NW), lower[0:WN, 0:WN], small[:, 1, :], start=True, stop=True)
                        nc.tensor.matmul(bank(4 + k, P, NW), ones[0:WN, :], small[:, 1, :], start=True,
                                         stop=True).then_inc(summed, 1)

                @block.vector
                def _(dve):
                    link = Chain(dve, dve_link)
                    v = nc.vector
                    v.memset(relraw[:, :], 0.0)
                    v.memset(zeros[:, :], 0.0).then_inc(zero_ready, 1)
                    link(v.memset(meta[:, :, :], 0.0))
                    for m in (dmeta, smeta, tmeta):
                        link(v.memset(m[:, T:T + PER_TURN, :], 0.0))
                    dve.wait_ge(const_made, 6)
                    dve.wait_ge(loaded, 64)
                    link(v.tensor_copy(meta[:, :, 2], wts[:, :]))
                    link(v.tensor_copy(meta[:, :, 5], keys[:, 2, :]))
                    kv, hi, lo, fix, acc_place = (kf[:, i, :] for i in range(5))
                    for k in range(2):
                        link(v.tensor_copy(kv, keys[:, k, :]))
                        link(v.tensor_copy(meta[:, :, 4 if k == 0 else 0], kv))
                        link(v.tensor_scalar(ki[:, :], kv, 1.0 / WN, None, ALU.mult))
                        link(v.tensor_copy(hi, ki[:, :]))
                        link(v.scalar_tensor_tensor(out=lo, in0=hi, scalar=-float(WN), in1=kv, op0=ALU.mult, op1=ALU.add))
                        for op, bound, sign in ((ALU.is_lt, 0.0, -1.0), (ALU.is_ge, float(WN), 1.0)):
                            link(v.tensor_scalar(fix, lo, bound, sign, op, ALU.mult))
                            link(v.tensor_tensor(hi, hi, fix, ALU.add))
                            link(v.scalar_tensor_tensor(out=lo, in0=fix, scalar=-float(WN), in1=lo, op0=ALU.mult, op1=ALU.add))
                        link(v.tensor_scalar(meta[:, :, 1 if k == 0 else 6], lo, 1.0, None, ALU.add))
                        link(v.tensor_tensor(onehot[:, :, :], hi.unsqueeze(1).broadcast_to([WN, NW, EJ]),
                                             wcol[:, :].unsqueeze(2).broadcast_to([WN, NW, EJ]), ALU.is_equal))
                        flat = onehot[:, :, :].rearrange("p w j -> p (w j)")
                        link(v.tensor_tensor_scan(cum[:, :], flat, flat, 0.0, ALU.add, ALU.max))
                        ends, count, tiles, tcum, off = (small[:, i, :] for i in range(5))
                        link(v.tensor_copy(ends, cumw[:, :, EJ - 1]))
                        link(v.tensor_copy(count[:, 0:1], ends[:, 0:1]))
                        v.tensor_tensor(count[:, 1:NW], ends[:, 1:NW], ends[:, 0:NW - 1], ALU.subtract).then_inc(counted, 1)
                        dve.wait_ge(summed, k + 1)
                        total = bank(4 + k, WN, NW)
                        link(v.tensor_scalar(smalli[:, 0, :], total, float(P - 1), None, ALU.add))
                        link(v.tensor_scalar(smalli[:, 1, :], smalli[:, 0, :], 7, None, ALU.arith_shift_right))
                        link(v.tensor_copy(tiles, smalli[:, 1, :]))
                        link(v.tensor_tensor_scan(tcum, tiles, tiles, 0.0, ALU.add, ALU.max))
                        link(v.tensor_tensor(off, tcum, tiles, ALU.subtract))
                        link(v.tensor_scalar(off, off, float(P), -1.0, ALU.mult, ALU.add))
                        link(v.tensor_tensor(off, off, bank(2 + k, WN, NW), ALU.add))
                        link(v.tensor_tensor(off, off, ends, ALU.subtract))
                        link(v.tensor_tensor(off, off, count, ALU.add))
                        link(v.tensor_tensor(cumw, cumw, off.unsqueeze(2).broadcast_to([WN, NW, EJ]), ALU.add))
                        link(v.tensor_tensor(cumw, cumw, onehot[:, :, :], ALU.mult))
                        link(v.tensor_reduce(acc_place, cumw.rearrange("p w j -> p j w"), AX.X, ALU.add))
                        link(v.tensor_copy(ki[:, :], acc_place))
                        link(v.tensor_scalar(place[:, k, :], ki[:, :], 7, None, ALU.arith_shift_right))
                        link(v.tensor_copy(fix, place[:, k, :]))
                        link(v.scalar_tensor_tensor(out=lo, in0=fix, scalar=-float(P), in1=acc_place, op0=ALU.mult, op1=ALU.add))
                        link(v.scalar_tensor_tensor(out=place[:, k, :], in0=lo, scalar=float(T), in1=fix, op0=ALU.mult,
                                                    op1=ALU.add))
                        link(v.tensor_tensor(wcmp[:, :, :], tcum[0:TQ, :].unsqueeze(1).broadcast_to([TQ, 4, NW]),
                                             tcol[:, :].unsqueeze(2).broadcast_to([TQ, 4, NW]), ALU.is_le))
                        link(v.tensor_reduce(wval[:, :], wcmp[:, :, :], AX.X, ALU.add))
                        v.tensor_scalar(wvali[:, k, :], wval[:, :], float(NW - 1), float(PITCH), ALU.min,
                                        ALU.mult).then_inc(wins, 1)
                    dve.wait_ge(wins, 2)
                    dve.sem_inc(placed, 1)
                    dve.wait_ge(consts, 2)
                    v.tensor_copy(ones_b[:, :], ones[:, :])
                    v.tensor_copy(ident_b[:, :], ident[:, :])
                    v.tensor_scalar(ident128[:, :], ident[:, :], float(P), None, ALU.mult)
                    v.tensor_scalar(lane_diag[:, :], ident[:, :], lane[:, 0:1], None, ALU.mult)
                    dve.wait_ge(weights_in, 16 * 24)
                    hi_, rest = relpart[:, 0, :], relpart[:, 1, :]
                    split_parts(link, relraw[:, :], relS, hi_, rest)

        QM = keep("QM", [WN, NW * PITCH])
        qmw = QM[:, :].rearrange("p (w c) -> p w c", c=PITCH)
        QM3 = keep("QM3", [WN, 3, NW * PITCH], BF16)
        qm3w = [QM3[:, i, :].rearrange("p (w c) -> p w c", c=PITCH) for i in range(3)]
        scores = keep("scores", [P, T, HEADS])

        def over_windows(col):
            return col.unsqueeze(2).broadcast_to([WN, NW, D])

        def over_nodes(row):
            return row.unsqueeze(1).broadcast_to([WN, NW, D])

        mean, var, std, rstd = (stat[:, i, :] for i in range(4, 8))

        def normalise(dve, link, squared, rooted, n, src_, eps=1e-5):
            v = nc.vector
            link(v.tensor_reduce(mean, src_, AX.X, ALU.add))
            link(v.tensor_scalar(mean, mean, 1.0 / D, None, ALU.mult))
            link(v.tensor_tensor(aux[:, :, :], src_, over_windows(mean), ALU.subtract))
            link(v.tensor_tensor(H[:, :, :], aux[:, :, :], aux[:, :, :], ALU.mult))
            link(v.tensor_reduce(var, H[:, :, :], AX.X, ALU.add))
            v.tensor_scalar(var, var, 1.0 / D, eps, ALU.mult, ALU.add).then_inc(squared, 1)
            dve.wait_ge(rooted, n)
            link(v.reciprocal(rstd, std))

        def root(act, squared, rooted, n):
            act.wait_ge(squared, n)
            nc.scalar.activation(std, var, ACT.Sqrt).then_inc(rooted, 1)

        def layernorm_relu(dve, link, squared, rooted, n):
            normalise(dve, link, squared, rooted, n, X[:, :, :])
            link(nc.vector.scalar_tensor_tensor(out=H[:, :, :], in0=aux[:, :, :], scalar=0.0, in1=over_windows(rstd),
                                                op0=ALU.max, op1=ALU.mult))

        BATCH = 5

        def product(title, source, weight, bias, width, prepare, prepare_root, finish, store, at_end=None):
            with stage(title) as (sb, sem):
                st = sb("st", [WN, BATCH, D])
                hT = sb("hT", [D, BATCH, WN])
                spare = sb("spare", [WN, NW, D]) if width > D else None
                ready, squared, rooted, link_sem = sem("ready"), sem("squared"), sem("rooted"), sem("link")
                picked, turned, turned_out = sem("picked"), sem("turned"), sem("turned_out")
                mixed, finished, stored = sem("mixed"), sem("finished"), sem("stored")
                stride = 256 if width <= 256 else 512
                with nc.Block() as block:
                    @block.vector
                    def _(dve):
                        link = Chain(dve, link_sem)
                        prepare(dve, link, squared, rooted)
                        dve.sem_inc(ready, 1)
                        dve.sem_inc(finished, 1)
                        with dve.Fori(0, NW // BATCH) as g:
                            dve.wait_ge(mixed, g + 2)
                            finish(g, banks(3, stride, BATCH, WN, width), spare).then_inc(finished, 1)
                        if at_end:
                            dve.wait_ge(finished, NW // BATCH + 1)
                            at_end(link)

                    @block.scalar
                    def _(act):
                        prepare_root(act, squared, rooted)
                        act.wait_ge(ready, 1)
                        with act.Fori(0, NW // BATCH) as g:
                            act.wait_ge(turned, g + 1)
                            act.copy(st[:, :, :], source[:, bass.ds(g * BATCH, BATCH), :]).then_inc(picked, 1)
                            act.wait_ge(turned, g + 2)
                            act.wait_ge(mixed, g + 1)
                            act.copy(hT[:, :, :], banks(0, 256, BATCH, D, WN)).then_inc(turned_out, 1)

                    @block.tensor
                    def _(pe):
                        pe.sem_inc(turned, 1)
                        pe.sem_inc(mixed, 1)
                        with pe.Fori(0, NW // BATCH) as g:
                            pe.wait_ge(picked, g + 1)
                            for i in range(BATCH):
                                last = nc.tensor.transpose(bank(0, D, WN, i * 256), st[:, i, :], ident[0:WN, 0:WN])
                            last.then_inc(turned, 1)
                            pe.wait_ge(turned_out, g + 1)
                            pe.wait_ge(finished, g + 1)
                            for i in range(BATCH):
                                o = bank(3, WN, width, i * stride)
                                last = nc.tensor.matmul(o, hT[:, i, :], weight, start=True, stop=bias is None)
                                if bias is not None:
                                    last = nc.tensor.matmul(o, ones[0:1, 0:WN], bias, start=False, stop=True)
                            last.then_inc(mixed, 1)

                    @block.sync
                    def _(sp):
                        sp.wait_ge(finished, NW // BATCH + 1)
                        n = 0
                        for o, a in store(spare):
                            sp.dma_start(o, a).then_inc(stored, 16)
                            n += 1
                        if n:
                            sp.wait_ge(stored, 16 * n)

        def edge_pass(kind, table, meta, off, name):
            with stage(name) as (sb, sem):
                MW = 2 if meta is tmeta else 4
                gbuf = sb("gbuf", [P, PARTS, PART, D])
                slot = sb("slot", [P, PARTS, PART], I32)
                mslot = sb("mslot", [P, PARTS, PART, MW])
                S = sb("S", [P, PARTS, PART, WN])
                hm = sb("hm", [P, 2, PART, PITCH])
                lt = sb("lt", [P, 2, PART, P], BF16 if kind in ("rel", "score", "attend") else F32)
                tmp = sb("tmp", [P, 2, PART, D])
                idx_ready, idx_seen, released = sem("idx_ready"), sem("idx_seen"), sem("released")
                landed = [sem(f"landed{p}") for p in range(PARTS)]
                s_ready, turned, turned_out, mixed, used = (sem("s_ready"), sem("turned"), sem("turned_out"),
                                                            sem("mixed"), sem("used"))
                msg_ready, added, made = sem("msg_ready"), sem("added"), sem("made")
                meta_ready = sem("meta_ready")
                index_made, cleared, pe_seen = sem("index_made"), sem("cleared"), sem("pe_seen")
                if kind == "mlp":
                    rows = sb("rows", [P, PARTS, PART, ROW])
                    rows_in = [sem(f"rows_in{p}") for p in range(PARTS)]
                dl = (lambda p: mslot[:, p, :, 2]) if kind == "rel" else (lambda p: mslot[:, p, :, 1])
                AHEAD = PARTS if kind == "mlp" else 0
                if kind == "gcn":
                    rank = sb("rank", [P, 2, PART])
                    rank_written = sem("rank_written")
                    lanes = sb("lanes", [P, PARTS, PART], BF16)
                    below = sb("below", [P, PARTS, PART, P])
                if kind == "rel":
                    toh = sb("toh", [P, PARTS, PART, 3 * 32], BF16)
                if kind in ("score", "attend"):
                    Sb = sb("Sb", [P, PARTS, PART, WN], BF16)
                    product_done = sem("product_done")
                    dsc = sb("dsc", [P, 2, PART, HEADS])
                WIDTH = {"mlp": D + 2, "gcn": D, "rel": D + 1, "attend": D + HEADS}.get(kind)
                rows_free = {"gcn": released, "score": used, "mlp": used, "rel": used, "attend": msg_ready}[kind]
                part = lambda g, p: g * PARTS + p
                tile = lambda g, p: bass.ds(g * PER_TURN + p * PART, PART)
                by_src = by_lane(dst_rows)

                def summed_at(p, cols):
                    return PS[0:WN, (p % 2) * 512:(p % 2) * 512 + PART * 256].rearrange("n (k c) -> n k c", k=PART)[:, :, 0:cols]

                def turned_at(p, parts, cols=P):
                    return PS[0:parts, (2 + p % 2) * 512:(2 + p % 2) * 512 + PART * 256].rearrange("n (k c) -> n k c", k=PART)[:, :, 0:cols]

                def turned_b(p, parts, cols=P):
                    return PS[0:parts, (2 + p % 2) * 512:(2 + p % 2) * 512 + P].bitcast(BF16).rearrange("n (k c) -> n k c", k=PART)[:, :, 0:cols]

                def mixed_at(p, parts, cols):
                    return PS[0:parts, (4 + p % 2) * 512:(4 + p % 2) * 512 + PART * 256].rearrange("n (k c) -> n k c", k=PART)[:, :, 0:cols]

                with nc.Block() as block:
                    @block.gpsimd
                    def _(pool):
                        def gather(g, p):
                            pool.wait_ge(idx_ready, part(g, p) + 1)
                            pool.sem_inc(idx_seen, 1)
                            for k in range(PART):
                                pool.indirect_dma_start(
                                    out=gbuf[:, p, k, :], out_offset=None, in_=table,
                                    in_offset=bass.IndirectOffsetOnAxis(ap=slot[:, p, k:k + 1], axis=0)
                                ).then_inc(landed[p], 16)
                        pipeline(pool, [(0, gather)])

                    @block.sync
                    def _(sp):
                        if kind == "mlp":
                            def fetch(g, p):
                                sp.wait_ge(turned, part(g, p) + 1)
                                sp.wait_ge(meta_ready, part(g, p) + 1)
                                sp.dma_start(rows[:, p, :, :], by_src[:, tile(g, p), :]).then_inc(rows_in[p], 16)
                            pipeline(sp, [(0, fetch)])

                    @block.scalar
                    def _(act):
                        if kind != "gcn":
                            act.sem_inc(turned_out, 2)
                        act.sem_inc(made, 2)
                        if kind == "mlp":
                            act.sem_inc(meta_ready, PARTS)
                        if kind != "mlp":
                            act.wait_ge(index_made, 1)

                        def pick(g, p):
                            act.wait_ge(rows_free, part(g, p) + 1)
                            if kind == "mlp":
                                act.wait_ge(rows_in[p], g * 16 + 16)
                                act.copy(slot[:, p, :], rows[:, p, :, A]).then_inc(idx_ready, 1)
                            else:
                                act.copy(slot[:, p, :], index[:, tile(g, p)]).then_inc(idx_ready, 1)

                        def pick_meta(g, p):
                            act.wait_ge(released, part(g, p) + 1)
                            if kind == "gcn":
                                act.copy(lanes[:, p, :], meta[:, tile(g, p), 1])
                            m = rows[:, p, :, A:ROW] if kind == "mlp" else meta[:, tile(g, p), :]
                            act.copy(mslot[:, p, :, :], m).then_inc(meta_ready, 1)

                        def evacuate(g, p):
                            q = part(g, p)
                            parts = {"mlp": A, "rel": 96}.get(kind, WN)
                            act.wait_ge(turned, q + (1 + AHEAD))
                            act.wait_ge(mixed, q + 1)
                            act.copy(lt[0:parts, p % 2, :, :], turned_at(p, parts) if kind == "mlp" else turned_b(p, parts)).then_inc(turned_out, 1)

                        def relu(g, p):
                            q = part(g, p)
                            act.wait_ge(used, q + 5)
                            act.wait_ge(released, q + 3)
                            nc.scalar.activation(hm[:, p % 2, :, 0:D], tmp[:, p % 2, :, :], ACT.Relu)
                            act.copy(hm[:, p % 2, :, D], mslot[:, p, :, 2]).then_inc(made, 1)

                        def exponent(g, p):
                            q = part(g, p)
                            act.wait_ge(used, q + 5)
                            act.wait_ge(released, q + 3)
                            nc.scalar.activation(hm[:, p % 2, :, D:D + HEADS], dsc[:, p % 2, :, :], ACT.Exp,
                                                 scale=float(HD) ** -0.5).then_inc(made, 1)

                        def save_sorted(g, p):
                            act.wait_ge(mixed, part(g, p) + 3)
                            act.copy(tmeta[:, tile(g, p), :], mixed_at(p, P, 2)).then_inc(used, 1)

                        if kind == "mlp":
                            pipeline(act, [(5, pick), (4, pick_meta), (3, evacuate), (2, relu)])
                        elif kind == "gcn":
                            act.sem_inc(used, 4)
                            pipeline(act, [(4, pick), (4, pick_meta), (1, save_sorted)])
                        elif kind in ("rel", "score"):
                            pipeline(act, [(5, pick), (4, pick_meta), (3, evacuate)])
                        else:
                            pipeline(act, [(5, pick), (4, pick_meta), (3, evacuate), (2, exponent)])

                    @block.tensor
                    def _(pe):
                        pe.sem_inc(mixed, 2)
                        if kind == "mlp":
                            pe.sem_inc(turned, PARTS)
                        if kind != "score":
                            pe.sem_inc(released, 4)
                        if kind == "rel":
                            pe.wait_ge(cleared, 1)

                        def turn(g, p):
                            q = part(g, p)
                            pe.wait_ge(turned_out, q + 1)
                            if kind == "mlp":
                                pe.wait_ge(rows_in[p], g * 16 + 16)
                                pe.sem_inc(pe_seen, 1)
                            else:
                                pe.wait_ge(s_ready, q + 1)
                            for k in range(PART):
                                if kind == "mlp":
                                    last = nc.tensor.transpose(turned_at(p, A)[:, k, :], rows[:, p, k, 0:A], ident[:, :])
                                elif kind == "rel":
                                    last = nc.tensor.transpose(turned_b(p, 96)[:, k, :], toh[:, p, k, :], ident_b[:, :])
                                else:
                                    last = nc.tensor.transpose(turned_b(p, WN)[:, k, :], Sb[:, p, k, :], ident_b[:, :])
                            last.then_inc(turned, 1)

                        def spread_keys(g, p):
                            pe.wait_ge(turned_out, part(g, p) + 1)
                            pe.wait_ge(meta_ready, part(g, p) + 1)
                            for k in range(PART):
                                o = turned_at(p, P)[:, k, :]
                                nc.tensor.matmul(o, lanes[:, p, k:k + 1].broadcast_to([P, P]), ident128[:, :], start=True, stop=False)
                                last = nc.tensor.matmul(o, ones_b[:, :], lane_diag[:, :], start=False, stop=True)
                            last.then_inc(turned, 1)

                        regs = [pe.alloc_register(f"{name}_pe_window{i}") for i in range(PER_TURN)]

                        def mix(g, p):
                            q = part(g, p)
                            if kind in ("score", "attend") and p == 0:
                                pe.load(regs, off[0:1, bass.ds(g * PER_TURN, PER_TURN)])
                            at = [pe.snap(regs[p * PART + k], min_val=0, max_val=(NW - 1) * PITCH) for k in range(PART)] if kind in ("score", "attend") else None
                            pe.wait_ge(turned_out, q + 3)
                            pe.wait_ge(used, q + 3)
                            for k in range(PART):
                                lhs = lt[:, p % 2, k, :]
                                if kind == "mlp":
                                    last = nc.tensor.matmul(mixed_at(p, P, D)[:, k, :], lhs[0:A, :], W1b[:, :], start=True, stop=True)
                                elif kind == "rel":
                                    last = nc.tensor.matmul(mixed_at(p, P, D)[:, k, :], lhs[0:96, :], relS[:, :], start=True, stop=True)
                                elif kind == "gcn":
                                    last = nc.tensor.matmul(mixed_at(p, P, 2)[:, k, :], lhs, mslot[:, p, k, 0:2], start=True, stop=True)
                                else:
                                    cols, skip = (D, 0) if kind == "score" else (HEADS, D)
                                    for i in range(3):
                                        last = nc.tensor.matmul(mixed_at(p, P, cols)[:, k, :], lhs[0:WN, :],
                                                                QM3[:, i, bass.ds(at[k] + skip, cols)], start=(i == 0), stop=(i == 2))
                            last.then_inc(mixed, 1)

                        def total(g, p):
                            q = part(g, p)
                            pe.wait_ge(s_ready, q + 1)
                            pe.wait_ge(added, q * 2 + 2)
                            if kind == "gcn":
                                pe.wait_ge(landed[p], g * 32 + 32)
                            elif kind == "mlp":
                                pe.wait_ge(made, q + 3)
                            elif kind == "rel":
                                pe.wait_ge(used, q + 5)
                            else:
                                pe.wait_ge(msg_ready, q + 5)
                            for k in range(PART):
                                rhs = gbuf[:, p, k, :] if kind == "gcn" else hm[:, p % 2, k, 0:WIDTH]
                                last = nc.tensor.matmul(summed_at(p, WIDTH)[:, k, :], S[:, p, k, :], rhs, start=True, stop=True)
                            last.then_inc(released, 1)

                        pipeline(pe, {"mlp": [(3, turn), (2, mix), (1, total)], "rel": [(3, turn), (2, mix), (1, total)],
                                      "gcn": [(3, spread_keys), (1, mix), (1, total)], "score": [(3, turn), (2, mix)],
                                      "attend": [(3, turn), (2, mix), (1, total)]}[kind])

                    @block.vector
                    def _(dve):
                        v = nc.vector
                        if kind != "mlp":
                            v.tensor_copy(index[:, :], meta[:, :, 0]).then_inc(index_made, 1)
                        v.memset(hm[:, :, :, :], 1.0).then_inc(cleared, 1)
                        v.memset(acc[:, :, :], 0.0).then_inc(cleared, 1)
                        dve.wait_ge(cleared, 2)
                        dve.sem_inc(added, 4)
                        if kind != "gcn":
                            dve.sem_inc(used, 4)
                        if kind == "gcn":
                            dve.sem_inc(turned_out, 2)
                        if kind == "score":
                            dve.sem_inc(released, 4)
                        if kind == "attend":
                            dve.sem_inc(msg_ready, 4)

                        def one_hot(g, p):
                            q = part(g, p)
                            dve.wait_ge(released, q + 1)
                            dve.wait_ge(meta_ready, q + (1 + AHEAD))
                            if kind == "mlp":
                                v.tensor_copy(dmeta[:, tile(g, p), :], mslot[:, p, :, :])
                            if kind == "gcn":
                                for k in range(PART):
                                    last = v.tensor_scalar(S[:, p, k, :], iota1[:, 0:WN], mslot[:, p, k, 1:2],
                                                           mslot[:, p, k, 2:3], ALU.is_equal, ALU.mult)
                            else:
                                last = v.tensor_tensor((Sb if kind == "score" else S)[:, p, :, :], iota1[:, 0:WN].unsqueeze(1).broadcast_to([P, PART, WN]),
                                                       dl(p).unsqueeze(2).broadcast_to([P, PART, WN]), ALU.is_equal)
                            if kind == "attend":
                                last = v.tensor_tensor(Sb[:, p, :, :], iota1[:, 0:WN].unsqueeze(1).broadcast_to([P, PART, WN]),
                                                       dl(p).unsqueeze(2).broadcast_to([P, PART, WN]), ALU.is_equal)
                            if kind == "rel":
                                last = v.tensor_tensor(toh[:, p, :, :].rearrange("e k (c r) -> e k c r", c=3),
                                                       iota[:, 0:32].unsqueeze(1).unsqueeze(1).broadcast_to([P, PART, 3, 32]),
                                                       mslot[:, p, :, 1:2].unsqueeze(2).broadcast_to([P, PART, 3, 32]), ALU.is_equal)
                            last.then_inc(s_ready, 1)

                        def sort_tile(g, p):
                            q = part(g, p)
                            dve.wait_ge(turned, q + 1)
                            for k in range(PART):
                                last = v.tensor_scalar(below[:, p, k, :], turned_at(p, P)[:, k, :], mslot[:, p, k, 3:4], 0.0,
                                                       ALU.is_lt, ALU.add, accum_out=rank[:, p % 2, k:k + 1])
                            last.then_inc(rank_written, 1)
                            dve.wait_ge(rank_written, q + 1)
                            dve.wait_ge(mixed, q + 1)
                            v.tensor_tensor(lt[:, p % 2, :, :], iota[:, :].unsqueeze(1).broadcast_to([P, PART, P]),
                                            rank[:, p % 2, :].unsqueeze(2).broadcast_to([P, PART, P]),
                                            ALU.is_equal).then_inc(turned_out, 1)

                        def add_gathered(g, p):
                            q = part(g, p)
                            dve.wait_ge(mixed, q + 3)
                            dve.wait_ge(landed[p], g * 32 + 32)
                            dve.wait_ge(made, q + 1)
                            v.tensor_tensor(tmp[:, p % 2, :, :], mixed_at(p, P, D), gbuf[:, p, :, :], ALU.add).then_inc(used, 1)

                        def times_relation(g, p):
                            q = part(g, p)
                            dve.wait_ge(mixed, q + 3)
                            dve.wait_ge(landed[p], g * 32 + 32)
                            dve.wait_ge(released, q + 3)
                            v.tensor_tensor(hm[:, p % 2, :, 0:D], mixed_at(p, P, D), gbuf[:, p, :, :], ALU.mult).then_inc(used, 1)

                        def score(g, p):
                            q = part(g, p)
                            dve.wait_ge(mixed, q + 3)
                            dve.wait_ge(landed[p], g * 32 + 32)
                            v.tensor_tensor(tmp[:, p % 2, :, :], mixed_at(p, P, D), gbuf[:, p, :, :], ALU.mult).then_inc(used, 1)
                            dve.wait_ge(used, q + 5)
                            dve.sem_inc(product_done, 1)
                            v.tensor_reduce(scores[:, tile(g, p), :],
                                            tmp[:, p % 2, :, :].rearrange("e k (h d) -> e k h d", h=HEADS),
                                            AX.X, ALU.add).then_inc(released, 1)

                        def shift(g, p):
                            q = part(g, p)
                            dve.wait_ge(mixed, q + 3)
                            dve.wait_ge(made, q + 1)
                            v.tensor_tensor(dsc[:, p % 2, :, :], scores[:, tile(g, p), :], mixed_at(p, P, HEADS),
                                            ALU.subtract).then_inc(used, 1)

                        def weigh(g, p):
                            q = part(g, p)
                            dve.wait_ge(made, q + 3)
                            dve.wait_ge(landed[p], g * 32 + 32)
                            for k in range(PART):
                                last = v.tensor_tensor(
                                    hm[:, p % 2, k, 0:D].rearrange("e (h d) -> e h d", h=HEADS),
                                    gbuf[:, p, k, :].rearrange("e (h d) -> e h d", h=HEADS),
                                    hm[:, p % 2, k, D:D + HEADS].unsqueeze(2).broadcast_to([P, HEADS, HD]), ALU.mult)
                            last.then_inc(msg_ready, 1)

                        regs = [dve.alloc_register(f"{name}_dve_window{i}") for i in range(PER_TURN)]
                        at = []

                        def add_up(g, p):
                            q = part(g, p)
                            if p == 0:
                                dve.load(regs, off[0:1, bass.ds(g * PER_TURN, PER_TURN)])
                                at[:] = [dve.snap(r, min_val=0, max_val=(NW - 1) * PITCH) for r in regs]
                            dve.wait_ge(released, q + 5)
                            for k in range(PART):
                                dve.wait_ge(added, q * 2 + (k + 3))
                                a = acc[:, k, bass.ds(at[p * PART + k], WIDTH)]
                                v.tensor_tensor(a, summed_at(p, WIDTH)[:, k, :], a, ALU.add).then_inc(added, 1)

                        pipeline(dve, {"mlp": [(3, one_hot), (2, add_gathered), (0, add_up)],
                                       "gcn": [(3, one_hot), (2, sort_tile), (0, add_up)],
                                       "rel": [(3, one_hot), (2, times_relation), (0, add_up)],
                                       "score": [(3, one_hot), (1, score)],
                                       "attend": [(3, one_hot), (1, weigh), (2, shift), (0, add_up)]}[kind])

        def greatest_scores():
            SLOTS = 5
            ROUNDS = TURNS // SLOTS
            G = PER_TURN
            R = G * HEADS
            assert ROUNDS * SLOTS == TURNS
            with stage("max") as (sb, sem):
                dsel = sb("dsel", [P, SLOTS, 2, G, HEADS])
                dlT = sb("dlT", [R, SLOTS, P])
                first = sb("first", [R, SLOTS, P + 1])
                reset = sb("reset", [R, SLOTS, P])
                best = sb("best", [R, SLOTS, P])
                mrhs = sb("mrhs", [P, SLOTS, G, HEADS + 1])
                S8 = sb("S8", [P, SLOTS, G, WN])
                gap = sb("gap", [WN, SLOTS, G])
                cand = sb("cand", [WN, SLOTS, G, HEADS])
                picked, turned, dl_out, scanned, back = (sem("picked"), sem("turned"), sem("dl_out"), sem("scanned"),
                                                         sem("back"))
                back_out, s_ready, spread, kept, link_sem = (sem("back_out"), sem("s_ready"), sem("spread"), sem("kept"),
                                                             sem("link"))
                steps_done, cleared, merged, pe_seen = sem("steps_done"), sem("cleared"), sem("merged"), sem("pe_seen")
                link2 = sem("link2")
                turn_of = lambda g, p: g * SLOTS + p

                turned_at = lambda p, at: bank(p % 3, R, P, at)
                spread_at = lambda p: bank(4 + p % 3, WN, G * (HEADS + 1))

                def rounds(eng, steps):
                    for ahead, f in steps:
                        for s in range(ahead):
                            f(0, s)
                    with eng.Fori(0, ROUNDS - 1) as g:
                        for p in range(SLOTS):
                            for ahead, f in steps:
                                f(g + (p + ahead) // SLOTS, (p + ahead) % SLOTS)
                    for p in range(SLOTS):
                        for ahead, f in steps:
                            if p + ahead < SLOTS:
                                f(ROUNDS - 1, p + ahead)

                with nc.Block() as block:
                    @block.scalar
                    def _(act):
                        def pick(g, p):
                            act.wait_ge(kept, turn_of(g, p) + 1)
                            t = bass.ds(turn_of(g, p) * G, G)
                            act.copy(dsel[:, p, 0, :, :], scores[:, t, :])
                            act.copy(dsel[:, p, 1, :, :], tmeta[:, t, 1].unsqueeze(2).broadcast_to([P, G, HEADS])).then_inc(picked, 1)

                        def lanes(g, p):
                            act.wait_ge(turned, turn_of(g, p) + 1)
                            act.copy(dlT[:, p, :], turned_at(p, P)).then_inc(dl_out, 1)

                        def unturn(g, p):
                            act.wait_ge(back, turn_of(g, p) + 1)
                            act.copy(mrhs[:, p, :, 0:HEADS], bank(3, P, R).rearrange("e (t h) -> e t h", t=G)).then_inc(back_out, 1)
                        act.wait_ge(cleared, 4)
                        act.sem_inc(back_out, 1)
                        rounds(act, [(3, pick), (2, lanes), (1, unturn)])

                    @block.tensor
                    def _(pe):
                        def turn(g, p):
                            pe.wait_ge(scanned, turn_of(g, p) + 1)
                            pe.sem_inc(pe_seen, 1)
                            pe.wait_ge(picked, turn_of(g, p) + 1)
                            pe.sem_inc(pe_seen, 1)
                            nc.tensor.transpose(turned_at(p, 0), dsel[:, p, 0, :, :].rearrange("e t h -> e (t h)"), ident[:, :])
                            nc.tensor.transpose(turned_at(p, P), dsel[:, p, 1, :, :].rearrange("e t h -> e (t h)"),
                                                ident[:, :]).then_inc(turned, 1)

                        def turn_back(g, p):
                            pe.wait_ge(back_out, turn_of(g, p) + 1)
                            pe.sem_inc(pe_seen, 1)
                            pe.wait_ge(scanned, turn_of(g, p) + 3)
                            pe.sem_inc(pe_seen, 1)
                            nc.tensor.transpose(bank(3, P, R), best[:, p, :], ident[0:R, 0:R]).then_inc(back, 1)

                        def spread_out(g, p):
                            pe.wait_ge(back_out, turn_of(g, p) + 2)
                            pe.wait_ge(kept, turn_of(g, p) + 4)
                            pe.wait_ge(s_ready, turn_of(g, p) + 1)
                            for i in range(G):
                                last = nc.tensor.matmul(spread_at(p)[:, i * (HEADS + 1):(i + 1) * (HEADS + 1)], S8[:, p, i, :],
                                                        mrhs[:, p, i, :], start=True, stop=True)
                            last.then_inc(spread, 1)
                        rounds(pe, [(3, turn), (0, spread_out), (1, turn_back)])

                    @block.vector
                    def _(dve):
                        v = nc.vector
                        v.memset(first[:, :, :], 1.0).then_inc(cleared, 1)
                        v.memset(mrhs[:, :, :, :], 1.0).then_inc(cleared, 1)
                        for k in range(2):
                            v.memset(acc[:, k, :], -BIG).then_inc(cleared, 1)
                        dve.wait_ge(cleared, 4)
                        dve.sem_inc(kept, SLOTS)

                        def scan(g, p):
                            t = turn_of(g, p)
                            dve.wait_ge(dl_out, t + 1)
                            v.tensor_tensor(first[:, p, 1:P], dlT[:, p, 1:P], dlT[:, p, 0:P - 1], ALU.not_equal).then_inc(link_sem, 1)
                            dve.wait_ge(link_sem, t * 3 + 1)
                            v.tensor_scalar(reset[:, p, :], first[:, p, 0:P], -BIG, None, ALU.mult).then_inc(link_sem, 1)
                            dve.wait_ge(link_sem, t * 3 + 2)
                            v.tensor_tensor_scan(best[:, p, :], reset[:, p, :], turned_at(p, 0), 0.0, ALU.add,
                                                 ALU.max).then_inc(link_sem, 1)
                            dve.wait_ge(link_sem, t * 3 + 3)
                            v.tensor_tensor(best[:, p, :], best[:, p, :], first[:, p, 1:P + 1], ALU.mult).then_inc(scanned, 1)

                        def one_hot(g, p):
                            v.tensor_tensor(S8[:, p, :, :], iota1[:, 0:WN].unsqueeze(1).broadcast_to([P, G, WN]),
                                            dsel[:, p, 1, :, 0].unsqueeze(2).broadcast_to([P, G, WN]), ALU.is_equal).then_inc(s_ready, 1)

                        regs = [dve.alloc_register(f"max_window{i}") for i in range(G)]

                        def keep_best(g, p):
                            t = turn_of(g, p)
                            dve.load(regs, off_d[0:1, bass.ds(t * G, G)])
                            at = [dve.snap(r, min_val=0, max_val=(NW - 1) * PITCH) for r in regs]
                            dve.wait_ge(spread, t + 1)
                            m = spread_at(p).rearrange("n (t c) -> n t c", t=G)
                            v.tensor_scalar(gap[:, p, :], m[:, :, HEADS], 1.0, -1.0, ALU.min, ALU.add).then_inc(steps_done, 1)
                            dve.wait_ge(steps_done, t * 2 + 1)
                            v.scalar_tensor_tensor(out=cand[:, p, :, :], in0=gap[:, p, :].unsqueeze(2).broadcast_to([WN, G, HEADS]),
                                                   scalar=BIG, in1=m[:, :, 0:HEADS], op0=ALU.mult, op1=ALU.add).then_inc(steps_done, 1)
                            dve.wait_ge(steps_done, t * 2 + 2)
                            for i in range(G):
                                dve.wait_ge(merged, t * G + (i + 1))
                                a = acc[:, i % 2, bass.ds(at[i] + D, HEADS)]
                                last = v.tensor_tensor(a, cand[:, p, i, :], a, ALU.max).then_inc(merged, 1)
                            dve.wait_ge(merged, t * G + (G + 2))
                            dve.sem_inc(kept, 1)

                        dve.sem_inc(merged, 2)
                        dve.sem_inc(scanned, 2)
                        rounds(dve, [(2, scan), (2, one_hot), (0, keep_best)])
                        dve.wait_ge(merged, T + 2)
                        link = Chain(dve, link2)
                        link(v.tensor_tensor(qmw[:, :, D:D + HEADS], accw[0][:, :, D:D + HEADS], accw[1][:, :, D:D + HEADS], ALU.max))
                        split_columns(link, D, D + HEADS, aux[:, :, 0:HEADS])

        def first_norm(dve, link, squared, rooted):
            layernorm_relu(dve, link, squared, rooted, 1)

        product("rows0", H, W1a[:, :], rows1[:, 2, :], D, first_norm, lambda act, s, r: root(act, s, r, 1),
                lambda g, rows, _: nc.vector.tensor_copy(aux[:, bass.ds(g * BATCH, BATCH), :], rows),
                lambda _: [(by_window(tab_p), aux[:, :, :])])
        edge_pass("mlp", tab_p, None, off_d, "layer0")

        with stage("update0") as (sb, sem):
            agg = sb("agg", [WN, BATCH, D + 2])
            st = sb("st", [WN, BATCH, D])
            aT, hT, uT = (sb(n, [D, BATCH, WN]) for n in ("aT", "hT", "uT"))
            cT = sb("cT", [1, BATCH, WN])
            agg_ready, st_ready, turned, a_out, h_out = (sem("agg_ready"), sem("st_ready"), sem("turned"), sem("a_out"),
                                                         sem("h_out"))
            mixed2, mixed2_out, mixed1, relu_out, mixed0, added = (sem("mixed2"), sem("mixed2_out"), sem("mixed1"),
                                                                   sem("relu_out"), sem("mixed0"), sem("added"))
            keyed = sem("keyed")
            with nc.Block() as block:
                @block.vector
                def _(dve):
                    v = nc.vector
                    v.tensor_scalar(dmeta[:, 0:T, 3], dmeta[:, 0:T, 1], float(P), lane[:, 0:1], ALU.mult, ALU.add).then_inc(keyed, 1)
                    dve.sem_inc(added, 1)
                    with dve.Fori(0, NW // BATCH) as g:
                        w = bass.ds(g * BATCH, BATCH)
                        dve.wait_ge(added, g + 1)
                        v.tensor_tensor(agg[:, :, :], accw[0][:, w, 0:D + 2], accw[1][:, w, 0:D + 2], ALU.add).then_inc(agg_ready, 1)
                        dve.wait_ge(agg_ready, g + 1)
                        v.tensor_copy(deg[:, w], agg[:, :, D])
                        dve.wait_ge(turned, g + 1)
                        v.tensor_copy(hT[:, :, :], banks(3, 256, BATCH, D, WN)).then_inc(h_out, 1)
                        dve.wait_ge(mixed0, g + 1)
                        v.tensor_tensor(X[:, w, :], X[:, w, :], banks(0, 256, BATCH, WN, D), ALU.add).then_inc(added, 1)

                @block.scalar
                def _(act):
                    with act.Fori(0, NW // BATCH) as g:
                        act.wait_ge(added, g + 1)
                        act.copy(st[:, :, :], H[:, bass.ds(g * BATCH, BATCH), :]).then_inc(st_ready, 1)
                        act.wait_ge(turned, g + 1)
                        act.copy(aT[:, :, :], banks(0, 256, BATCH, D, WN)).then_inc(a_out, 1)
                        act.copy(cT[:, :, :], banks(6, 128, BATCH, 1, WN)).then_inc(a_out, 1)
                        act.wait_ge(mixed2, g + 1)
                        act.copy(aT[:, :, :], banks(0, 256, BATCH, D, WN)).then_inc(mixed2_out, 1)
                        act.wait_ge(mixed1, g + 1)
                        nc.scalar.activation(uT[:, :, :], banks(3, 256, BATCH, D, WN), ACT.Relu, bias=c1col[:, 0:1]).then_inc(relu_out, 1)

                @block.tensor
                def _(pe):
                    with pe.Fori(0, NW // BATCH) as g:
                        pe.wait_ge(agg_ready, g + 1)
                        pe.wait_ge(st_ready, g + 1)
                        for i in range(BATCH):
                            nc.tensor.transpose(bank(0, D, WN, i * 256), agg[:, i, 0:D], ident[0:WN, 0:WN])
                            nc.tensor.transpose(bank(3, D, WN, i * 256), st[:, i, :], ident[0:WN, 0:WN])
                            last = nc.tensor.transpose(bank(6, 1, WN, i * 128), agg[:, i, D + 1:D + 2], ident[0:WN, 0:WN])
                        last.then_inc(turned, 1)
                        pe.wait_ge(a_out, g * 2 + 2)
                        for i in range(BATCH):
                            nc.tensor.matmul(bank(0, D, WN, i * 256), W2s[:, :], aT[:, i, :], start=True, stop=False)
                            last = nc.tensor.matmul(bank(0, D, WN, i * 256), rows1[:, 0, :], cT[:, i, :], start=False, stop=True)
                        last.then_inc(mixed2, 1)
                        pe.wait_ge(mixed2_out, g + 1)
                        pe.wait_ge(h_out, g + 1)
                        for i in range(BATCH):
                            nc.tensor.matmul(bank(3, D, WN, i * 256), U1a[:, :], hT[:, i, :], start=True, stop=False)
                            last = nc.tensor.matmul(bank(3, D, WN, i * 256), U1b[:, :], aT[:, i, :], start=False, stop=True)
                        last.then_inc(mixed1, 1)
                        pe.wait_ge(relu_out, g + 1)
                        for i in range(BATCH):
                            nc.tensor.matmul(bank(0, WN, D, i * 256), uT[:, i, :], U2s[:, :], start=True, stop=False)
                            last = nc.tensor.matmul(bank(0, WN, D, i * 256), ones[0:1, 0:WN], rows1[:, 1, :], start=False, stop=True)
                        last.then_inc(mixed0, 1)

        def second_norm(dve, link, squared, rooted):
            v = nc.vector
            layernorm_relu(dve, link, squared, rooted, 1)
            link(v.tensor_scalar(deg, deg, 1.0, None, ALU.add))
            v.tensor_scalar(var, deg, 1.0e-30, None, ALU.max).then_inc(squared, 1)
            dve.wait_ge(rooted, 2)
            link(v.reciprocal(rstd, std))
            link(v.scalar_tensor_tensor(out=dinv, in0=deg, scalar=0.0, in1=rstd, op0=ALU.is_gt, op1=ALU.mult))

        product("rows1", H, gWs[:, :], None, D, second_norm, lambda act, s, r: (root(act, s, r, 1), root(act, s, r, 2)),
                lambda g, rows, _: nc.vector.tensor_tensor(
                    aux[:, bass.ds(g * BATCH, BATCH), :], rows,
                    dinv[:, bass.ds(g * BATCH, BATCH)].unsqueeze(2).broadcast_to([WN, BATCH, D]), ALU.mult),
                lambda _: [(by_window(tab_h), aux[:, :, :])])
        edge_pass("gcn", tab_h, dmeta, off_d, "layer1")

        with stage("update1") as (sb, sem):
            link_sem, squared, rooted, summed = sem("link"), sem("squared"), sem("rooted"), sem("summed")
            elu_in, elu_out, col_in, stored, done = sem("elu_in"), sem("elu_out"), sem("col_in"), sem("stored"), sem("done")
            brow = sb("brow", [WN, 4, D])
            with nc.Block() as block:
                @block.vector
                def _(dve):
                    link = Chain(dve, link_sem)
                    v = nc.vector
                    h, a = H[:, :, :], aux[:, :, :]
                    link(v.tensor_tensor(h, accw[0][:, :, 0:D], accw[1][:, :, 0:D], ALU.add))
                    link(v.tensor_tensor(h, h, a, ALU.add))
                    link(v.tensor_tensor(h, h, over_windows(dinv), ALU.mult))
                    link(v.tensor_tensor(h, h, over_nodes(vecs[:, 0, :]), ALU.add))
                    v.tensor_scalar(a, h, 0.0, None, ALU.min).then_inc(elu_in, 1)
                    dve.wait_ge(elu_out, 1)
                    link(v.scalar_tensor_tensor(out=h, in0=h, scalar=0.0, in1=a, op0=ALU.max, op1=ALU.add))
                    v.tensor_scalar(h, h, -1.0, None, ALU.add).then_inc(col_in, 1)
                    dve.wait_ge(summed, 1)
                    link(v.tensor_scalar(brow[:, 0, :], bank(0, WN, D), 1.0 / N, None, ALU.mult))
                    link(v.tensor_tensor(a, h, over_nodes(brow[:, 0, :]), ALU.subtract))
                    v.tensor_tensor(h, a, a, ALU.mult).then_inc(col_in, 1)
                    dve.wait_ge(summed, 2)
                    v.tensor_scalar(brow[:, 1, :], bank(1, WN, D), 1.0 / N, 1e-5, ALU.mult, ALU.add).then_inc(squared, 1)
                    dve.wait_ge(rooted, 1)
                    link(v.reciprocal(brow[:, 3, :], brow[:, 2, :]))
                    link(v.tensor_tensor(brow[:, 3, :], brow[:, 3, :], vecs[:, 1, :], ALU.mult))
                    link(v.tensor_tensor(a, a, over_nodes(brow[:, 3, :]), ALU.mult))
                    link(v.tensor_tensor(a, a, over_nodes(vecs[:, 2, :]), ALU.add))
                    normalise(dve, link, squared, rooted, 2, a)
                    link(v.tensor_tensor(a, a, over_windows(rstd), ALU.mult))
                    link(v.tensor_tensor(a, a, over_nodes(vecs[:, 3, :]), ALU.mult))
                    link(v.tensor_tensor(a, a, over_nodes(vecs[:, 4, :]), ALU.add))
                    link(v.tensor_tensor(X[:, :, :], X[:, :, :], a, ALU.add))
                    layernorm_relu(dve, link, squared, rooted, 3)
                    link(v.tensor_tensor(X[:, :, :], X[:, :, :], H[:, :, :], ALU.add))
                    dve.sem_inc(done, 1)

                @block.scalar
                def _(act):
                    act.wait_ge(elu_in, 1)
                    nc.scalar.activation(aux[:, :, :], aux[:, :, :], ACT.Exp).then_inc(elu_out, 1)
                    act.wait_ge(squared, 1)
                    nc.scalar.activation(brow[:, 2, :], brow[:, 1, :], ACT.Sqrt).then_inc(rooted, 1)
                    root(act, squared, rooted, 2)
                    root(act, squared, rooted, 3)

                @block.tensor
                def _(pe):
                    for k in range(2):
                        pe.wait_ge(col_in, k + 1)
                        for w in range(NW):
                            last = nc.tensor.matmul(bank(k, WN, D), ones[0:WN, 0:WN], H[:, w, :], start=(w == 0), stop=(w == NW - 1))
                        last.then_inc(summed, 1)

                @block.sync
                def _(sp):
                    sp.wait_ge(done, 1)
                    sp.dma_start(by_window(tab_x0), H[:, :, :]).then_inc(stored, 16)
                    sp.wait_ge(stored, 16)

        def hop_end(title, last_hop, table_out):
            with stage(title) as (sb, sem):
                link_sem, squared, rooted, stored, done = sem("link"), sem("squared"), sem("rooted"), sem("stored"), sem("done")
                with nc.Block() as block:
                    @block.vector
                    def _(dve):
                        link = Chain(dve, link_sem)
                        v = nc.vector
                        a = aux[:, :, :]
                        link(v.tensor_tensor(a, accw[0][:, :, 0:D], accw[1][:, :, 0:D], ALU.add))
                        link(v.tensor_tensor(denom, accw[0][:, :, D], accw[1][:, :, D], ALU.add))
                        link(v.tensor_scalar(denom, denom, 1.0, None, ALU.max))
                        link(v.reciprocal(rstd, denom))
                        link(v.tensor_tensor(a, a, over_windows(rstd), ALU.mult))
                        link(v.tensor_tensor(H[:, :, :], a, a, ALU.mult))
                        v.tensor_reduce(var, H[:, :, :], AX.X, ALU.add).then_inc(squared, 1)
                        dve.wait_ge(rooted, 1)
                        link(v.tensor_scalar(std, std, 1e-12, None, ALU.max))
                        link(v.reciprocal(rstd, std))
                        link(v.tensor_tensor(a, a, over_windows(rstd), ALU.mult))
                        dve.sem_inc(done, 1)
                        v.tensor_tensor(X[:, :, :], X[:, :, :], a, ALU.add)

                    @block.scalar
                    def _(act):
                        root(act, squared, rooted, 1)

                    @block.sync
                    def _(sp):
                        if not last_hop:
                            sp.wait_ge(done, 1)
                            sp.dma_start(by_window(table_out), aux[:, :, :]).then_inc(stored, 16)
                            sp.wait_ge(stored, 16)

        for i, (t_in, t_out) in enumerate(((tab_x0, tab_x1), (tab_x1, tab_x2), (tab_x2, None))):
            edge_pass("rel", t_in, smeta, off_s, f"hop{i}")
            hop_end(f"end{i}", i == 2, t_out)

        def split_qkv(g, rows, spare):
            w = bass.ds(g * BATCH, BATCH)
            nc.vector.tensor_copy(qmw[:, w, 0:D], rows[:, :, 0:D])
            nc.vector.tensor_copy(aux[:, w, :], rows[:, :, D:2 * D])
            return nc.vector.tensor_copy(spare[:, w, :], rows[:, :, 2 * D:3 * D])

        def split_columns(link, lo, hi, rest):
            v = nc.vector
            q = qmw[:, :, lo:hi]
            link(v.tensor_copy(qm3w[0][:, :, lo:hi], q))
            link(v.tensor_tensor(rest, q, qm3w[0][:, :, lo:hi], ALU.subtract))
            link(v.tensor_copy(qm3w[1][:, :, lo:hi], rest))
            link(v.tensor_tensor(rest, rest, qm3w[1][:, :, lo:hi], ALU.subtract))
            v.tensor_copy(qm3w[2][:, :, lo:hi], rest)

        X3 = H[:, :, :]
        product("qkv", H, qkvT[:, :], qkvb[:, :], 3 * D, first_norm, lambda act, s, r: root(act, s, r, 1), split_qkv,
                lambda spare: [(by_window(tab_k), aux[:, :, :]), (by_window(tab_v), spare[:, :, :])],
                lambda link: split_columns(link, 0, D, X3))
        edge_pass("score", tab_k, tmeta, off_d, "scores")
        greatest_scores()
        edge_pass("attend", tab_v, tmeta, off_d, "attend")

        def last_rows(dve, link, squared, rooted):
            v = nc.vector
            link(v.tensor_tensor(aux[:, :, :], accw[0][:, :, 0:D], accw[1][:, :, 0:D], ALU.add))
            den = H[:, :, 0:HEADS]
            link(v.tensor_tensor(den, accw[0][:, :, D:D + HEADS], accw[1][:, :, D:D + HEADS], ALU.add))
            link(v.tensor_scalar(den, den, 1.0e-30, None, ALU.max))
            link(v.reciprocal(den, den))
            for h in range(HEADS):
                a = aux[:, :, h * HD:(h + 1) * HD]
                link(v.tensor_tensor(a, a, den[:, :, h:h + 1].broadcast_to([WN, NW, HD]), ALU.mult))
            link(v.tensor_tensor(X[:, :, :], X[:, :, :], over_nodes(vecs[:, 5, :]), ALU.add))

        def add_rows(g, rows, _):
            w = bass.ds(g * BATCH, BATCH)
            return nc.vector.tensor_tensor(X[:, w, :], X[:, w, :], rows, ALU.add)

        product("output", aux, outT[:, :], None, D, last_rows, lambda act, s, r: None, add_rows,
                lambda _: [(by_window(out), X[:, :, :])])


_INS = ['x', 'src', 'dst', 'edge_attr_64', 'edge_type_20', 'edge_weight', 'L0_gnn_W1', 'L0_gnn_b1', 'L0_gnn_W2',
        'L0_gnn_b2', 'L0_gnn_U1', 'L0_gnn_c1', 'L0_gnn_U2', 'L0_gnn_c2', 'L1_gnn_W', 'L1_gnn_b', 'L1_gnn_bn_gamma',
        'L1_gnn_bn_beta', 'L1_gnn_ln_gamma', 'L1_gnn_ln_beta', 'L2_gnn_relation_embed', 'L3_gnn_qkv_w',
        'L3_gnn_qkv_b', 'L3_gnn_out_w', 'L3_gnn_out_b']


def kernel(**inputs):
    import numpy as _np
    import concourse.bacc as _bacc
    from concourse import mybir as _mybir
    from concourse.bass_utils import run_bass_kernel_spmd as _run

    nc = _bacc.Bacc("TRN2", target_bir_lowering=False, num_devices=1)
    arrays, args = {}, []
    for name in _INS:
        a = _np.ascontiguousarray(inputs[name])
        arrays[f"in_{name}_dram"] = a
        args.append(nc.dram_tensor(f"in_{name}_dram", a.shape, _mybir.dt.from_np(a.dtype), kind="ExternalInput").ap())
    args.append(nc.dram_tensor("out_0_dram", (3125, 128), _mybir.dt.float32, kind="ExternalOutput").ap())
    program(nc, *args)
    r = _run(nc, [arrays], core_ids=[0])
    return r.results[0]["out_0_dram"]
```

```python
from contextlib import ExitStack, contextmanager

import concourse.bass as bass
from concourse import mybir

F32 = mybir.dt.float32
BF16 = mybir.dt.bfloat16
I32 = mybir.dt.int32
ALU = mybir.AluOpType
ACT = mybir.ActivationFunctionType
AX = mybir.AxisListType

P = 128
BIG = 1.0e30
PART = 2
PARTS = 10
MSGS = 5
MAXG = 8
PITCH = 136
ROW = 68


def program(nc, x_in, src, dst, attr, etype, eweight, W1, b1, W2, b2, U1, c1, U2, c2, gW, gb, bn_g, bn_b,
            ln_g, ln_b, rel, qkv_w, qkv_b, out_w, out_b, out):
    N, D = x_in.shape
    E, A = attr.shape
    NREL = rel.shape[0]
    WN = 125
    NW = N // WN
    EJ = E // WN
    HEADS = 8
    HD = D // HEADS
    PER_TURN = PART * PARTS
    T = -(-((E + NW * (P - 1)) // P) // PER_TURN) * PER_TURN
    TURNS = T // PER_TURN
    NQ = T // PART
    assert N == NW * WN and E == EJ * WN and D == 128 and A == 64 and NW % 5 == 0

    dst_rows = nc.dram_tensor("dst_rows", (P * T, ROW), F32, kind="Internal").ap()
    win_tab = nc.dram_tensor("win_tab", (2, T), I32, kind="Internal").ap()
    tables = [nc.dram_tensor(f"table{i}", (N, D), F32, kind="Internal").ap() for i in range(7)]
    tab_p, tab_h, tab_x0, tab_x1, tab_x2, tab_k, tab_v = tables

    by_window = lambda ap: ap.rearrange("(w p) d -> p w d", p=WN)
    by_lane = lambda ap: ap.rearrange("(l t) c -> l t c", l=P)

    outer = ExitStack()

    def keep(name, shape, dt=F32):
        return outer.enter_context(nc.sbuf_tensor(name, shape, dt))

    @contextmanager
    def stage(title):
        snap = nc.snapshot_sems()
        ctx = ExitStack()
        with ctx:
            def sb(name, shape, dt=F32):
                return ctx.enter_context(nc.sbuf_tensor(f"{title}_{name}", shape, dt))
            yield sb, lambda name: nc.alloc_semaphore(f"{title}_{name}")
        nc.clear_and_free_semaphores(nc.allocated_since(snap))
        nc.all_engine_barrier()

    def pipeline(eng, steps):
        furthest = max(ahead for ahead, _ in steps)
        peeled = -(-furthest // PARTS)

        def straight(parts):
            for at in parts:
                for ahead, f in steps:
                    if 0 <= at + ahead < NQ:
                        f((at + ahead) // PARTS, (at + ahead) % PARTS)
        straight(range(-furthest, 0))
        with eng.Fori(0, TURNS - peeled) as g:
            for p in range(PARTS):
                for ahead, f in steps:
                    f(g + (p + ahead) // PARTS, (p + ahead) % PARTS)
        straight(range((TURNS - peeled) * PARTS, NQ))

    def split_parts(link, x, out3, part_f, rest):
        v = nc.vector
        b = [slice(32 * i, 32 * i + 32) for i in range(3)]
        link(v.tensor_copy(out3[:, :], x))
        link(v.tensor_copy(part_f, out3[:, :]))
        link(v.tensor_tensor(rest, x, part_f, ALU.subtract))
        for i in (1, 2):
            link(v.tensor_copy(out3[b[i], :], rest[b[i], :]))
        link(v.tensor_copy(part_f[b[2], :], out3[b[2], :]))
        link(v.tensor_tensor(rest[b[2], :], rest[b[2], :], part_f[b[2], :], ALU.subtract))
        link(v.tensor_copy(out3[b[2], :], rest[b[2], :]))

    class Chain:
        def __init__(self, eng, sem):
            self.eng, self.sem, self.n = eng, sem, 0

        def __call__(self, ins):
            self.n += 1
            ins.then_inc(self.sem, 1)
            self.eng.wait_ge(self.sem, self.n)

    with outer:
        PS = outer.enter_context(nc.psum_tensor("PS", [P, 8 * 512], F32))

        def bank(b, parts, cols, at=0):
            return PS[0:parts, b * 512 + at:b * 512 + at + cols]

        def banks(b, stride, n, parts, cols):
            return PS[0:parts, b * 512:b * 512 + n * stride].rearrange("p (i c) -> p i c", c=stride)[:, :, 0:cols]

        X = keep("X", [WN, NW, D])
        H = keep("H", [WN, NW, D])
        acc = keep("acc", [WN, 2, NW * PITCH])
        accw = [acc[:, k, :].rearrange("p (w c) -> p w c", c=PITCH) for k in range(2)]
        aux = keep("aux", [WN, NW, D])
        ident = keep("ident", [P, P])
        ones = keep("ones", [P, P])
        ones_b = keep("ones_b", [P, P], BF16)
        ident_b = keep("ident_b", [P, P], BF16)
        ident128 = keep("ident128", [P, P], BF16)
        lane_diag = keep("lane_diag", [P, P], BF16)
        lane = keep("lane", [P, 1])
        iota = keep("iota", [P, P])
        iota1 = keep("iota1", [P, P])
        dmeta = keep("dmeta", [P, T + PER_TURN, 4])
        smeta = keep("smeta", [P, T + PER_TURN, 4])
        tmeta = keep("tmeta", [P, T + PER_TURN, 2])
        index = keep("index", [P, T + PER_TURN], I32)
        off_d = keep("off_d", [1, T], I32)
        off_s = keep("off_s", [1, T], I32)
        stat = keep("stat", [WN, 16, NW])
        cnt_d, deg, dinv, denom = (stat[:, i, :] for i in range(4))
        W1a = keep("W1a", [D, D])
        W1b = keep("W1b", [A, D])
        W2s = keep("W2s", [D, D])
        U1a = keep("U1a", [D, D])
        U1b = keep("U1b", [D, D])
        U2s = keep("U2s", [D, D])
        gWs = keep("gWs", [D, D])
        relS = keep("relS", [96, D], BF16)
        qkvT = keep("qkvT", [D, 3 * D])
        outT = keep("outT", [D, D])
        rows1 = keep("rows1", [1, 3, D])
        c1col = keep("c1col", [D, 1])
        vecs = keep("vecs", [WN, 6, D])
        qkvb = keep("qkvb", [1, 3 * D])

        with stage("places") as (sb, sem):
            raw = sb("raw", [P, 4, D])
            relraw = sb("relraw", [96, D])
            relpart = sb("relpart", [96, 2, D])
            keys = sb("keys", [WN, 3, EJ], I32)
            wts = sb("wts", [WN, EJ])
            ZT = 8
            zeros = sb("zeros", [P, ZT * ROW])
            lower = sb("lower", [P, P])
            wcol = sb("wcol", [WN, NW])
            TQ = T // 4
            tcol = sb("tcol", [TQ, 4])
            onehot = sb("onehot", [WN, NW, EJ], BF16)
            cum_all = sb("cum", [P, NW * EJ])
            cum = cum_all[0:WN, :]
            cumw = cum[:, :].rearrange("p (w j) -> p w j", j=EJ)
            kf = H[:, :, :].rearrange("p w d -> p (w d)")[:, 0:5 * EJ].rearrange("p (i j) -> p i j", i=5)
            ki = sb("ki", [WN, EJ], I32)
            place = sb("place", [WN, 2, EJ], I32)
            small = sb("small", [WN, 10, NW])
            smalli = sb("smalli", [WN, 2, NW], I32)
            wcmp = sb("wcmp", [TQ, 4, NW])
            wval = sb("wval", [TQ, 4])
            wvali = sb("wvali", [TQ, 2, 4], I32)
            meta = sb("meta", [WN, EJ, 9])
            RING = 17
            HALF = [(0, 9), (9, 8)]
            CHUNKS = EJ // RING
            assert CHUNKS * RING == EJ and TQ <= P
            rowbuf = sb("rowbuf", [WN, RING, ROW])
            smallbuf = sb("smallbuf", [WN, RING, 5])
            placebuf = sb("placebuf", [WN, RING], I32)
            tiles_b = sb("tiles_b", [WN, T], BF16)
            zeros_b = sb("zeros_b", [WN, T], BF16)
            SLOTS = HALF[0][1]
            LAG = HALF[1][1]
            CODE = T + 3 * P
            assert T <= 512 and SLOTS * CODE <= NW * EJ and NREL <= 32 and N <= 4096
            spots = onehot[:, :, :].rearrange("p w j -> p (w j)")[:, 0:SLOTS * CODE].rearrange("p (s c) -> p s c", c=CODE)
            CODE_BANK = (6, 7, 0)

            loaded, zero_ready, zeroed = sem("loaded"), sem("zero_ready"), sem("zeroed")
            const_made, consts = sem("const_made"), sem("consts")
            weights_in, turned, turned_out = sem("weights_in"), sem("turned"), sem("turned_out")
            counted, summed = sem("counted"), sem("summed")
            wins, wins_out, wins_in = sem("wins"), sem("wins_out"), sem("wins_in")
            dve_link, placed = sem("dve_link"), sem("placed")
            attr_in = [sem(f"attr_in{h}") for h in range(2)]
            scattered = [sem(f"scattered{h}") for h in range(2)]
            staged, staged_seen = sem("staged"), sem("staged_seen")
            spotted, spots_used, decoded_in = sem("spotted"), sem("spots_used"), sem("decoded_in")

            with nc.Block() as block:
                @block.sync
                def _(sp):
                    sp.wait_ge(zero_ready, 1)
                    for i, a in enumerate((dst, src, etype)):
                        sp.dma_start(keys[:, i, :], a.rearrange("(p j) -> p j", p=WN)).then_inc(loaded, 16)
                    sp.dma_start(wts[:, :], eweight.rearrange("(p j) -> p j", p=WN)).then_inc(loaded, 16)
                    sp.wait_ge(zero_ready, 1)
                    z = zeros[:, :].unsqueeze(1).broadcast_to([P, T // ZT, ZT * ROW])
                    sp.dma_start(dst_rows.rearrange("(l g t) c -> l g (t c)", l=P, t=ZT), z).then_inc(zeroed, 16)
                    plain = [(X[:, :, :], by_window(x_in)), (W1a[:, :], W1[0:D, :]), (W1b[:, :], W1[D:D + A, :]),
                             (W2s[:, :], W2), (U1a[:, :], U1[0:D, :]), (U1b[:, :], U1[D:2 * D, :]), (U2s[:, :], U2),
                             (gWs[:, :], gW), (raw[:, 3, :], out_w),
                             (rows1[:, 0, :], b2.unsqueeze(0)), (rows1[:, 1, :], c2.unsqueeze(0)),
                             (rows1[:, 2, :], b1.unsqueeze(0)), (qkvb[:, :], qkv_b.unsqueeze(0)),
                             (c1col[:, :], c1.unsqueeze(1)),
                             (raw[:, 0:3, :], qkv_w.rearrange("(i p) d -> p i d", p=P))]
                    plain += [(relraw[32 * i:32 * i + NREL, :], rel) for i in range(3)]
                    plain += [(vecs[:, i, :], a.partition_broadcast(WN)) for i, a in enumerate((gb, bn_g, bn_b, ln_g, ln_b, out_b))]
                    for o, a in plain:
                        sp.dma_start(o, a).then_inc(weights_in, 16)
                    sp.wait_ge(wins, 2)
                    for i in range(2):
                        sp.dma_start(win_tab[i].rearrange("(p q) -> p q", q=4), wvali[:, i, :]).then_inc(wins_out, 16)
                    sp.wait_ge(wins_out, 32)
                    for i, o in enumerate((off_d, off_s)):
                        sp.dma_start(o[:, :], win_tab[i:i + 1, :]).then_inc(wins_in, 16)
                    sp.wait_ge(wins_in, 32)
                    at = attr.rearrange("(p j) a -> p j a", p=WN)

                    def load(c):
                        for h, (lo, n) in enumerate(HALF):
                            if not isinstance(c, int):
                                sp.wait_ge(scattered[h], c * (16 * n))
                            sp.dma_start(rowbuf[:, lo:lo + n, 0:A], at[:, bass.ds(c * RING + lo, n), :]).then_inc(attr_in[h], 16)
                    load(0)
                    with sp.Fori(1, CHUNKS) as c:
                        load(c)
                    for h, (lo, n) in enumerate(HALF):
                        sp.wait_ge(scattered[h], 16 * n * CHUNKS)
                    sp.wait_ge(weights_in, 16 * len(plain))

                @block.gpsimd
                def _(pool):
                    pool.memset(ones[:, :], 1.0).then_inc(const_made, 1)
                    for t in (iota, iota1):
                        pool.iota(t[:, :], [[1, P]], base=0 if t is iota else 1, channel_multiplier=0,
                                  allow_small_or_imprecise_dtypes=True).then_inc(const_made, 1)
                    pool.iota(wcol[:, :], [[1, NW]], base=0, channel_multiplier=0,
                              allow_small_or_imprecise_dtypes=True).then_inc(const_made, 1)
                    pool.iota(tcol[:, :], [[1, 4]], base=0, channel_multiplier=4,
                              allow_small_or_imprecise_dtypes=True).then_inc(const_made, 1)
                    pool.iota(lane[:, :], [[0, 1]], base=0, channel_multiplier=1,
                              allow_small_or_imprecise_dtypes=True).then_inc(const_made, 1)
                    pool.iota(tiles_b[:, :], [[1, T]], base=-(T // 2), channel_multiplier=0,
                              allow_small_or_imprecise_dtypes=True).then_inc(const_made, 1)
                    pool.wait_ge(const_made, 7)
                    pool.affine_select(out=ident[:, :], in_=ones[:, :], compare_op=ALU.is_equal, fill=0.0, base=0,
                                       pattern=[[-1, P]], channel_multiplier=1).then_inc(consts, 1)
                    pool.affine_select(out=lower[:, :], in_=ones[:, :], compare_op=ALU.is_gt, fill=0.0, base=0,
                                       pattern=[[1, P]], channel_multiplier=-1).then_inc(consts, 1)
                    pool.wait_ge(zeroed, 16)

                    def send(c):
                        for h, (lo, n) in enumerate(HALF):
                            pool.wait_ge(staged, c * 2 + (h + 1))
                            pool.sem_inc(staged_seen, 1)
                            pool.wait_ge(attr_in[h], c * 16 + 16)
                            pool.sem_inc(staged_seen, 1)
                            for j in range(lo, lo + n):
                                pool.indirect_dma_start(
                                    out=dst_rows, in_=rowbuf[:, j, :], in_offset=None,
                                    out_offset=bass.IndirectOffsetOnAxis(ap=placebuf[:, j:j + 1], axis=0)
                                ).then_inc(scattered[h], 16)
                    with pool.Fori(0, CHUNKS) as c:
                        send(c)

                @block.scalar
                def _(act):
                    act.wait_ge(turned, 1)
                    act.copy(qkvT[:, :], bank(0, P, 3 * D)).then_inc(turned_out, 1)
                    act.copy(outT[:, :], bank(1, P, D)).then_inc(turned_out, 1)
                    act.wait_ge(placed, 1)

                    def put(c):
                        for h, (lo, n) in enumerate(HALF):
                            if not isinstance(c, int):
                                act.wait_ge(scattered[h], c * (16 * n))
                                act.wait_ge(spotted, c * RING + (lo + n - RING))
                            j = bass.ds(c * RING + lo, n)
                            act.copy(rowbuf[:, lo:lo + n, A:ROW], meta[:, j, 0:4])
                            act.copy(smallbuf[:, lo:lo + n, :], meta[:, j, 4:9])
                            act.copy(placebuf[:, lo:lo + n], place[:, 0, j]).then_inc(staged, 1)
                    put(0)
                    with act.Fori(1, CHUNKS) as c:
                        put(c)

                @block.tensor
                def _(pe):
                    pe.wait_ge(consts, 2)
                    pe.wait_ge(weights_in, 16 * 24)
                    for i in range(3):
                        nc.tensor.transpose(bank(0, P, D, i * D), raw[:, i, :], ident[:, :])
                    nc.tensor.transpose(bank(1, P, D), raw[:, 3, :], ident[:, :]).then_inc(turned, 1)
                    for k in range(2):
                        pe.wait_ge(counted, k + 1)
                        nc.tensor.matmul(bank(2 + k, WN, NW), lower[0:WN, 0:WN], small[:, 1, :], start=True, stop=True)
                        nc.tensor.matmul(bank(4 + k, P, NW), ones[0:WN, :], small[:, 1, :], start=True,
                                         stop=True).then_inc(summed, 1)
                    pe.wait_ge(turned_out, 2)
                    pe.wait_ge(placed, 1)
                    for i in range(3):
                        nc.tensor.matmul(bank(CODE_BANK[i], P, T), zeros_b[:, 0:P], zeros_b[:, :], start=True, stop=False)
                    with pe.Fori(0, CHUNKS) as c:
                        for s in range(RING):
                            pe.wait_ge(spotted, c * RING + (s + 1))
                            spot = spots[:, s % SLOTS, :]
                            for i in range(3):
                                last = nc.tensor.matmul(bank(CODE_BANK[i], P, T), spot[:, T + i * P:T + (i + 1) * P],
                                                        spot[:, 0:T], start=False, stop=False)
                            last.then_inc(spots_used, 1)
                    for i in range(3):
                        last = nc.tensor.matmul(bank(CODE_BANK[i], P, T), zeros_b[:, 0:P], zeros_b[:, :], start=False, stop=True)
                    last.then_inc(decoded_in, 1)

                @block.vector
                def _(dve):
                    link = Chain(dve, dve_link)
                    v = nc.vector
                    v.memset(relraw[:, :], 0.0)
                    v.memset(zeros_b[:, :], 0.0)
                    v.memset(zeros[:, :], 0.0).then_inc(zero_ready, 1)
                    link(v.memset(meta[:, :, :], 0.0))
                    for m in (dmeta, smeta, tmeta):
                        link(v.memset(m[:, T:T + PER_TURN, :], 0.0))
                    link(v.memset(smeta[:, 0:T, 3], 0.0))
                    dve.wait_ge(const_made, 7)
                    dve.wait_ge(loaded, 64)
                    link(v.tensor_copy(meta[:, :, 2], wts[:, :]))
                    kv, hi, lo, fix, acc_place = (kf[:, i, :] for i in range(5))
                    for k in range(2):
                        link(v.tensor_copy(kv, keys[:, k, :]))
                        if k == 1:
                            link(v.tensor_copy(meta[:, :, 0], kv))
                        link(v.tensor_scalar(ki[:, :], kv, 1.0 / WN, None, ALU.mult))
                        link(v.tensor_copy(hi, ki[:, :]))
                        link(v.scalar_tensor_tensor(out=lo, in0=hi, scalar=-float(WN), in1=kv, op0=ALU.mult, op1=ALU.add))
                        for op, bound, sign in ((ALU.is_lt, 0.0, -1.0), (ALU.is_ge, float(WN), 1.0)):
                            link(v.tensor_scalar(fix, lo, bound, sign, op, ALU.mult))
                            link(v.tensor_tensor(hi, hi, fix, ALU.add))
                            link(v.scalar_tensor_tensor(out=lo, in0=fix, scalar=-float(WN), in1=lo, op0=ALU.mult, op1=ALU.add))
                        if k == 0:
                            link(v.tensor_scalar(meta[:, :, 1], lo, 1.0, None, ALU.add))
                        else:
                            link(v.tensor_scalar(fix, lo, 1.0, 32.0, ALU.add, ALU.mult))
                            link(v.tensor_copy(lo, keys[:, 2, :]))
                            link(v.tensor_tensor(fix, fix, lo, ALU.add))
                            link(v.tensor_copy(lo, keys[:, 0, :]))
                            link(v.scalar_tensor_tensor(out=fix, in0=fix, scalar=4096.0, in1=lo, op0=ALU.mult, op1=ALU.add))
                            link(v.tensor_copy(place[:, 1, :], fix))
                            for i, (shift, mask) in enumerate(((16, 255), (8, 255), (0, 255))):
                                link(v.tensor_scalar(ki[:, :], place[:, 1, :], shift, mask, ALU.arith_shift_right, ALU.bitwise_and))
                                link(v.tensor_copy(meta[:, :, 6 + i], ki[:, :]))
                        link(v.tensor_tensor(onehot[:, :, :], hi.unsqueeze(1).broadcast_to([WN, NW, EJ]),
                                             wcol[:, :].unsqueeze(2).broadcast_to([WN, NW, EJ]), ALU.is_equal))
                        flat = onehot[:, :, :].rearrange("p w j -> p (w j)")
                        link(v.tensor_tensor_scan(cum[:, :], flat, flat, 0.0, ALU.add, ALU.max))
                        ends, count, tiles, tcum, off = (small[:, i, :] for i in range(5))
                        link(v.tensor_copy(ends, cumw[:, :, EJ - 1]))
                        link(v.tensor_copy(count[:, 0:1], ends[:, 0:1]))
                        v.tensor_tensor(count[:, 1:NW], ends[:, 1:NW], ends[:, 0:NW - 1], ALU.subtract).then_inc(counted, 1)
                        dve.wait_ge(summed, k + 1)
                        total = bank(4 + k, WN, NW)
                        link(v.tensor_scalar(smalli[:, 0, :], total, float(P - 1), None, ALU.add))
                        link(v.tensor_scalar(smalli[:, 1, :], smalli[:, 0, :], 7, None, ALU.arith_shift_right))
                        link(v.tensor_copy(tiles, smalli[:, 1, :]))
                        link(v.tensor_tensor_scan(tcum, tiles, tiles, 0.0, ALU.add, ALU.max))
                        link(v.tensor_tensor(off, tcum, tiles, ALU.subtract))
                        link(v.tensor_scalar(off, off, float(P), -1.0, ALU.mult, ALU.add))
                        link(v.tensor_tensor(off, off, bank(2 + k, WN, NW), ALU.add))
                        link(v.tensor_tensor(off, off, ends, ALU.subtract))
                        link(v.tensor_tensor(off, off, count, ALU.add))
                        link(v.tensor_tensor(cumw, cumw, off.unsqueeze(2).broadcast_to([WN, NW, EJ]), ALU.add))
                        link(v.tensor_tensor(cumw, cumw, onehot[:, :, :], ALU.mult))
                        link(v.tensor_reduce(acc_place, cumw.rearrange("p w j -> p j w"), AX.X, ALU.add))
                        link(v.tensor_copy(ki[:, :], acc_place))
                        link(v.tensor_scalar(place[:, k, :], ki[:, :], 7, None, ALU.arith_shift_right))
                        link(v.tensor_copy(fix, place[:, k, :]))
                        link(v.scalar_tensor_tensor(out=lo, in0=fix, scalar=-float(P), in1=acc_place, op0=ALU.mult, op1=ALU.add))
                        if k == 0:
                            link(v.scalar_tensor_tensor(out=place[:, 0, :], in0=lo, scalar=float(T), in1=fix, op0=ALU.mult,
                                                        op1=ALU.add))
                        else:
                            link(v.tensor_copy(meta[:, :, 5], lo))
                            link(v.tensor_scalar(meta[:, :, 4], fix, float(T // 2), None, ALU.subtract))
                        link(v.tensor_tensor(wcmp[:, :, :], tcum[0:TQ, :].unsqueeze(1).broadcast_to([TQ, 4, NW]),
                                             tcol[:, :].unsqueeze(2).broadcast_to([TQ, 4, NW]), ALU.is_le))
                        link(v.tensor_reduce(wval[:, :], wcmp[:, :, :], AX.X, ALU.add))
                        v.tensor_scalar(wvali[:, k, :], wval[:, :], float(NW - 1), float(PITCH), ALU.min,
                                        ALU.mult).then_inc(wins, 1)
                    dve.wait_ge(wins, 2)
                    dve.sem_inc(placed, 1)
                    dve.sem_inc(spots_used, LAG)
                    with dve.Fori(0, CHUNKS) as c:
                        for h, (lo_, n) in enumerate(HALF):
                            dve.wait_ge(staged, c * 2 + (h + 1))
                            for s in range(lo_, lo_ + n):
                                dve.wait_ge(spots_used, c * RING + (s + 1))
                                spot = spots[:, s % SLOTS, :]
                                v.tensor_scalar(spot[:, 0:T], tiles_b[:, :], smallbuf[:, s, 0:1], None, ALU.is_equal)
                                for i in range(3):
                                    last = v.tensor_scalar(spot[:, T + i * P:T + (i + 1) * P], iota[0:WN, :], smallbuf[:, s, 1:2],
                                                           smallbuf[:, s, 2 + i:3 + i], ALU.is_equal, ALU.mult)
                                last.then_inc(spotted, 1)
                    dve.wait_ge(consts, 2)
                    v.tensor_copy(ones_b[:, :], ones[:, :])
                    v.tensor_copy(ident_b[:, :], ident[:, :])
                    v.tensor_scalar(ident128[:, :], ident[:, :], float(P), None, ALU.mult)
                    v.tensor_scalar(lane_diag[:, :], ident[:, :], lane[:, 0:1], None, ALU.mult)
                    dve.wait_ge(weights_in, 16 * 24)
                    hi_, rest = relpart[:, 0, :], relpart[:, 1, :]
                    split_parts(link, relraw[:, :], relS, hi_, rest)
                    code, codei = cum_all[:, 0:T], cum_all[:, T:2 * T].bitcast(I32)
                    parti = cum_all[:, 2 * T:3 * T].bitcast(I32)
                    dve.wait_ge(decoded_in, 1)
                    link(v.tensor_copy(code, bank(CODE_BANK[2], P, T)))
                    for i, unit in ((1, 256.0), (0, 65536.0)):
                        link(v.scalar_tensor_tensor(out=code, in0=bank(CODE_BANK[i], P, T), scalar=unit, in1=code,
                                                    op0=ALU.mult, op1=ALU.add))
                    link(v.tensor_copy(codei, code))
                    for i, shift, mask in ((0, 0, 4095), (1, 12, 31), (2, 17, 127)):
                        link(v.tensor_scalar(parti, codei, shift, mask, ALU.arith_shift_right, ALU.bitwise_and))
                        link(v.tensor_copy(smeta[:, 0:T, i], parti))

        QM = keep("QM", [WN, NW * PITCH])
        qmw = QM[:, :].rearrange("p (w c) -> p w c", c=PITCH)
        QM3 = keep("QM3", [WN, 3, NW * PITCH], BF16)
        qm3w = [QM3[:, i, :].rearrange("p (w c) -> p w c", c=PITCH) for i in range(3)]
        scores = keep("scores", [P, T, HEADS])

        def over_windows(col):
            return col.unsqueeze(2).broadcast_to([WN, NW, D])

        def over_nodes(row):
            return row.unsqueeze(1).broadcast_to([WN, NW, D])

        mean, var, std, rstd = (stat[:, i, :] for i in range(4, 8))

        def normalise(dve, link, squared, rooted, n, src_, eps=1e-5):
            v = nc.vector
            link(v.tensor_reduce(mean, src_, AX.X, ALU.add))
            link(v.tensor_scalar(mean, mean, 1.0 / D, None, ALU.mult))
            link(v.tensor_tensor(aux[:, :, :], src_, over_windows(mean), ALU.subtract))
            link(v.tensor_tensor(H[:, :, :], aux[:, :, :], aux[:, :, :], ALU.mult))
            link(v.tensor_reduce(var, H[:, :, :], AX.X, ALU.add))
            v.tensor_scalar(var, var, 1.0 / D, eps, ALU.mult, ALU.add).then_inc(squared, 1)
            dve.wait_ge(rooted, n)
            link(v.reciprocal(rstd, std))

        def root(act, squared, rooted, n):
            act.wait_ge(squared, n)
            nc.scalar.activation(std, var, ACT.Sqrt).then_inc(rooted, 1)

        def layernorm_relu(dve, link, squared, rooted, n):
            normalise(dve, link, squared, rooted, n, X[:, :, :])
            link(nc.vector.scalar_tensor_tensor(out=H[:, :, :], in0=aux[:, :, :], scalar=0.0, in1=over_windows(rstd),
                                                op0=ALU.max, op1=ALU.mult))

        BATCH = 5

        def product(title, source, weight, bias, width, prepare, prepare_root, finish, store, at_end=None):
            with stage(title) as (sb, sem):
                st = sb("st", [WN, BATCH, D])
                hT = sb("hT", [D, BATCH, WN])
                spare = sb("spare", [WN, NW, D]) if width > D else None
                ready, squared, rooted, link_sem = sem("ready"), sem("squared"), sem("rooted"), sem("link")
                picked, turned, turned_out = sem("picked"), sem("turned"), sem("turned_out")
                mixed, finished, stored = sem("mixed"), sem("finished"), sem("stored")
                stride = 256 if width <= 256 else 512
                with nc.Block() as block:
                    @block.vector
                    def _(dve):
                        link = Chain(dve, link_sem)
                        prepare(dve, link, squared, rooted)
                        dve.sem_inc(ready, 1)
                        dve.sem_inc(finished, 1)
                        with dve.Fori(0, NW // BATCH) as g:
                            dve.wait_ge(mixed, g + 2)
                            finish(g, banks(3, stride, BATCH, WN, width), spare).then_inc(finished, 1)
                        if at_end:
                            dve.wait_ge(finished, NW // BATCH + 1)
                            at_end(link)

                    @block.scalar
                    def _(act):
                        prepare_root(act, squared, rooted)
                        act.wait_ge(ready, 1)
                        with act.Fori(0, NW // BATCH) as g:
                            act.wait_ge(turned, g + 1)
                            act.copy(st[:, :, :], source[:, bass.ds(g * BATCH, BATCH), :]).then_inc(picked, 1)
                            act.wait_ge(turned, g + 2)
                            act.wait_ge(mixed, g + 1)
                            act.copy(hT[:, :, :], banks(0, 256, BATCH, D, WN)).then_inc(turned_out, 1)

                    @block.tensor
                    def _(pe):
                        pe.sem_inc(turned, 1)
                        pe.sem_inc(mixed, 1)
                        with pe.Fori(0, NW // BATCH) as g:
                            pe.wait_ge(picked, g + 1)
                            for i in range(BATCH):
                                last = nc.tensor.transpose(bank(0, D, WN, i * 256), st[:, i, :], ident[0:WN, 0:WN])
                            last.then_inc(turned, 1)
                            pe.wait_ge(turned_out, g + 1)
                            pe.wait_ge(finished, g + 1)
                            for i in range(BATCH):
                                o = bank(3, WN, width, i * stride)
                                last = nc.tensor.matmul(o, hT[:, i, :], weight, start=True, stop=bias is None)
                                if bias is not None:
                                    last = nc.tensor.matmul(o, ones[0:1, 0:WN], bias, start=False, stop=True)
                            last.then_inc(mixed, 1)

                    @block.sync
                    def _(sp):
                        sp.wait_ge(finished, NW // BATCH + 1)
                        n = 0
                        for o, a in store(spare):
                            sp.dma_start(o, a).then_inc(stored, 16)
                            n += 1
                        if n:
                            sp.wait_ge(stored, 16 * n)

        def edge_pass(kind, table, meta, off, name):
            with stage(name) as (sb, sem):
                MW = 2 if meta is tmeta else 4
                gbuf = sb("gbuf", [P, PARTS, PART, D])
                slot = sb("slot", [P, PARTS, PART], I32)
                mslot = sb("mslot", [P, PARTS, PART, MW])
                S = sb("S", [P, PARTS, PART, WN])
                hm = sb("hm", [P, MSGS, PART, PITCH])
                lt = sb("lt", [P, 2, PART, P], BF16 if kind in ("rel", "score", "attend") else F32)
                tmp = sb("tmp", [P, MSGS, PART, D])
                idx_ready, idx_seen, released = sem("idx_ready"), sem("idx_seen"), sem("released")
                landed = [sem(f"landed{p}") for p in range(PARTS)]
                s_ready, turned, turned_out, mixed, used = (sem("s_ready"), sem("turned"), sem("turned_out"),
                                                            sem("mixed"), sem("used"))
                msg_ready, added, made = sem("msg_ready"), sem("added"), sem("made")
                meta_ready = sem("meta_ready")
                index_made, cleared, pe_seen = sem("index_made"), sem("cleared"), sem("pe_seen")
                if kind == "mlp":
                    rows = sb("rows", [P, PARTS, PART, ROW])
                    rows_in = [sem(f"rows_in{p}") for p in range(PARTS)]
                dl = (lambda p: mslot[:, p, :, 2]) if kind == "rel" else (lambda p: mslot[:, p, :, 1])
                AHEAD = PARTS if kind == "mlp" else 0
                if kind == "gcn":
                    rank = sb("rank", [P, 2, PART])
                    rank_written = sem("rank_written")
                    lanes = sb("lanes", [P, PARTS, PART], BF16)
                    below = sb("below", [P, PARTS, PART, P])
                if kind == "rel":
                    toh = sb("toh", [P, PARTS, PART, 3 * 32], BF16)
                if kind in ("score", "attend"):
                    Sb = sb("Sb", [P, PARTS, PART, WN], BF16)
                    product_done = sem("product_done")
                    dsc = sb("dsc", [P, MSGS, PART, HEADS])
                WIDTH = {"mlp": D + 2, "gcn": D, "rel": D + 1, "attend": D + HEADS}.get(kind)
                rows_free = {"gcn": released, "score": used, "mlp": used, "rel": used, "attend": msg_ready}[kind]
                part = lambda g, p: g * PARTS + p
                tile = lambda g, p: bass.ds(g * PER_TURN + p * PART, PART)
                by_src = by_lane(dst_rows)

                def summed_at(p, cols):
                    return PS[0:WN, (p % 2) * 512:(p % 2) * 512 + PART * 256].rearrange("n (k c) -> n k c", k=PART)[:, :, 0:cols]

                def turned_at(p, parts, cols=P):
                    return PS[0:parts, (2 + p % 2) * 512:(2 + p % 2) * 512 + PART * 256].rearrange("n (k c) -> n k c", k=PART)[:, :, 0:cols]

                def turned_b(p, parts, cols=P):
                    return PS[0:parts, (2 + p % 2) * 512:(2 + p % 2) * 512 + P].bitcast(BF16).rearrange("n (k c) -> n k c", k=PART)[:, :, 0:cols]

                def mixed_at(p, parts, cols):
                    return PS[0:parts, (4 + p % 2) * 512:(4 + p % 2) * 512 + PART * 256].rearrange("n (k c) -> n k c", k=PART)[:, :, 0:cols]

                with nc.Block() as block:
                    @block.gpsimd
                    def _(pool):
                        def gather(g, p):
                            pool.wait_ge(idx_ready, part(g, p) + 1)
                            pool.sem_inc(idx_seen, 1)
                            for k in range(PART):
                                pool.indirect_dma_start(
                                    out=gbuf[:, p, k, :], out_offset=None, in_=table,
                                    in_offset=bass.IndirectOffsetOnAxis(ap=slot[:, p, k:k + 1], axis=0)
                                ).then_inc(landed[p], 16)
                        pipeline(pool, [(0, gather)])

                    @block.sync
                    def _(sp):
                        if kind == "mlp":
                            def fetch(g, p):
                                sp.wait_ge(turned, part(g, p) + 1)
                                sp.wait_ge(meta_ready, part(g, p) + 1)
                                sp.dma_start(rows[:, p, :, :], by_src[:, tile(g, p), :]).then_inc(rows_in[p], 16)
                            pipeline(sp, [(0, fetch)])

                    @block.scalar
                    def _(act):
                        if kind != "gcn":
                            act.sem_inc(turned_out, 2)
                        act.sem_inc(made, MSGS)
                        if kind == "mlp":
                            act.sem_inc(meta_ready, PARTS)
                        if kind != "mlp":
                            act.wait_ge(index_made, 1)

                        def pick(g, p):
                            act.wait_ge(rows_free, part(g, p) + 1)
                            if kind == "mlp":
                                act.wait_ge(rows_in[p], g * 16 + 16)
                                act.copy(slot[:, p, :], rows[:, p, :, A]).then_inc(idx_ready, 1)
                            else:
                                act.copy(slot[:, p, :], index[:, tile(g, p)]).then_inc(idx_ready, 1)

                        def pick_meta(g, p):
                            act.wait_ge(released, part(g, p) + 1)
                            if kind == "gcn":
                                act.copy(lanes[:, p, :], meta[:, tile(g, p), 1])
                            m = rows[:, p, :, A:ROW] if kind == "mlp" else meta[:, tile(g, p), :]
                            act.copy(mslot[:, p, :, :], m).then_inc(meta_ready, 1)

                        def evacuate(g, p):
                            q = part(g, p)
                            parts = {"mlp": A, "rel": 96}.get(kind, WN)
                            act.wait_ge(turned, q + (1 + AHEAD))
                            act.wait_ge(mixed, q + 1)
                            act.copy(lt[0:parts, p % 2, :, :], turned_at(p, parts) if kind == "mlp" else turned_b(p, parts)).then_inc(turned_out, 1)

                        def relu(g, p):
                            q = part(g, p)
                            act.wait_ge(used, q + PARTS + 1)
                            act.wait_ge(released, q + PARTS - MSGS + 1)
                            nc.scalar.activation(hm[:, p % MSGS, :, 0:D], tmp[:, p % MSGS, :, :], ACT.Relu)
                            act.copy(hm[:, p % MSGS, :, D], mslot[:, p, :, 2]).then_inc(made, 1)

                        def exponent(g, p):
                            q = part(g, p)
                            act.wait_ge(used, q + PARTS + 1)
                            act.wait_ge(released, q + PARTS - MSGS + 1)
                            nc.scalar.activation(hm[:, p % MSGS, :, D:D + HEADS], dsc[:, p % MSGS, :, :], ACT.Exp,
                                                 scale=float(HD) ** -0.5).then_inc(made, 1)

                        def save_sorted(g, p):
                            act.wait_ge(mixed, part(g, p) + 3)
                            act.copy(tmeta[:, tile(g, p), :], mixed_at(p, P, 2)).then_inc(used, 1)

                        if kind == "mlp":
                            pipeline(act, [(8, pick), (6, pick_meta), (4, evacuate), (2, relu)])
                        elif kind == "gcn":
                            act.sem_inc(used, PARTS)
                            pipeline(act, [(8, pick), (6, pick_meta), (2, save_sorted)])
                        elif kind in ("rel", "score"):
                            pipeline(act, [(8, pick), (6, pick_meta), (4, evacuate)])
                        else:
                            pipeline(act, [(8, pick), (8, pick_meta), (5, evacuate), (3, exponent)])

                    @block.tensor
                    def _(pe):
                        pe.sem_inc(mixed, 2)
                        if kind == "mlp":
                            pe.sem_inc(turned, PARTS)
                        if kind != "score":
                            pe.sem_inc(released, PARTS)
                        if kind == "rel":
                            pe.wait_ge(cleared, 1)

                        def turn(g, p):
                            q = part(g, p)
                            pe.wait_ge(turned_out, q + 1)
                            if kind == "mlp":
                                pe.wait_ge(rows_in[p], g * 16 + 16)
                                pe.sem_inc(pe_seen, 1)
                            else:
                                pe.wait_ge(s_ready, q + 1)
                            for k in range(PART):
                                if kind == "mlp":
                                    last = nc.tensor.transpose(turned_at(p, A)[:, k, :], rows[:, p, k, 0:A], ident[:, :])
                                elif kind == "rel":
                                    last = nc.tensor.transpose(turned_b(p, 96)[:, k, :], toh[:, p, k, :], ident_b[:, :])
                                else:
                                    last = nc.tensor.transpose(turned_b(p, WN)[:, k, :], Sb[:, p, k, :], ident_b[:, :])
                            last.then_inc(turned, 1)

                        def spread_keys(g, p):
                            pe.wait_ge(turned_out, part(g, p) + 1)
                            pe.wait_ge(meta_ready, part(g, p) + 1)
                            for k in range(PART):
                                o = turned_at(p, P)[:, k, :]
                                nc.tensor.matmul(o, lanes[:, p, k:k + 1].broadcast_to([P, P]), ident128[:, :], start=True, stop=False)
                                last = nc.tensor.matmul(o, ones_b[:, :], lane_diag[:, :], start=False, stop=True)
                            last.then_inc(turned, 1)

                        regs = [pe.alloc_register(f"{name}_pe_window{i}") for i in range(MSGS * PART)]

                        def mix(g, p):
                            q = part(g, p)
                            if kind in ("score", "attend") and p % MSGS == 0:
                                pe.load(regs, off[0:1, bass.ds(g * PER_TURN + p * PART, MSGS * PART)])
                            at = [pe.snap(regs[p % MSGS * PART + k], min_val=0, max_val=(NW - 1) * PITCH) for k in range(PART)] if kind in ("score", "attend") else None
                            pe.wait_ge(turned_out, q + 3)
                            pe.wait_ge(used, q + PARTS - 1)
                            for k in range(PART):
                                lhs = lt[:, p % 2, k, :]
                                if kind == "mlp":
                                    last = nc.tensor.matmul(mixed_at(p, P, D)[:, k, :], lhs[0:A, :], W1b[:, :], start=True, stop=True)
                                elif kind == "rel":
                                    last = nc.tensor.matmul(mixed_at(p, P, D)[:, k, :], lhs[0:96, :], relS[:, :], start=True, stop=True)
                                elif kind == "gcn":
                                    last = nc.tensor.matmul(mixed_at(p, P, 2)[:, k, :], lhs, mslot[:, p, k, 0:2], start=True, stop=True)
                                else:
                                    cols, skip = (D, 0) if kind == "score" else (HEADS, D)
                                    for i in range(3):
                                        last = nc.tensor.matmul(mixed_at(p, P, cols)[:, k, :], lhs[0:WN, :],
                                                                QM3[:, i, bass.ds(at[k] + skip, cols)], start=(i == 0), stop=(i == 2))
                            last.then_inc(mixed, 1)

                        def total(g, p):
                            q = part(g, p)
                            pe.wait_ge(s_ready, q + 1)
                            pe.wait_ge(added, q * 2 + 2)
                            if kind == "gcn":
                                pe.wait_ge(landed[p], g * 32 + 32)
                            elif kind == "mlp":
                                pe.wait_ge(made, q + MSGS + 1)
                            elif kind == "rel":
                                pe.wait_ge(used, q + PARTS + 1)
                            else:
                                pe.wait_ge(msg_ready, q + PARTS + 1)
                            for k in range(PART):
                                rhs = gbuf[:, p, k, :] if kind == "gcn" else hm[:, p % MSGS, k, 0:WIDTH]
                                last = nc.tensor.matmul(summed_at(p, WIDTH)[:, k, :], S[:, p, k, :], rhs, start=True, stop=True)
                            last.then_inc(released, 1)

                        pipeline(pe, {"mlp": [(4, turn), (3, mix), (1, total)], "rel": [(4, turn), (3, mix), (1, total)],
                                      "gcn": [(4, spread_keys), (2, mix), (1, total)], "score": [(4, turn), (3, mix)],
                                      "attend": [(6, turn), (4, mix), (1, total)]}[kind])

                    @block.vector
                    def _(dve):
                        v = nc.vector
                        if kind != "mlp":
                            v.tensor_copy(index[:, :], meta[:, :, 0]).then_inc(index_made, 1)
                        v.memset(hm[:, :, :, :], 1.0).then_inc(cleared, 1)
                        v.memset(acc[:, :, :], 0.0).then_inc(cleared, 1)
                        dve.wait_ge(cleared, 2)
                        dve.sem_inc(added, 4)
                        if kind != "gcn":
                            dve.sem_inc(used, PARTS)
                        if kind == "gcn":
                            dve.sem_inc(turned_out, 2)
                        if kind == "score":
                            dve.sem_inc(released, PARTS)
                        if kind == "attend":
                            dve.sem_inc(msg_ready, PARTS)

                        def one_hot(g, p):
                            q = part(g, p)
                            dve.wait_ge(released, q + 1)
                            dve.wait_ge(meta_ready, q + (1 + AHEAD))
                            if kind == "mlp":
                                v.tensor_copy(dmeta[:, tile(g, p), :], mslot[:, p, :, :])
                            if kind == "gcn":
                                for k in range(PART):
                                    last = v.tensor_scalar(S[:, p, k, :], iota1[:, 0:WN], mslot[:, p, k, 1:2],
                                                           mslot[:, p, k, 2:3], ALU.is_equal, ALU.mult)
                            else:
                                last = v.tensor_tensor((Sb if kind == "score" else S)[:, p, :, :], iota1[:, 0:WN].unsqueeze(1).broadcast_to([P, PART, WN]),
                                                       dl(p).unsqueeze(2).broadcast_to([P, PART, WN]), ALU.is_equal)
                            if kind == "attend":
                                last = v.tensor_tensor(Sb[:, p, :, :], iota1[:, 0:WN].unsqueeze(1).broadcast_to([P, PART, WN]),
                                                       dl(p).unsqueeze(2).broadcast_to([P, PART, WN]), ALU.is_equal)
                            if kind == "rel":
                                last = v.tensor_tensor(toh[:, p, :, :].rearrange("e k (c r) -> e k c r", c=3),
                                                       iota[:, 0:32].unsqueeze(1).unsqueeze(1).broadcast_to([P, PART, 3, 32]),
                                                       mslot[:, p, :, 1:2].unsqueeze(2).broadcast_to([P, PART, 3, 32]), ALU.is_equal)
                            last.then_inc(s_ready, 1)

                        def sort_tile(g, p):
                            q = part(g, p)
                            dve.wait_ge(turned, q + 1)
                            for k in range(PART):
                                last = v.tensor_scalar(below[:, p, k, :], turned_at(p, P)[:, k, :], mslot[:, p, k, 3:4], 0.0,
                                                       ALU.is_lt, ALU.add, accum_out=rank[:, p % 2, k:k + 1])
                            last.then_inc(rank_written, 1)
                            dve.wait_ge(rank_written, q + 1)
                            dve.wait_ge(mixed, q + 1)
                            v.tensor_tensor(lt[:, p % 2, :, :], iota[:, :].unsqueeze(1).broadcast_to([P, PART, P]),
                                            rank[:, p % 2, :].unsqueeze(2).broadcast_to([P, PART, P]),
                                            ALU.is_equal).then_inc(turned_out, 1)

                        def add_gathered(g, p):
                            q = part(g, p)
                            dve.wait_ge(mixed, q + 3)
                            dve.wait_ge(landed[p], g * 32 + 32)
                            dve.wait_ge(made, q + 1)
                            v.tensor_tensor(tmp[:, p % MSGS, :, :], mixed_at(p, P, D), gbuf[:, p, :, :], ALU.add).then_inc(used, 1)

                        def times_relation(g, p):
                            q = part(g, p)
                            dve.wait_ge(mixed, q + 3)
                            dve.wait_ge(landed[p], g * 32 + 32)
                            dve.wait_ge(released, q + PARTS - MSGS + 1)
                            v.tensor_tensor(hm[:, p % MSGS, :, 0:D], mixed_at(p, P, D), gbuf[:, p, :, :], ALU.mult).then_inc(used, 1)

                        def score(g, p):
                            q = part(g, p)
                            dve.wait_ge(mixed, q + 3)
                            dve.wait_ge(landed[p], g * 32 + 32)
                            v.tensor_tensor(tmp[:, p % MSGS, :, :], mixed_at(p, P, D), gbuf[:, p, :, :], ALU.mult).then_inc(used, 1)
                            dve.wait_ge(used, q + PARTS + 1)
                            dve.sem_inc(product_done, 1)
                            v.tensor_reduce(scores[:, tile(g, p), :],
                                            tmp[:, p % MSGS, :, :].rearrange("e k (h d) -> e k h d", h=HEADS),
                                            AX.X, ALU.add).then_inc(released, 1)

                        def shift(g, p):
                            q = part(g, p)
                            dve.wait_ge(mixed, q + 3)
                            dve.wait_ge(made, q + 1)
                            v.tensor_tensor(dsc[:, p % MSGS, :, :], scores[:, tile(g, p), :], mixed_at(p, P, HEADS),
                                            ALU.subtract).then_inc(used, 1)

                        def weigh(g, p):
                            q = part(g, p)
                            dve.wait_ge(made, q + MSGS + 1)
                            dve.wait_ge(landed[p], g * 32 + 32)
                            for k in range(PART):
                                last = v.tensor_tensor(
                                    hm[:, p % MSGS, k, 0:D].rearrange("e (h d) -> e h d", h=HEADS),
                                    gbuf[:, p, k, :].rearrange("e (h d) -> e h d", h=HEADS),
                                    hm[:, p % MSGS, k, D:D + HEADS].unsqueeze(2).broadcast_to([P, HEADS, HD]), ALU.mult)
                            last.then_inc(msg_ready, 1)

                        regs = [dve.alloc_register(f"{name}_dve_window{i}") for i in range(MSGS * PART)]
                        at = []

                        def add_up(g, p):
                            q = part(g, p)
                            if p % MSGS == 0:
                                dve.load(regs, off[0:1, bass.ds(g * PER_TURN + p * PART, MSGS * PART)])
                                at[:] = [dve.snap(r, min_val=0, max_val=(NW - 1) * PITCH) for r in regs]
                            dve.wait_ge(released, q + PARTS + 1)
                            for k in range(PART):
                                dve.wait_ge(added, q * 2 + (k + 3))
                                a = acc[:, k, bass.ds(at[p % MSGS * PART + k], WIDTH)]
                                v.tensor_tensor(a, summed_at(p, WIDTH)[:, k, :], a, ALU.add).then_inc(added, 1)

                        pipeline(dve, {"mlp": [(5, one_hot), (2, add_gathered), (0, add_up)],
                                       "gcn": [(5, one_hot), (3, sort_tile), (0, add_up)],
                                       "rel": [(5, one_hot), (2, times_relation), (0, add_up)],
                                       "score": [(5, one_hot), (2, score)],
                                       "attend": [(7, one_hot), (3, shift), (2, weigh), (0, add_up)]}[kind])

        def greatest_scores():
            SLOTS = 5
            ROUNDS = T // MAXG // SLOTS
            G = MAXG
            R = G * HEADS
            assert ROUNDS * SLOTS * G == T
            with stage("max") as (sb, sem):
                dsel = sb("dsel", [P, SLOTS, 2, G, HEADS])
                dlT = sb("dlT", [R, SLOTS, P])
                first = sb("first", [R, SLOTS, P + 1])
                reset = sb("reset", [R, SLOTS, P])
                best = sb("best", [R, SLOTS, P])
                mrhs = sb("mrhs", [P, SLOTS, G, HEADS + 1])
                S8 = sb("S8", [P, SLOTS, G, WN])
                gap = sb("gap", [WN, SLOTS, G])
                cand = sb("cand", [WN, SLOTS, G, HEADS])
                picked, turned, dl_out, scanned, back = (sem("picked"), sem("turned"), sem("dl_out"), sem("scanned"),
                                                         sem("back"))
                back_out, s_ready, spread, kept, link_sem = (sem("back_out"), sem("s_ready"), sem("spread"), sem("kept"),
                                                             sem("link"))
                steps_done, cleared, merged, pe_seen = sem("steps_done"), sem("cleared"), sem("merged"), sem("pe_seen")
                link2 = sem("link2")
                turn_of = lambda g, p: g * SLOTS + p

                turned_at = lambda p, at: bank(p % 3, R, P, at)
                spread_at = lambda p: bank(4 + p % 3, WN, G * (HEADS + 1))

                def rounds(eng, steps):
                    for ahead, f in steps:
                        for s in range(ahead):
                            f(0, s)
                    with eng.Fori(0, ROUNDS - 1) as g:
                        for p in range(SLOTS):
                            for ahead, f in steps:
                                f(g + (p + ahead) // SLOTS, (p + ahead) % SLOTS)
                    for p in range(SLOTS):
                        for ahead, f in steps:
                            if p + ahead < SLOTS:
                                f(ROUNDS - 1, p + ahead)

                with nc.Block() as block:
                    @block.scalar
                    def _(act):
                        def pick(g, p):
                            act.wait_ge(kept, turn_of(g, p) + 1)
                            t = bass.ds(turn_of(g, p) * G, G)
                            act.copy(dsel[:, p, 0, :, :], scores[:, t, :])
                            act.copy(dsel[:, p, 1, :, :], tmeta[:, t, 1].unsqueeze(2).broadcast_to([P, G, HEADS])).then_inc(picked, 1)

                        def lanes(g, p):
                            act.wait_ge(turned, turn_of(g, p) + 1)
                            act.copy(dlT[:, p, :], turned_at(p, P)).then_inc(dl_out, 1)

                        def unturn(g, p):
                            act.wait_ge(back, turn_of(g, p) + 1)
                            act.copy(mrhs[:, p, :, 0:HEADS], bank(3, P, R).rearrange("e (t h) -> e t h", t=G)).then_inc(back_out, 1)
                        act.wait_ge(cleared, 4)
                        act.sem_inc(back_out, 1)
                        rounds(act, [(3, pick), (2, lanes), (1, unturn)])

                    @block.tensor
                    def _(pe):
                        def turn(g, p):
                            pe.wait_ge(scanned, turn_of(g, p) + 1)
                            pe.sem_inc(pe_seen, 1)
                            pe.wait_ge(picked, turn_of(g, p) + 1)
                            pe.sem_inc(pe_seen, 1)
                            nc.tensor.transpose(turned_at(p, 0), dsel[:, p, 0, :, :].rearrange("e t h -> e (t h)"), ident[:, :])
                            nc.tensor.transpose(turned_at(p, P), dsel[:, p, 1, :, :].rearrange("e t h -> e (t h)"),
                                                ident[:, :]).then_inc(turned, 1)

                        def turn_back(g, p):
                            pe.wait_ge(back_out, turn_of(g, p) + 1)
                            pe.sem_inc(pe_seen, 1)
                            pe.wait_ge(scanned, turn_of(g, p) + 3)
                            pe.sem_inc(pe_seen, 1)
                            nc.tensor.transpose(bank(3, P, R), best[:, p, :], ident[0:R, 0:R]).then_inc(back, 1)

                        def spread_out(g, p):
                            pe.wait_ge(back_out, turn_of(g, p) + 2)
                            pe.wait_ge(kept, turn_of(g, p) + 4)
                            pe.wait_ge(s_ready, turn_of(g, p) + 1)
                            for i in range(G):
                                last = nc.tensor.matmul(spread_at(p)[:, i * (HEADS + 1):(i + 1) * (HEADS + 1)], S8[:, p, i, :],
                                                        mrhs[:, p, i, :], start=True, stop=True)
                            last.then_inc(spread, 1)
                        rounds(pe, [(3, turn), (0, spread_out), (1, turn_back)])

                    @block.vector
                    def _(dve):
                        v = nc.vector
                        v.memset(first[:, :, :], 1.0).then_inc(cleared, 1)
                        v.memset(mrhs[:, :, :, :], 1.0).then_inc(cleared, 1)
                        for k in range(2):
                            v.memset(acc[:, k, :], -BIG).then_inc(cleared, 1)
                        dve.wait_ge(cleared, 4)
                        dve.sem_inc(kept, SLOTS)

                        def scan(g, p):
                            t = turn_of(g, p)
                            dve.wait_ge(dl_out, t + 1)
                            v.tensor_tensor(first[:, p, 1:P], dlT[:, p, 1:P], dlT[:, p, 0:P - 1], ALU.not_equal).then_inc(link_sem, 1)
                            dve.wait_ge(link_sem, t * 3 + 1)
                            v.tensor_scalar(reset[:, p, :], first[:, p, 0:P], -BIG, None, ALU.mult).then_inc(link_sem, 1)
                            dve.wait_ge(link_sem, t * 3 + 2)
                            v.tensor_tensor_scan(best[:, p, :], reset[:, p, :], turned_at(p, 0), 0.0, ALU.add,
                                                 ALU.max).then_inc(link_sem, 1)
                            dve.wait_ge(link_sem, t * 3 + 3)
                            v.tensor_tensor(best[:, p, :], best[:, p, :], first[:, p, 1:P + 1], ALU.mult).then_inc(scanned, 1)

                        def one_hot(g, p):
                            v.tensor_tensor(S8[:, p, :, :], iota1[:, 0:WN].unsqueeze(1).broadcast_to([P, G, WN]),
                                            dsel[:, p, 1, :, 0].unsqueeze(2).broadcast_to([P, G, WN]), ALU.is_equal).then_inc(s_ready, 1)

                        regs = [dve.alloc_register(f"max_window{i}") for i in range(G)]

                        def keep_best(g, p):
                            t = turn_of(g, p)
                            dve.load(regs, off_d[0:1, bass.ds(t * G, G)])
                            at = [dve.snap(r, min_val=0, max_val=(NW - 1) * PITCH) for r in regs]
                            dve.wait_ge(spread, t + 1)
                            m = spread_at(p).rearrange("n (t c) -> n t c", t=G)
                            v.tensor_scalar(gap[:, p, :], m[:, :, HEADS], 1.0, -1.0, ALU.min, ALU.add).then_inc(steps_done, 1)
                            dve.wait_ge(steps_done, t * 2 + 1)
                            v.scalar_tensor_tensor(out=cand[:, p, :, :], in0=gap[:, p, :].unsqueeze(2).broadcast_to([WN, G, HEADS]),
                                                   scalar=BIG, in1=m[:, :, 0:HEADS], op0=ALU.mult, op1=ALU.add).then_inc(steps_done, 1)
                            dve.wait_ge(steps_done, t * 2 + 2)
                            for i in range(G):
                                dve.wait_ge(merged, t * G + (i + 1))
                                a = acc[:, i % 2, bass.ds(at[i] + D, HEADS)]
                                last = v.tensor_tensor(a, cand[:, p, i, :], a, ALU.max).then_inc(merged, 1)
                            dve.wait_ge(merged, t * G + (G + 2))
                            dve.sem_inc(kept, 1)

                        dve.sem_inc(merged, 2)
                        dve.sem_inc(scanned, 2)
                        rounds(dve, [(2, scan), (2, one_hot), (0, keep_best)])
                        dve.wait_ge(merged, T + 2)
                        link = Chain(dve, link2)
                        link(v.tensor_tensor(qmw[:, :, D:D + HEADS], accw[0][:, :, D:D + HEADS], accw[1][:, :, D:D + HEADS], ALU.max))
                        split_columns(link, D, D + HEADS, aux[:, :, 0:HEADS])

        def first_norm(dve, link, squared, rooted):
            layernorm_relu(dve, link, squared, rooted, 1)

        product("rows0", H, W1a[:, :], rows1[:, 2, :], D, first_norm, lambda act, s, r: root(act, s, r, 1),
                lambda g, rows, _: nc.vector.tensor_copy(aux[:, bass.ds(g * BATCH, BATCH), :], rows),
                lambda _: [(by_window(tab_p), aux[:, :, :])])
        edge_pass("mlp", tab_p, None, off_d, "layer0")

        with stage("update0") as (sb, sem):
            agg = sb("agg", [WN, BATCH, D + 2])
            st = sb("st", [WN, BATCH, D])
            aT, hT, uT = (sb(n, [D, BATCH, WN]) for n in ("aT", "hT", "uT"))
            cT = sb("cT", [1, BATCH, WN])
            agg_ready, st_ready, turned, a_out, h_out = (sem("agg_ready"), sem("st_ready"), sem("turned"), sem("a_out"),
                                                         sem("h_out"))
            mixed2, mixed2_out, mixed1, relu_out, mixed0, added = (sem("mixed2"), sem("mixed2_out"), sem("mixed1"),
                                                                   sem("relu_out"), sem("mixed0"), sem("added"))
            keyed = sem("keyed")
            with nc.Block() as block:
                @block.vector
                def _(dve):
                    v = nc.vector
                    v.tensor_scalar(dmeta[:, 0:T, 3], dmeta[:, 0:T, 1], float(P), lane[:, 0:1], ALU.mult, ALU.add).then_inc(keyed, 1)
                    dve.sem_inc(added, 1)
                    with dve.Fori(0, NW // BATCH) as g:
                        w = bass.ds(g * BATCH, BATCH)
                        dve.wait_ge(added, g + 1)
                        v.tensor_tensor(agg[:, :, :], accw[0][:, w, 0:D + 2], accw[1][:, w, 0:D + 2], ALU.add).then_inc(agg_ready, 1)
                        dve.wait_ge(agg_ready, g + 1)
                        v.tensor_copy(deg[:, w], agg[:, :, D])
                        dve.wait_ge(turned, g + 1)
                        v.tensor_copy(hT[:, :, :], banks(3, 256, BATCH, D, WN)).then_inc(h_out, 1)
                        dve.wait_ge(mixed0, g + 1)
                        v.tensor_tensor(X[:, w, :], X[:, w, :], banks(0, 256, BATCH, WN, D), ALU.add).then_inc(added, 1)

                @block.scalar
                def _(act):
                    with act.Fori(0, NW // BATCH) as g:
                        act.wait_ge(added, g + 1)
                        act.copy(st[:, :, :], H[:, bass.ds(g * BATCH, BATCH), :]).then_inc(st_ready, 1)
                        act.wait_ge(turned, g + 1)
                        act.copy(aT[:, :, :], banks(0, 256, BATCH, D, WN)).then_inc(a_out, 1)
                        act.copy(cT[:, :, :], banks(6, 128, BATCH, 1, WN)).then_inc(a_out, 1)
                        act.wait_ge(mixed2, g + 1)
                        act.copy(aT[:, :, :], banks(0, 256, BATCH, D, WN)).then_inc(mixed2_out, 1)
                        act.wait_ge(mixed1, g + 1)
                        nc.scalar.activation(uT[:, :, :], banks(3, 256, BATCH, D, WN), ACT.Relu, bias=c1col[:, 0:1]).then_inc(relu_out, 1)

                @block.tensor
                def _(pe):
                    with pe.Fori(0, NW // BATCH) as g:
                        pe.wait_ge(agg_ready, g + 1)
                        pe.wait_ge(st_ready, g + 1)
                        for i in range(BATCH):
                            nc.tensor.transpose(bank(0, D, WN, i * 256), agg[:, i, 0:D], ident[0:WN, 0:WN])
                            nc.tensor.transpose(bank(3, D, WN, i * 256), st[:, i, :], ident[0:WN, 0:WN])
                            last = nc.tensor.transpose(bank(6, 1, WN, i * 128), agg[:, i, D + 1:D + 2], ident[0:WN, 0:WN])
                        last.then_inc(turned, 1)
                        pe.wait_ge(a_out, g * 2 + 2)
                        for i in range(BATCH):
                            nc.tensor.matmul(bank(0, D, WN, i * 256), W2s[:, :], aT[:, i, :], start=True, stop=False)
                            last = nc.tensor.matmul(bank(0, D, WN, i * 256), rows1[:, 0, :], cT[:, i, :], start=False, stop=True)
                        last.then_inc(mixed2, 1)
                        pe.wait_ge(mixed2_out, g + 1)
                        pe.wait_ge(h_out, g + 1)
                        for i in range(BATCH):
                            nc.tensor.matmul(bank(3, D, WN, i * 256), U1a[:, :], hT[:, i, :], start=True, stop=False)
                            last = nc.tensor.matmul(bank(3, D, WN, i * 256), U1b[:, :], aT[:, i, :], start=False, stop=True)
                        last.then_inc(mixed1, 1)
                        pe.wait_ge(relu_out, g + 1)
                        for i in range(BATCH):
                            nc.tensor.matmul(bank(0, WN, D, i * 256), uT[:, i, :], U2s[:, :], start=True, stop=False)
                            last = nc.tensor.matmul(bank(0, WN, D, i * 256), ones[0:1, 0:WN], rows1[:, 1, :], start=False, stop=True)
                        last.then_inc(mixed0, 1)

        def second_norm(dve, link, squared, rooted):
            v = nc.vector
            layernorm_relu(dve, link, squared, rooted, 1)
            link(v.tensor_scalar(deg, deg, 1.0, None, ALU.add))
            v.tensor_scalar(var, deg, 1.0e-30, None, ALU.max).then_inc(squared, 1)
            dve.wait_ge(rooted, 2)
            link(v.reciprocal(rstd, std))
            link(v.scalar_tensor_tensor(out=dinv, in0=deg, scalar=0.0, in1=rstd, op0=ALU.is_gt, op1=ALU.mult))

        product("rows1", H, gWs[:, :], None, D, second_norm, lambda act, s, r: (root(act, s, r, 1), root(act, s, r, 2)),
                lambda g, rows, _: nc.vector.tensor_tensor(
                    aux[:, bass.ds(g * BATCH, BATCH), :], rows,
                    dinv[:, bass.ds(g * BATCH, BATCH)].unsqueeze(2).broadcast_to([WN, BATCH, D]), ALU.mult),
                lambda _: [(by_window(tab_h), aux[:, :, :])])
        edge_pass("gcn", tab_h, dmeta, off_d, "layer1")

        with stage("update1") as (sb, sem):
            link_sem, squared, rooted, summed = sem("link"), sem("squared"), sem("rooted"), sem("summed")
            elu_in, elu_out, col_in, stored, done = sem("elu_in"), sem("elu_out"), sem("col_in"), sem("stored"), sem("done")
            brow = sb("brow", [WN, 4, D])
            with nc.Block() as block:
                @block.vector
                def _(dve):
                    link = Chain(dve, link_sem)
                    v = nc.vector
                    h, a = H[:, :, :], aux[:, :, :]
                    link(v.tensor_tensor(h, accw[0][:, :, 0:D], accw[1][:, :, 0:D], ALU.add))
                    link(v.tensor_tensor(h, h, a, ALU.add))
                    link(v.tensor_tensor(h, h, over_windows(dinv), ALU.mult))
                    link(v.tensor_tensor(h, h, over_nodes(vecs[:, 0, :]), ALU.add))
                    v.tensor_scalar(a, h, 0.0, None, ALU.min).then_inc(elu_in, 1)
                    dve.wait_ge(elu_out, 1)
                    link(v.scalar_tensor_tensor(out=h, in0=h, scalar=0.0, in1=a, op0=ALU.max, op1=ALU.add))
                    v.tensor_scalar(h, h, -1.0, None, ALU.add).then_inc(col_in, 1)
                    dve.wait_ge(summed, 1)
                    link(v.tensor_scalar(brow[:, 0, :], bank(0, WN, D), 1.0 / N, None, ALU.mult))
                    link(v.tensor_tensor(a, h, over_nodes(brow[:, 0, :]), ALU.subtract))
                    v.tensor_tensor(h, a, a, ALU.mult).then_inc(col_in, 1)
                    dve.wait_ge(summed, 2)
                    v.tensor_scalar(brow[:, 1, :], bank(1, WN, D), 1.0 / N, 1e-5, ALU.mult, ALU.add).then_inc(squared, 1)
                    dve.wait_ge(rooted, 1)
                    link(v.reciprocal(brow[:, 3, :], brow[:, 2, :]))
                    link(v.tensor_tensor(brow[:, 3, :], brow[:, 3, :], vecs[:, 1, :], ALU.mult))
                    link(v.tensor_tensor(a, a, over_nodes(brow[:, 3, :]), ALU.mult))
                    link(v.tensor_tensor(a, a, over_nodes(vecs[:, 2, :]), ALU.add))
                    normalise(dve, link, squared, rooted, 2, a)
                    link(v.tensor_tensor(a, a, over_windows(rstd), ALU.mult))
                    link(v.tensor_tensor(a, a, over_nodes(vecs[:, 3, :]), ALU.mult))
                    link(v.tensor_tensor(a, a, over_nodes(vecs[:, 4, :]), ALU.add))
                    link(v.tensor_tensor(X[:, :, :], X[:, :, :], a, ALU.add))
                    layernorm_relu(dve, link, squared, rooted, 3)
                    link(v.tensor_tensor(X[:, :, :], X[:, :, :], H[:, :, :], ALU.add))
                    dve.sem_inc(done, 1)

                @block.scalar
                def _(act):
                    act.wait_ge(elu_in, 1)
                    nc.scalar.activation(aux[:, :, :], aux[:, :, :], ACT.Exp).then_inc(elu_out, 1)
                    act.wait_ge(squared, 1)
                    nc.scalar.activation(brow[:, 2, :], brow[:, 1, :], ACT.Sqrt).then_inc(rooted, 1)
                    root(act, squared, rooted, 2)
                    root(act, squared, rooted, 3)

                @block.tensor
                def _(pe):
                    for k in range(2):
                        pe.wait_ge(col_in, k + 1)
                        for w in range(NW):
                            last = nc.tensor.matmul(bank(k, WN, D), ones[0:WN, 0:WN], H[:, w, :], start=(w == 0), stop=(w == NW - 1))
                        last.then_inc(summed, 1)

                @block.sync
                def _(sp):
                    sp.wait_ge(done, 1)
                    sp.dma_start(by_window(tab_x0), H[:, :, :]).then_inc(stored, 16)
                    sp.wait_ge(stored, 16)

        def hop_end(title, last_hop, table_out):
            with stage(title) as (sb, sem):
                link_sem, squared, rooted, stored, done = sem("link"), sem("squared"), sem("rooted"), sem("stored"), sem("done")
                with nc.Block() as block:
                    @block.vector
                    def _(dve):
                        link = Chain(dve, link_sem)
                        v = nc.vector
                        a = aux[:, :, :]
                        link(v.tensor_tensor(a, accw[0][:, :, 0:D], accw[1][:, :, 0:D], ALU.add))
                        link(v.tensor_tensor(denom, accw[0][:, :, D], accw[1][:, :, D], ALU.add))
                        link(v.tensor_scalar(denom, denom, 1.0, None, ALU.max))
                        link(v.reciprocal(rstd, denom))
                        link(v.tensor_tensor(a, a, over_windows(rstd), ALU.mult))
                        link(v.tensor_tensor(H[:, :, :], a, a, ALU.mult))
                        v.tensor_reduce(var, H[:, :, :], AX.X, ALU.add).then_inc(squared, 1)
                        dve.wait_ge(rooted, 1)
                        link(v.tensor_scalar(std, std, 1e-12, None, ALU.max))
                        link(v.reciprocal(rstd, std))
                        link(v.tensor_tensor(a, a, over_windows(rstd), ALU.mult))
                        dve.sem_inc(done, 1)
                        v.tensor_tensor(X[:, :, :], X[:, :, :], a, ALU.add)

                    @block.scalar
                    def _(act):
                        root(act, squared, rooted, 1)

                    @block.sync
                    def _(sp):
                        if not last_hop:
                            sp.wait_ge(done, 1)
                            sp.dma_start(by_window(table_out), aux[:, :, :]).then_inc(stored, 16)
                            sp.wait_ge(stored, 16)

        for i, (t_in, t_out) in enumerate(((tab_x0, tab_x1), (tab_x1, tab_x2), (tab_x2, None))):
            edge_pass("rel", t_in, smeta, off_s, f"hop{i}")
            hop_end(f"end{i}", i == 2, t_out)

        def split_qkv(g, rows, spare):
            w = bass.ds(g * BATCH, BATCH)
            nc.vector.tensor_copy(qmw[:, w, 0:D], rows[:, :, 0:D])
            nc.vector.tensor_copy(aux[:, w, :], rows[:, :, D:2 * D])
            return nc.vector.tensor_copy(spare[:, w, :], rows[:, :, 2 * D:3 * D])

        def split_columns(link, lo, hi, rest):
            v = nc.vector
            q = qmw[:, :, lo:hi]
            link(v.tensor_copy(qm3w[0][:, :, lo:hi], q))
            link(v.tensor_tensor(rest, q, qm3w[0][:, :, lo:hi], ALU.subtract))
            link(v.tensor_copy(qm3w[1][:, :, lo:hi], rest))
            link(v.tensor_tensor(rest, rest, qm3w[1][:, :, lo:hi], ALU.subtract))
            v.tensor_copy(qm3w[2][:, :, lo:hi], rest)

        X3 = H[:, :, :]
        product("qkv", H, qkvT[:, :], qkvb[:, :], 3 * D, first_norm, lambda act, s, r: root(act, s, r, 1), split_qkv,
                lambda spare: [(by_window(tab_k), aux[:, :, :]), (by_window(tab_v), spare[:, :, :])],
                lambda link: split_columns(link, 0, D, X3))
        edge_pass("score", tab_k, tmeta, off_d, "scores")
        greatest_scores()
        edge_pass("attend", tab_v, tmeta, off_d, "attend")

        def last_rows(dve, link, squared, rooted):
            v = nc.vector
            link(v.tensor_tensor(aux[:, :, :], accw[0][:, :, 0:D], accw[1][:, :, 0:D], ALU.add))
            den = H[:, :, 0:HEADS]
            link(v.tensor_tensor(den, accw[0][:, :, D:D + HEADS], accw[1][:, :, D:D + HEADS], ALU.add))
            link(v.tensor_scalar(den, den, 1.0e-30, None, ALU.max))
            link(v.reciprocal(den, den))
            for h in range(HEADS):
                a = aux[:, :, h * HD:(h + 1) * HD]
                link(v.tensor_tensor(a, a, den[:, :, h:h + 1].broadcast_to([WN, NW, HD]), ALU.mult))
            link(v.tensor_tensor(X[:, :, :], X[:, :, :], over_nodes(vecs[:, 5, :]), ALU.add))

        def add_rows(g, rows, _):
            w = bass.ds(g * BATCH, BATCH)
            return nc.vector.tensor_tensor(X[:, w, :], X[:, w, :], rows, ALU.add)

        product("output", aux, outT[:, :], None, D, last_rows, lambda act, s, r: None, add_rows,
                lambda _: [(by_window(out), X[:, :, :])])


_INS = ['x', 'src', 'dst', 'edge_attr_64', 'edge_type_20', 'edge_weight', 'L0_gnn_W1', 'L0_gnn_b1', 'L0_gnn_W2',
        'L0_gnn_b2', 'L0_gnn_U1', 'L0_gnn_c1', 'L0_gnn_U2', 'L0_gnn_c2', 'L1_gnn_W', 'L1_gnn_b', 'L1_gnn_bn_gamma',
        'L1_gnn_bn_beta', 'L1_gnn_ln_gamma', 'L1_gnn_ln_beta', 'L2_gnn_relation_embed', 'L3_gnn_qkv_w',
        'L3_gnn_qkv_b', 'L3_gnn_out_w', 'L3_gnn_out_b']


def kernel(**inputs):
    import numpy as _np
    import concourse.bacc as _bacc
    from concourse import mybir as _mybir
    from concourse.bass_utils import run_bass_kernel_spmd as _run

    nc = _bacc.Bacc("TRN2", target_bir_lowering=False, num_devices=1)
    arrays, args = {}, []
    for name in _INS:
        a = _np.ascontiguousarray(inputs[name])
        arrays[f"in_{name}_dram"] = a
        args.append(nc.dram_tensor(f"in_{name}_dram", a.shape, _mybir.dt.from_np(a.dtype), kind="ExternalInput").ap())
    args.append(nc.dram_tensor("out_0_dram", (3125, 128), _mybir.dt.float32, kind="ExternalOutput").ap())
    program(nc, *args)
    r = _run(nc, [arrays], core_ids=[0])
    return r.results[0]["out_0_dram"]
```

```python
from contextlib import ExitStack, contextmanager

import concourse.bass as bass
from concourse import mybir

F32 = mybir.dt.float32
BF16 = mybir.dt.bfloat16
F16 = mybir.dt.float16
I32 = mybir.dt.int32
ALU = mybir.AluOpType
ACT = mybir.ActivationFunctionType
AX = mybir.AxisListType

P = 128
BIG = 1.0e30
PART = 2
PARTS = 10
MSGS = 5
GROUP = 5
PITCH = 136
ROW = 68


def program(nc, x_in, src, dst, attr, etype, eweight, W1, b1, W2, b2, U1, c1, U2, c2, gW, gb, bn_g, bn_b,
            ln_g, ln_b, rel, qkv_w, qkv_b, out_w, out_b, out):
    N, D = x_in.shape
    E, A = attr.shape
    NREL = rel.shape[0]
    WN = 125
    NW = N // WN
    EJ = E // WN
    HEADS = 8
    HD = D // HEADS
    PER_TURN = PART * PARTS
    T = -(-((E + NW * (P - 1)) // P) // PER_TURN) * PER_TURN
    TURNS = T // PER_TURN
    NQ = T // PART
    assert N == NW * WN and E == EJ * WN and D == 128 and A == 64 and NW % 5 == 0

    dst_rows = nc.dram_tensor("dst_rows", (P * T, ROW), F32, kind="Internal").ap()
    win_tab = nc.dram_tensor("win_tab", (2, T), I32, kind="Internal").ap()
    tables = [nc.dram_tensor(f"table{i}", (N, D), F32, kind="Internal").ap() for i in range(5)]
    tab_p, tab_h, tab_x0, tab_x1, tab_x2 = tables
    tab_kv = nc.dram_tensor("tab_kv", (N, 2 * D), F32, kind="Internal").ap()
    edge_v = nc.dram_tensor("edge_v", (P * T, D), F32, kind="Internal").ap()

    by_window = lambda ap: ap.rearrange("(w p) d -> p w d", p=WN)
    by_lane = lambda ap: ap.rearrange("(l t) c -> l t c", l=P)

    outer = ExitStack()

    def keep(name, shape, dt=F32):
        return outer.enter_context(nc.sbuf_tensor(name, shape, dt))

    @contextmanager
    def stage(title):
        snap = nc.snapshot_sems()
        ctx = ExitStack()
        with ctx:
            def sb(name, shape, dt=F32):
                return ctx.enter_context(nc.sbuf_tensor(f"{title}_{name}", shape, dt))
            yield sb, lambda name: nc.alloc_semaphore(f"{title}_{name}")
        nc.clear_and_free_semaphores(nc.allocated_since(snap))
        nc.all_engine_barrier()

    def pipeline(eng, steps):
        furthest = max(ahead for ahead, _ in steps)
        peeled = -(-furthest // PARTS)

        def straight(parts):
            for at in parts:
                for ahead, f in steps:
                    if 0 <= at + ahead < NQ:
                        f((at + ahead) // PARTS, (at + ahead) % PARTS)
        straight(range(-furthest, 0))
        with eng.Fori(0, TURNS - peeled) as g:
            for p in range(PARTS):
                for ahead, f in steps:
                    f(g + (p + ahead) // PARTS, (p + ahead) % PARTS)
        straight(range((TURNS - peeled) * PARTS, NQ))

    def split_parts(link, x, out3, part_f, rest):
        v = nc.vector
        b = [slice(32 * i, 32 * i + 32) for i in range(3)]
        link(v.tensor_copy(out3[:, :], x))
        link(v.tensor_copy(part_f, out3[:, :]))
        link(v.tensor_tensor(rest, x, part_f, ALU.subtract))
        for i in (1, 2):
            link(v.tensor_copy(out3[b[i], :], rest[b[i], :]))
        link(v.tensor_copy(part_f[b[2], :], out3[b[2], :]))
        link(v.tensor_tensor(rest[b[2], :], rest[b[2], :], part_f[b[2], :], ALU.subtract))
        link(v.tensor_copy(out3[b[2], :], rest[b[2], :]))

    class Chain:
        def __init__(self, eng, sem):
            self.eng, self.sem, self.n = eng, sem, 0

        def __call__(self, ins):
            self.n += 1
            ins.then_inc(self.sem, 1)
            self.eng.wait_ge(self.sem, self.n)

    with outer:
        PS = outer.enter_context(nc.psum_tensor("PS", [P, 8 * 512], F32))

        def bank(b, parts, cols, at=0):
            return PS[0:parts, b * 512 + at:b * 512 + at + cols]

        def banks(b, stride, n, parts, cols):
            return PS[0:parts, b * 512:b * 512 + n * stride].rearrange("p (i c) -> p i c", c=stride)[:, :, 0:cols]

        X = keep("X", [WN, NW, D])
        H = keep("H", [WN, NW, D])
        acc = keep("acc", [WN, 2, NW * PITCH])
        accw = [acc[:, k, :].rearrange("p (w c) -> p w c", c=PITCH) for k in range(2)]
        aux = keep("aux", [WN, NW, D])
        ident = keep("ident", [P, P])
        ones = keep("ones", [P, P])
        ones_b = keep("ones_b", [P, P], BF16)
        ident_b = keep("ident_b", [P, P], BF16)
        ident128 = keep("ident128", [P, P], BF16)
        lane_diag = keep("lane_diag", [P, P], BF16)
        lane = keep("lane", [P, 1])
        iota = keep("iota", [P, P])
        iota1 = keep("iota1", [P, P])
        dmeta = keep("dmeta", [P, T + PER_TURN, 4])
        smeta = keep("smeta", [P, T + PER_TURN, 4])
        tmeta = keep("tmeta", [P, T + PER_TURN, 2])
        index = keep("index", [P, T + PER_TURN], I32)
        off_d = keep("off_d", [1, T], I32)
        off_s = keep("off_s", [1, T], I32)
        last_tile = keep("last_tile", [1, NW], I32)
        stat = keep("stat", [WN, 16, NW])
        cnt_d, deg, dinv, denom = (stat[:, i, :] for i in range(4))
        W1a = keep("W1a", [D, D])
        W1b = keep("W1b", [A, D])
        W2U = keep("W2U", [D, D])
        U1a = keep("U1a", [D, D])
        U1b = keep("U1b", [D, D])
        U2s = keep("U2s", [D, D])
        gWs = keep("gWs", [D, D])
        relS = keep("relS", [96, D], BF16)
        qkvT = keep("qkvT", [D, 3 * D])
        outT = keep("outT", [D, D])
        b2U = keep("b2U", [1, D])
        c1col = keep("c1col", [D, 1])
        vecs = keep("vecs", [WN, 8, D])
        qkvb = keep("qkvb", [WN, 3 * D])

        with stage("places") as (sb, sem):
            raw = sb("raw", [P, 5, D])
            W2T = sb("W2T", [D, D])
            b2col = sb("b2col", [D, 1])
            relraw = sb("relraw", [96, D])
            relpart = sb("relpart", [96, 2, D])
            keys = sb("keys", [WN, 3, EJ], I32)
            wts = sb("wts", [WN, EJ])
            ZT = 4
            zeros = sb("zeros", [P, ZT * ROW])
            lower = sb("lower", [P, P])
            wcol = sb("wcol", [WN, NW])
            TQ = T // 4
            tcol = sb("tcol", [TQ, 4])
            onehot = sb("onehot", [WN, NW, EJ], BF16)
            cum_all = sb("cum", [P, NW * EJ])
            cum = cum_all[0:WN, :]
            cumw = cum[:, :].rearrange("p (w j) -> p w j", j=EJ)
            kf = H[:, :, :].rearrange("p w d -> p (w d)")[:, 0:5 * EJ].rearrange("p (i j) -> p i j", i=5)
            ki = sb("ki", [WN, EJ], I32)
            place = sb("place", [WN, 2, EJ], I32)
            small = sb("small", [WN, 10, NW])
            smalli = sb("smalli", [WN, 2, NW], I32)
            wcmp = sb("wcmp", [TQ, 4, NW])
            wval = sb("wval", [TQ, 4])
            wvali = sb("wvali", [TQ, 2, 4], I32)
            meta = sb("meta", [WN, EJ, 4])
            codes = sb("codes", [WN, EJ, 4])
            RING = 17
            HALF = [(0, 9), (9, 8)]
            CHUNKS = EJ // RING
            assert CHUNKS * RING == EJ and TQ <= P
            rowbuf = sb("rowbuf", [WN, RING, ROW])
            smallbuf = sb("smallbuf", [WN, RING, 4])
            placebuf = sb("placebuf", [WN, RING], I32)
            tiles_b = sb("tiles_b", [WN, T], BF16)
            zeros_b = zeros[0:WN, :].bitcast(BF16)[:, 0:T]
            iota_b = sb("iota_b", [WN, P], BF16)
            hi_b = sb("hi_b", [WN, EJ], BF16)
            SLOTS = HALF[0][1]
            LAG = HALF[1][1]
            CODE = T + 2 * P
            assert T <= 512 and SLOTS * CODE <= NW * EJ and NREL <= 32 and 2048 < N <= 4096
            spots = onehot[:, :, :].rearrange("p w j -> p (w j)")[:, 0:SLOTS * CODE].bitcast(F16).rearrange("p (s c) -> p s c", c=CODE)
            CODE_BANK = (6, 7)

            loaded, zero_ready, zeroed = sem("loaded"), sem("zero_ready"), sem("zeroed")
            const_made, consts = sem("const_made"), sem("consts")
            weights_in, turned, turned_out = sem("weights_in"), sem("turned"), sem("turned_out")
            counted, summed = sem("counted"), sem("summed")
            wins, wins_out, wins_in = sem("wins"), sem("wins_out"), sem("wins_in")
            dve_link, placed = sem("dve_link"), sem("placed")
            attr_in = [sem(f"attr_in{h}") for h in range(2)]
            scattered = [sem(f"scattered{h}") for h in range(2)]
            staged, staged_seen = sem("staged"), sem("staged_seen")
            codes_in, spotted, spots_used, decoded_in = sem("codes_in"), sem("spotted"), sem("spots_used"), sem("decoded_in")

            with nc.Block() as block:
                @block.sync
                def _(sp):
                    sp.wait_ge(zero_ready, 1)
                    for i, a in enumerate((dst, src, etype)):
                        sp.dma_start(keys[:, i, :], a.rearrange("(p j) -> p j", p=WN)).then_inc(loaded, 16)
                    sp.dma_start(wts[:, :], eweight.rearrange("(p j) -> p j", p=WN)).then_inc(loaded, 16)
                    z = zeros[:, :].unsqueeze(1).broadcast_to([P, T // ZT, ZT * ROW])
                    sp.dma_start(dst_rows.rearrange("(l g t) c -> l g (t c)", l=P, t=ZT), z).then_inc(zeroed, 16)
                    plain = [(X[:, :, :], by_window(x_in)), (W1a[:, :], W1[0:D, :]), (W1b[:, :], W1[D:D + A, :]),
                             (raw[:, 4, :], W2), (U1a[:, :], U1[0:D, :]), (U1b[:, :], U1[D:2 * D, :]), (U2s[:, :], U2),
                             (gWs[:, :], gW), (raw[:, 3, :], out_w),
                             (b2col[:, :], b2.unsqueeze(1)), (qkvb[:, :], qkv_b.partition_broadcast(WN)),
                             (c1col[:, :], c1.unsqueeze(1)),
                             (raw[:, 0:3, :], qkv_w.rearrange("(i p) d -> p i d", p=P))]
                    plain += [(relraw[32 * i:32 * i + NREL, :], rel) for i in range(3)]
                    plain += [(vecs[:, i, :], a.partition_broadcast(WN)) for i, a in enumerate((gb, bn_g, bn_b, ln_g, ln_b, out_b, b1, c2))]
                    for o, a in plain:
                        sp.dma_start(o, a).then_inc(weights_in, 16)
                    at = attr.rearrange("(p j) a -> p j a", p=WN)

                    def load(c):
                        for h, (lo, n) in enumerate(HALF):
                            if not isinstance(c, int):
                                sp.wait_ge(scattered[h], c * (16 * n))
                            sp.dma_start(rowbuf[:, lo:lo + n, 0:A], at[:, bass.ds(c * RING + lo, n), :]).then_inc(attr_in[h], 16)
                    load(0)
                    with sp.Fori(1, CHUNKS) as c:
                        load(c)
                    sp.wait_ge(wins, 2)
                    for i in range(2):
                        sp.dma_start(win_tab[i].rearrange("(p q) -> p q", q=4), wvali[:, i, :]).then_inc(wins_out, 16)
                    sp.wait_ge(wins_out, 32)
                    for i, o in enumerate((off_d, off_s)):
                        sp.dma_start(o[:, :], win_tab[i:i + 1, :]).then_inc(wins_in, 16)
                    sp.wait_ge(wins_in, 32)
                    for h, (lo, n) in enumerate(HALF):
                        sp.wait_ge(scattered[h], 16 * n * CHUNKS)
                    sp.wait_ge(weights_in, 16 * len(plain))

                @block.gpsimd
                def _(pool):
                    pool.memset(ones[:, :], 1.0).then_inc(const_made, 1)
                    for t in (iota, iota1):
                        pool.iota(t[:, :], [[1, P]], base=0 if t is iota else 1, channel_multiplier=0,
                                  allow_small_or_imprecise_dtypes=True).then_inc(const_made, 1)
                    pool.iota(wcol[:, :], [[1, NW]], base=0, channel_multiplier=0,
                              allow_small_or_imprecise_dtypes=True).then_inc(const_made, 1)
                    pool.iota(tcol[:, :], [[1, 4]], base=0, channel_multiplier=4,
                              allow_small_or_imprecise_dtypes=True).then_inc(const_made, 1)
                    pool.iota(lane[:, :], [[0, 1]], base=0, channel_multiplier=1,
                              allow_small_or_imprecise_dtypes=True).then_inc(const_made, 1)
                    pool.iota(tiles_b[:, :], [[1, T]], base=-(T // 2), channel_multiplier=0,
                              allow_small_or_imprecise_dtypes=True).then_inc(const_made, 1)
                    pool.iota(iota_b[:, :], [[1, P]], base=0, channel_multiplier=0,
                              allow_small_or_imprecise_dtypes=True).then_inc(const_made, 1)
                    pool.wait_ge(const_made, 8)
                    pool.affine_select(out=ident[:, :], in_=ones[:, :], compare_op=ALU.is_equal, fill=0.0, base=0,
                                       pattern=[[-1, P]], channel_multiplier=1).then_inc(consts, 1)
                    pool.affine_select(out=lower[:, :], in_=ones[:, :], compare_op=ALU.is_gt, fill=0.0, base=0,
                                       pattern=[[1, P]], channel_multiplier=-1).then_inc(consts, 1)
                    pool.wait_ge(zeroed, 16)

                    def send(c):
                        for h, (lo, n) in enumerate(HALF):
                            pool.wait_ge(staged, c * 2 + (h + 1))
                            pool.sem_inc(staged_seen, 1)
                            pool.wait_ge(attr_in[h], c * 16 + 16)
                            pool.sem_inc(staged_seen, 1)
                            for j in range(lo, lo + n):
                                pool.indirect_dma_start(
                                    out=dst_rows, in_=rowbuf[:, j, :], in_offset=None,
                                    out_offset=bass.IndirectOffsetOnAxis(ap=placebuf[:, j:j + 1], axis=0)
                                ).then_inc(scattered[h], 16)
                    with pool.Fori(0, CHUNKS) as c:
                        send(c)

                @block.scalar
                def _(act):
                    act.wait_ge(turned, 1)
                    act.copy(qkvT[:, :], bank(0, P, 3 * D)).then_inc(turned_out, 1)
                    act.copy(outT[:, :], bank(1, P, D)).then_inc(turned_out, 1)
                    act.copy(W2T[:, :], bank(1, P, D, D)).then_inc(turned_out, 1)
                    act.wait_ge(turned, 2)
                    act.copy(W2U[:, :], bank(1, P, D, 2 * D))
                    act.copy(b2U[:, :], bank(1, 1, D, 3 * D))
                    act.wait_ge(placed, 1)

                    def put(c):
                        for h, (lo, n) in enumerate(HALF):
                            if not isinstance(c, int):
                                act.wait_ge(scattered[h], c * (16 * n))
                            j = bass.ds(c * RING + lo, n)
                            act.copy(rowbuf[:, lo:lo + n, A:ROW], meta[:, j, 0:4])
                            act.copy(placebuf[:, lo:lo + n], place[:, 0, j]).then_inc(staged, 1)
                    put(0)
                    with act.Fori(1, CHUNKS) as c:
                        put(c)

                @block.tensor
                def _(pe):
                    pe.wait_ge(consts, 2)
                    for k in range(2):
                        if k == 1:
                            pe.wait_ge(weights_in, 16 * 24)
                            for i in range(3):
                                nc.tensor.transpose(bank(0, P, D, i * D), raw[:, i, :], ident[:, :])
                            for i in (3, 4):
                                last = nc.tensor.transpose(bank(1, P, D, (i - 3) * D), raw[:, i, :], ident[:, :])
                            last.then_inc(turned, 1)
                            pe.wait_ge(turned_out, 3)
                            nc.tensor.matmul(bank(1, P, D, 2 * D), W2T[:, :], U1b[:, :], start=True, stop=True)
                            nc.tensor.matmul(bank(1, 1, D, 3 * D), b2col[:, :], U1b[:, :], start=True, stop=True).then_inc(turned, 1)
                        pe.wait_ge(counted, k + 1)
                        nc.tensor.matmul(bank(2 + k, WN, NW), lower[0:WN, 0:WN], small[:, 1, :], start=True, stop=True)
                        nc.tensor.matmul(bank(4 + k, P, NW), ones[0:WN, :], small[:, 1, :], start=True,
                                         stop=True).then_inc(summed, 1)
                    pe.wait_ge(placed, 2)
                    for i in range(2):
                        nc.tensor.matmul(bank(CODE_BANK[i], P, T), zeros_b[:, 0:P], zeros_b[:, :], start=True, stop=False)
                    with pe.Fori(0, CHUNKS) as c:
                        for s in range(RING):
                            pe.wait_ge(spotted, c * RING + (s + 1))
                            spot = spots[:, s % SLOTS, :]
                            for i in range(2):
                                last = nc.tensor.matmul(bank(CODE_BANK[i], P, T), spot[:, T + i * P:T + (i + 1) * P],
                                                        spot[:, 0:T], start=False, stop=False)
                            last.then_inc(spots_used, 1)
                    for i in range(2):
                        last = nc.tensor.matmul(bank(CODE_BANK[i], P, T), zeros_b[:, 0:P], zeros_b[:, :], start=False, stop=True)
                    last.then_inc(decoded_in, 1)

                @block.vector
                def _(dve):
                    link = Chain(dve, dve_link)
                    v = nc.vector
                    v.memset(relraw[:, :], 0.0)
                    v.memset(zeros[:, :], 0.0).then_inc(zero_ready, 1)
                    link(v.memset(meta[:, :, :], 0.0))
                    for m in (dmeta, smeta, tmeta):
                        link(v.memset(m[:, T:T + PER_TURN, :], 0.0))
                    link(v.memset(smeta[:, 0:T, 3], 0.0))
                    dve.wait_ge(const_made, 8)
                    dve.wait_ge(loaded, 64)
                    link(v.tensor_copy(meta[:, :, 0], keys[:, 1, :]))
                    link(v.tensor_copy(meta[:, :, 2], wts[:, :]))
                    kv, hi, lo, fix, acc_place = (kf[:, i, :] for i in range(5))
                    for k in range(2):
                        link(v.tensor_copy(kv, keys[:, k, :]))
                        link(v.tensor_scalar(ki[:, :], kv, 1.0 / WN, None, ALU.mult))
                        link(v.tensor_copy(hi, ki[:, :]))
                        link(v.scalar_tensor_tensor(out=lo, in0=hi, scalar=-float(WN), in1=kv, op0=ALU.mult, op1=ALU.add))
                        for op, bound, sign in ((ALU.is_lt, 0.0, -1.0), (ALU.is_ge, float(WN), 1.0)):
                            link(v.tensor_scalar(fix, lo, bound, sign, op, ALU.mult))
                            link(v.tensor_tensor(hi, hi, fix, ALU.add))
                            link(v.scalar_tensor_tensor(out=lo, in0=fix, scalar=-float(WN), in1=lo, op0=ALU.mult, op1=ALU.add))
                        if k == 0:
                            link(v.tensor_scalar(meta[:, :, 1], lo, 1.0, None, ALU.add))
                        else:
                            link(v.tensor_scalar(fix, lo, 1.0, 32.0, ALU.add, ALU.mult))
                            link(v.tensor_copy(lo, keys[:, 2, :]))
                            link(v.tensor_tensor(fix, fix, lo, ALU.add))
                            link(v.tensor_copy(lo, keys[:, 0, :]))
                            link(v.scalar_tensor_tensor(out=fix, in0=fix, scalar=4096.0, in1=lo, op0=ALU.mult, op1=ALU.add))
                            link(v.tensor_copy(place[:, 1, :], fix))
                            link(v.tensor_scalar(ki[:, :], place[:, 1, :], 4095, None, ALU.bitwise_and))
                            link(v.tensor_scalar(codes[:, :, 3], ki[:, :], 2048.0, None, ALU.subtract))
                            link(v.tensor_scalar(ki[:, :], place[:, 1, :], 12, None, ALU.arith_shift_right))
                            link(v.tensor_copy(lo, ki[:, :]))
                            link(v.tensor_scalar(fix, lo, 2048.0, -4097.0, ALU.is_gt, ALU.mult))
                            link(v.tensor_tensor(codes[:, :, 2], lo, fix, ALU.add))
                        link(v.tensor_copy(hi_b[:, :], hi))
                        for w in range(NW):
                            last = v.tensor_scalar(onehot[:, w, :], hi_b[:, :], wcol[:, w:w + 1], None, ALU.is_equal)
                        link(last)
                        flat = onehot[:, :, :].rearrange("p w j -> p (w j)")
                        link(v.tensor_tensor_scan(cum[:, :], flat, flat, 0.0, ALU.add, ALU.max))
                        ends, count, tiles, tcum, off = (small[:, i, :] for i in range(5))
                        link(v.tensor_copy(ends, cumw[:, :, EJ - 1]))
                        link(v.tensor_copy(count[:, 0:1], ends[:, 0:1]))
                        v.tensor_tensor(count[:, 1:NW], ends[:, 1:NW], ends[:, 0:NW - 1], ALU.subtract).then_inc(counted, 1)
                        dve.wait_ge(summed, k + 1)
                        total = bank(4 + k, WN, NW)
                        link(v.tensor_scalar(smalli[:, 0, :], total, float(P - 1), None, ALU.add))
                        link(v.tensor_scalar(smalli[:, 1, :], smalli[:, 0, :], 7, None, ALU.arith_shift_right))
                        link(v.tensor_copy(tiles, smalli[:, 1, :]))
                        link(v.tensor_tensor_scan(tcum, tiles, tiles, 0.0, ALU.add, ALU.max))
                        if k == 0:
                            link(v.tensor_scalar(last_tile[:, :], tcum[0:1, :], -1.0, 0.0, ALU.add, ALU.max))
                        link(v.tensor_tensor(off, tcum, tiles, ALU.subtract))
                        link(v.tensor_scalar(off, off, float(P), -1.0, ALU.mult, ALU.add))
                        link(v.tensor_tensor(off, off, bank(2 + k, WN, NW), ALU.add))
                        link(v.tensor_tensor(off, off, ends, ALU.subtract))
                        link(v.tensor_tensor(off, off, count, ALU.add))
                        for w in range(NW):
                            last = v.scalar_tensor_tensor(out=cumw[:, w, :], in0=cumw[:, w, :], scalar=off[:, w:w + 1],
                                                          in1=onehot[:, w, :], op0=ALU.add, op1=ALU.mult)
                        link(last)
                        link(v.tensor_reduce(acc_place, cumw.rearrange("p w j -> p j w"), AX.X, ALU.add))
                        link(v.tensor_copy(ki[:, :], acc_place))
                        link(v.tensor_scalar(place[:, k, :], ki[:, :], 7, None, ALU.arith_shift_right))
                        link(v.tensor_copy(fix, place[:, k, :]))
                        link(v.scalar_tensor_tensor(out=lo, in0=fix, scalar=-float(P), in1=acc_place, op0=ALU.mult, op1=ALU.add))
                        if k == 0:
                            link(v.scalar_tensor_tensor(out=place[:, 0, :], in0=lo, scalar=float(T), in1=fix, op0=ALU.mult,
                                                        op1=ALU.add))
                            dve.sem_inc(placed, 1)
                        else:
                            link(v.tensor_copy(codes[:, :, 1], lo))
                            link(v.tensor_scalar(codes[:, :, 0], fix, float(T // 2), None, ALU.subtract))
                            dve.sem_inc(placed, 1)
                        link(v.tensor_tensor(wcmp[:, :, :], tcum[0:TQ, :].unsqueeze(1).broadcast_to([TQ, 4, NW]),
                                             tcol[:, :].unsqueeze(2).broadcast_to([TQ, 4, NW]), ALU.is_le))
                        link(v.tensor_reduce(wval[:, :], wcmp[:, :, :], AX.X, ALU.add))
                        v.tensor_scalar(wvali[:, k, :], wval[:, :], float(NW - 1), float(PITCH), ALU.min,
                                        ALU.mult).then_inc(wins, 1)
                    dve.sem_inc(spots_used, LAG)
                    with dve.Fori(0, CHUNKS) as c:
                        for h, (lo_, n) in enumerate(HALF):
                            v.tensor_copy(smallbuf[:, lo_:lo_ + n, :], codes[:, bass.ds(c * RING + lo_, n), :]).then_inc(codes_in, 1)
                            dve.wait_ge(codes_in, c * 2 + (h + 1))
                            for s in range(lo_, lo_ + n):
                                dve.wait_ge(spots_used, c * RING + (s + 1))
                                spot = spots[:, s % SLOTS, :]
                                v.tensor_scalar(spot[:, 0:T], tiles_b[:, :], smallbuf[:, s, 0:1], None, ALU.is_equal)
                                for i in range(2):
                                    last = v.tensor_scalar(spot[:, T + i * P:T + (i + 1) * P], iota_b[:, :], smallbuf[:, s, 1:2],
                                                           smallbuf[:, s, 2 + i:3 + i], ALU.is_equal, ALU.mult)
                                last.then_inc(spotted, 1)
                    dve.wait_ge(consts, 2)
                    v.tensor_copy(ones_b[:, :], ones[:, :])
                    v.tensor_copy(ident_b[:, :], ident[:, :])
                    v.tensor_scalar(ident128[:, :], ident[:, :], float(P), None, ALU.mult)
                    v.tensor_scalar(lane_diag[:, :], ident[:, :], lane[:, 0:1], None, ALU.mult)
                    dve.wait_ge(weights_in, 16 * 24)
                    hi_, rest = relpart[:, 0, :], relpart[:, 1, :]
                    split_parts(link, relraw[:, :], relS, hi_, rest)
                    code, codei = cum_all[:, 0:T], cum_all[:, T:2 * T].bitcast(I32)
                    parti = cum_all[:, 2 * T:3 * T].bitcast(I32)
                    partf = cum_all[:, 2 * T:3 * T]
                    dve.wait_ge(decoded_in, 1)
                    link(v.tensor_copy(code, bank(CODE_BANK[0], P, T)))
                    link(v.tensor_scalar(partf, code, 0.0, 4097.0, ALU.is_lt, ALU.mult))
                    link(v.tensor_tensor(code, code, partf, ALU.add))
                    link(v.tensor_scalar(code, code, 4096.0, 2048.0, ALU.mult, ALU.add))
                    link(v.tensor_tensor(code, code, bank(CODE_BANK[1], P, T), ALU.add))
                    link(v.tensor_copy(codei, code))
                    for i, shift, mask in ((0, 0, 4095), (1, 12, 31), (2, 17, 127)):
                        link(v.tensor_scalar(parti, codei, shift, mask, ALU.arith_shift_right, ALU.bitwise_and))
                        link(v.tensor_copy(smeta[:, 0:T, i], parti))

        QM = keep("QM", [WN, NW * PITCH])
        qmw = QM[:, :].rearrange("p (w c) -> p w c", c=PITCH)
        QM3 = keep("QM3", [WN, 3, NW * PITCH], BF16)
        qm3w = [QM3[:, i, :].rearrange("p (w c) -> p w c", c=PITCH) for i in range(3)]
        scores = keep("scores", [P, T, HEADS])

        def over_windows(col):
            return col.unsqueeze(2).broadcast_to([WN, NW, D])

        def over_nodes(row):
            return row.unsqueeze(1).broadcast_to([WN, NW, D])

        mean, var, std, rstd = (stat[:, i, :] for i in range(4, 8))

        HALVES = (slice(0, NW // 2 + 1), slice(NW // 2 + 1, NW))

        def normalise(dve, link, squared, rooted, n, src_, m=0, eps=1e-5):
            v = nc.vector
            link(v.tensor_reduce(mean, src_, AX.X, ALU.add))
            link(v.tensor_scalar(mean, mean, 1.0 / D, None, ALU.mult))
            for h in HALVES:
                v.tensor_tensor(aux[:, h, :], src_[:, h, :], over_windows(mean)[:, h, :], ALU.subtract).then_inc(squared[1], 1)
            for i, h in enumerate(HALVES):
                dve.wait_ge(rooted[1], 2 * m + i + 1)
                link(v.tensor_reduce(var[:, h], H[:, h, :], AX.X, ALU.add))
            v.tensor_scalar(var, var, 1.0 / D, eps, ALU.mult, ALU.add).then_inc(squared[0], 1)
            dve.wait_ge(rooted[0], n)
            link(v.reciprocal(rstd, std))

        def squares(act, squared, rooted, m=0):
            for i, h in enumerate(HALVES):
                act.wait_ge(squared[1], 2 * m + i + 1)
                nc.scalar.activation(H[:, h, :], aux[:, h, :], ACT.Square).then_inc(rooted[1], 1)

        def root(act, squared, rooted, n):
            act.wait_ge(squared[0], n)
            nc.scalar.activation(std, var, ACT.Sqrt).then_inc(rooted[0], 1)

        def layernorm_relu(dve, link, squared, rooted, n, m=0):
            normalise(dve, link, squared, rooted, n, X[:, :, :], m)
            link(nc.vector.scalar_tensor_tensor(out=H[:, :, :], in0=aux[:, :, :], scalar=0.0, in1=over_windows(rstd),
                                                op0=ALU.max, op1=ALU.mult))

        BATCH = 5

        def product(title, source, weight, width, prepare, prepare_root, finish, store, after=None):
            with stage(title) as (sb, sem):
                st = sb("st", [WN, BATCH, D])
                hT = sb("hT", [D, BATCH, WN])
                spare = sb("spare", [WN, NW, D]) if width > D else None
                ready, squared, rooted, link_sem = sem("ready"), (sem("squared"), sem("centred")), (sem("rooted"), sem("squares")), sem("link")
                picked, turned, turned_out = sem("picked"), sem("turned"), sem("turned_out")
                mixed, finished, stored = sem("mixed"), sem("finished"), sem("stored")
                after_sem = sem("after")
                stride = 256 if width <= 256 else 512
                with nc.Block() as block:
                    @block.vector
                    def _(dve):
                        link = Chain(dve, link_sem)
                        prepare(dve, link, squared, rooted)
                        dve.sem_inc(ready, 1)
                        dve.sem_inc(finished, 1)
                        with dve.Fori(0, NW // BATCH) as g:
                            dve.wait_ge(mixed, g + 2)
                            finish(g, banks(3, stride, BATCH, WN, width), spare).then_inc(finished, 1)
                            if after:
                                after(dve, g, finished, after_sem)

                    @block.scalar
                    def _(act):
                        prepare_root(act, squared, rooted)
                        act.wait_ge(ready, 1)
                        with act.Fori(0, NW // BATCH) as g:
                            act.wait_ge(turned, g + 1)
                            act.copy(st[:, :, :], source[:, bass.ds(g * BATCH, BATCH), :]).then_inc(picked, 1)
                            act.wait_ge(turned, g + 2)
                            act.wait_ge(mixed, g + 1)
                            act.copy(hT[:, :, :], banks(0, 256, BATCH, D, WN)).then_inc(turned_out, 1)

                    @block.tensor
                    def _(pe):
                        pe.sem_inc(turned, 1)
                        pe.sem_inc(mixed, 1)
                        with pe.Fori(0, NW // BATCH) as g:
                            pe.wait_ge(picked, g + 1)
                            for i in range(BATCH):
                                last = nc.tensor.transpose(bank(0, D, WN, i * 256), st[:, i, :], ident[0:WN, 0:WN])
                            last.then_inc(turned, 1)
                            pe.wait_ge(turned_out, g + 1)
                            pe.wait_ge(finished, g + 1)
                            for i in range(BATCH):
                                o = bank(3, WN, width, i * stride)
                                last = nc.tensor.matmul(o, hT[:, i, :], weight, start=True, stop=True)
                            last.then_inc(mixed, 1)

                    @block.sync
                    def _(sp):
                        with sp.Fori(0, NW // BATCH) as g:
                            sp.wait_ge(finished, g + 2)
                            moves = store(bass.ds(g * BATCH, BATCH), spare)
                            for o, a in moves:
                                sp.dma_start(o, a).then_inc(stored, 16)
                        sp.wait_ge(stored, 16 * len(moves) * (NW // BATCH))

        def edge_pass(kind, table, meta, off, name):
            with stage(name) as (sb, sem):
                MW = 2 if meta is tmeta else 4
                gbuf = sb("gbuf", [P, PARTS, PART, 2 * D if kind == "score" else D])
                slot = sb("slot", [P, PARTS, PART], I32)
                mslot = sb("mslot", [P, PARTS, PART, MW])
                if kind != "score":
                    S = sb("S", [P, PARTS, PART, WN])
                    hm = sb("hm", [P, MSGS, PART, PITCH])
                lt = sb("lt", [P, 2, PART, P], {"mlp": F32, "gcn": F16}.get(kind, BF16))
                tmp = sb("tmp", [P, MSGS, PART, D])
                idx_ready, idx_seen, released = sem("idx_ready"), sem("idx_seen"), sem("released")
                landed = [sem(f"landed{p}") for p in range(PARTS)]
                s_ready, turned, turned_out, mixed, used = (sem("s_ready"), sem("turned"), sem("turned_out"),
                                                            sem("mixed"), sem("used"))
                msg_ready, added, made = sem("msg_ready"), sem("added"), sem("made")
                meta_ready = sem("meta_ready")
                index_made, cleared, pe_seen = sem("index_made"), sem("cleared"), sem("pe_seen")
                if kind == "mlp":
                    rows = sb("rows", [P, PARTS, PART, ROW])
                    rows_in = [sem(f"rows_in{p}") for p in range(PARTS)]
                dl = (lambda p: mslot[:, p, :, 2]) if kind == "rel" else (lambda p: mslot[:, p, :, 1])
                AHEAD = PARTS if kind in ("mlp", "attend") else 0
                if kind == "gcn":
                    rank = sb("rank", [P, 2, PART])
                    rank_written = sem("rank_written")
                    lanes = sb("lanes", [P, PARTS, PART], BF16)
                    below = sb("below", [P, PARTS, PART, P])
                    pairs = sb("pairs", [P, T, 2], F16)
                    pairs_made = sem("pairs_made")
                if kind == "rel":
                    toh = sb("toh", [P, PARTS, PART, 3 * 32], BF16)
                if kind in ("score", "attend"):
                    Sb = sb("Sb", [P, PARTS, PART, WN], BF16)
                    product_seen = sem("product_seen")
                    dsc = sb("dsc", [P, MSGS, PART, HEADS])
                    dmax = sb("dmax", [P, MSGS, PART, HEADS])
                    nodes_ready, shifted = sem("nodes_ready"), sem("shifted")
                    stored = [sem(f"stored{p}") for p in range(PARTS)]
                if kind == "score":
                    G = GROUP * PART
                    R = G * HEADS
                    GROUPS = NQ // GROUP
                    assert PARTS == 2 * GROUP and R <= P and HEADS * T <= 2 * NW * PITCH
                    dsel = sb("dsel", [P, 2, 2, G, HEADS])
                    dlT = sb("dlT", [R, 2, P])
                    first = sb("first", [R, 2, P + 1])
                    reset = sb("reset", [R, 2, P])
                    best = sb("best", [R, 2, P])
                    mrhs = sb("mrhs", [P, 2, G, HEADS + 1])
                    S8 = sb("S8", [P, 2, G, WN])
                    gap = sb("gap", [WN, 2, G])
                    window_of = sb("window_of", [WN, T])
                    window_reset = sb("window_reset", [WN, T])
                    off_f = sb("off_f", [1, T])
                    cand = acc[:, :, :].rearrange("p k c -> p (k c)")[:, 0:HEADS * T].rearrange("p (h t) -> p h t", h=HEADS)
                    off_ready, off_spread, link2 = sem("off_ready"), sem("off_spread"), sem("link2")
                    picked, lanes_turned, dl_out, scanned, back = (sem("picked"), sem("lanes_turned"), sem("dl_out"),
                                                                   sem("scanned"), sem("back"))
                    back_out, runs_ready, spread, kept, gap_ready = (sem("back_out"), sem("runs_ready"), sem("spread"),
                                                                     sem("kept"), sem("gap_ready"))
                    group = lambda g, p: g * 2 + p // GROUP
                    spread_at = lambda p: bank(6 + p // GROUP, WN, G * (HEADS + 1))
                WIDTH = {"mlp": D + 2, "gcn": D, "rel": D + 1, "attend": D + HEADS}.get(kind)
                rows_free = {"gcn": msg_ready, "score": used, "mlp": used, "rel": used, "attend": msg_ready}[kind]
                part = lambda g, p: g * PARTS + p
                tile = lambda g, p: bass.ds(g * PER_TURN + p * PART, PART)
                by_dst = by_lane(dst_rows)
                landing = 16 * (1 if kind == "attend" else PART)

                def summed_at(p, cols):
                    return PS[0:WN, (p % 2) * 512:(p % 2) * 512 + PART * 256].rearrange("n (k c) -> n k c", k=PART)[:, :, 0:cols]

                def turned_at(p, parts, cols=P):
                    return PS[0:parts, (2 + p % 2) * 512:(2 + p % 2) * 512 + PART * 256].rearrange("n (k c) -> n k c", k=PART)[:, :, 0:cols]

                def turned_b(p, parts, cols=P):
                    return PS[0:parts, (2 + p % 2) * 512:(2 + p % 2) * 512 + P].bitcast(BF16).rearrange("n (k c) -> n k c", k=PART)[:, :, 0:cols]

                def mixed_at(p, parts, cols):
                    return PS[0:parts, (4 + p % 2) * 512:(4 + p % 2) * 512 + PART * 256].rearrange("n (k c) -> n k c", k=PART)[:, :, 0:cols]

                with nc.Block() as block:
                    @block.gpsimd
                    def _(pool):
                        def gather(g, p):
                            pool.wait_ge(idx_ready, part(g, p) + 1)
                            pool.sem_inc(idx_seen, 1)
                            for k in range(PART):
                                pool.indirect_dma_start(
                                    out=gbuf[:, p, k, :], out_offset=None, in_=table,
                                    in_offset=bass.IndirectOffsetOnAxis(ap=slot[:, p, k:k + 1], axis=0)
                                ).then_inc(landed[p], 16)
                        def shift(g, p):
                            q = part(g, p)
                            pool.wait_ge(used, q + PARTS + 1)
                            pool.wait_ge(made, q + 1)
                            nc.gpsimd.tensor_tensor(dsc[:, p % MSGS, :, :], scores[:, tile(g, p), :], dmax[:, p % MSGS, :, :],
                                            ALU.subtract).then_inc(shifted, 1)

                        def weigh(g, p):
                            q = part(g, p)
                            pool.wait_ge(made, q + MSGS + 1)
                            pool.wait_ge(landed[p], (g + 1) * landing)
                            last = nc.gpsimd.tensor_tensor(
                                hm[:, p % MSGS, :, 0:D].rearrange("e k (h d) -> e k h d", h=HEADS),
                                gbuf[:, p, :, :].rearrange("e k (h d) -> e k h d", h=HEADS),
                                hm[:, p % MSGS, :, D:D + HEADS].unsqueeze(3).broadcast_to([P, PART, HEADS, HD]), ALU.mult)
                            last.then_inc(msg_ready, 1)

                        pipeline(pool, [(3, shift), (2, weigh)] if kind == "attend" else [(0, gather)])

                    @block.sync
                    def _(sp):
                        if kind == "mlp":
                            def fetch(g, p):
                                sp.wait_ge(turned, part(g, p) + 1)
                                sp.wait_ge(meta_ready, part(g, p) + 1)
                                sp.dma_start(rows[:, p, :, :], by_dst[:, tile(g, p), :]).then_inc(rows_in[p], 16)
                            pipeline(sp, [(0, fetch)])
                        if kind == "score":
                            def store_v(g, p):
                                sp.wait_ge(landed[p], (g + 1) * landing)
                                sp.dma_start(by_lane(edge_v)[:, tile(g, p), :], gbuf[:, p, :, D:2 * D]).then_inc(stored[p], 16)
                            for p in range(PARTS):
                                sp.sem_inc(stored[p], 16)
                            pipeline(sp, [(0, store_v)])
                            for p in range(PARTS):
                                sp.wait_ge(stored[p], (TURNS + 1) * 16)
                        if kind == "attend":
                            def fetch_v(g, p):
                                sp.wait_ge(msg_ready, part(g, p) + 1)
                                sp.dma_start(gbuf[:, p, :, :], by_lane(edge_v)[:, tile(g, p), :]).then_inc(landed[p], 16)
                            pipeline(sp, [(0, fetch_v)])

                    @block.scalar
                    def _(act):
                        if kind != "gcn":
                            act.sem_inc(turned_out, 2)
                        act.sem_inc(made, MSGS)
                        if AHEAD:
                            act.sem_inc(meta_ready, PARTS)
                        if kind not in ("mlp", "attend"):
                            act.wait_ge(index_made, 1)

                        def pick(g, p):
                            act.wait_ge(rows_free, part(g, p) + 1)
                            if kind == "score":
                                act.wait_ge(stored[p], g * 16 + 16)
                            if kind == "mlp":
                                act.wait_ge(rows_in[p], g * 16 + 16)
                                act.copy(slot[:, p, :], rows[:, p, :, A]).then_inc(idx_ready, 1)
                            else:
                                act.copy(slot[:, p, :], index[:, tile(g, p)]).then_inc(idx_ready, 1)

                        def pick_meta(g, p):
                            act.wait_ge(released, part(g, p) + 1)
                            if kind == "gcn":
                                act.copy(lanes[:, p, :], meta[:, tile(g, p), 1])
                            m = rows[:, p, :, A:ROW] if kind == "mlp" else meta[:, tile(g, p), :]
                            act.copy(mslot[:, p, :, :], m).then_inc(meta_ready, 1)

                        def evacuate(g, p):
                            q = part(g, p)
                            parts = {"mlp": A, "rel": 96}.get(kind, WN)
                            act.wait_ge(turned, q + (1 + AHEAD))
                            act.wait_ge(mixed, q + 1)
                            act.copy(lt[0:parts, p % 2, :, :], turned_at(p, parts) if kind == "mlp" else turned_b(p, parts)).then_inc(turned_out, 1)

                        def relu(g, p):
                            q = part(g, p)
                            act.wait_ge(used, q + PARTS + 1)
                            act.wait_ge(released, q + PARTS - MSGS + 1)
                            nc.scalar.activation(hm[:, p % MSGS, :, 0:D], tmp[:, p % MSGS, :, :], ACT.Relu)
                            act.copy(hm[:, p % MSGS, :, D], mslot[:, p, :, 2]).then_inc(made, 1)

                        def exponent(g, p):
                            q = part(g, p)
                            act.wait_ge(shifted, q + 1)
                            act.wait_ge(released, q + PARTS - MSGS + 1)
                            nc.scalar.activation(hm[:, p % MSGS, :, D:D + HEADS], dsc[:, p % MSGS, :, :], ACT.Exp,
                                                 scale=float(HD) ** -0.5).then_inc(made, 1)

                        def copy_nodes(g, p):
                            act.wait_ge(s_ready, part(g, p) + 1)
                            act.wait_ge(turned, part(g, p) + 1)
                            act.copy(Sb[:, p, :, :], S[:, p, :, :]).then_inc(nodes_ready, 1)

                        def weight_rows(g, p):
                            q = part(g, p)
                            act.wait_ge(landed[p], (g + 1) * landing)
                            act.wait_ge(meta_ready, q + 1)
                            act.wait_ge(released, q + PARTS - MSGS + 1)
                            for k in range(PART):
                                last = nc.scalar.activation(hm[:, p % MSGS, k, 0:D], gbuf[:, p, k, :], ACT.Copy,
                                                            scale=mslot[:, p, k, 2:3])
                            last.then_inc(msg_ready, 1)

                        def save_sorted(g, p):
                            act.wait_ge(mixed, part(g, p) + 3)
                            act.copy(tmeta[:, tile(g, p), :], mixed_at(p, P, 2)).then_inc(used, 1)

                        def pick_scores(g, p):
                            if p % GROUP < GROUP - 1:
                                return
                            n, s = group(g, p), p // GROUP
                            act.wait_ge(released, part(g, p) + PARTS + 1)
                            act.wait_ge(runs_ready, n * GROUP + GROUP)
                            t = bass.ds(n * G, G)
                            act.copy(dsel[:, s, 0, :, :], scores[:, t, :])
                            act.copy(dsel[:, s, 1, :, :], tmeta[:, t, 1].unsqueeze(2).broadcast_to([P, G, HEADS])).then_inc(picked, 1)

                        def evacuate_lanes(g, p):
                            if p % GROUP == GROUP - 1:
                                act.wait_ge(lanes_turned, group(g, p) + 1)
                                act.copy(dlT[:, p // GROUP, :], bank(0, R, P, P)).then_inc(dl_out, 1)

                        def evacuate_maxima(g, p):
                            if p % GROUP == GROUP - 1:
                                act.wait_ge(back, group(g, p) + 1)
                                act.wait_ge(kept, group(g, p) + 1)
                                act.copy(mrhs[:, p // GROUP, :, 0:HEADS],
                                         bank(1, P, R).rearrange("e (t h) -> e t h", t=G)).then_inc(back_out, 1)

                        if kind == "score":
                            act.wait_ge(cleared, 2)
                            act.sem_inc(back_out, 1)

                        if kind == "mlp":
                            pipeline(act, [(8, pick), (6, pick_meta), (4, evacuate), (2, relu)])
                        elif kind == "gcn":
                            act.sem_inc(used, PARTS)
                            act.wait_ge(cleared, 1)
                            act.sem_inc(msg_ready, PARTS)
                            pipeline(act, [(8, pick), (6, pick_meta), (3, weight_rows), (2, save_sorted)])
                        elif kind == "score":
                            pipeline(act, [(18, pick), (16, pick_meta), (14, evacuate), (11, pick_scores), (9, evacuate_lanes),
                                           (6, evacuate_maxima)])
                        elif kind == "rel":
                            pipeline(act, [(8, pick), (6, pick_meta), (4, evacuate)])
                        else:
                            pipeline(act, [(9, pick_meta), (7, copy_nodes), (6, evacuate), (3, exponent)])

                    @block.tensor
                    def _(pe):
                        pe.sem_inc(mixed, 2)
                        if AHEAD:
                            pe.sem_inc(turned, PARTS)
                        if kind != "score":
                            pe.sem_inc(released, PARTS)
                        if kind == "rel":
                            pe.wait_ge(cleared, 1)
                        if kind == "gcn":
                            pe.wait_ge(pairs_made, 2)

                        def turn(g, p):
                            q = part(g, p)
                            pe.wait_ge(turned_out, q + 1)
                            if kind == "mlp":
                                pe.wait_ge(rows_in[p], g * 16 + 16)
                                pe.sem_inc(pe_seen, 1)
                            else:
                                pe.wait_ge(nodes_ready if kind == "attend" else s_ready, q + 1)
                            for k in range(PART):
                                if kind == "mlp":
                                    last = nc.tensor.transpose(turned_at(p, A)[:, k, :], rows[:, p, k, 0:A], ident[:, :])
                                elif kind == "rel":
                                    last = nc.tensor.transpose(turned_b(p, 96)[:, k, :], toh[:, p, k, :], ident_b[:, :])
                                else:
                                    last = nc.tensor.transpose(turned_b(p, WN)[:, k, :], Sb[:, p, k, :], ident_b[:, :])
                            last.then_inc(turned, 1)

                        def spread_keys(g, p):
                            pe.wait_ge(turned_out, part(g, p) + 1)
                            pe.wait_ge(meta_ready, part(g, p) + 1)
                            for k in range(PART):
                                o = turned_at(p, P)[:, k, :]
                                nc.tensor.matmul(o, lanes[:, p, k:k + 1].broadcast_to([P, P]), ident128[:, :], start=True, stop=False)
                                last = nc.tensor.matmul(o, ones_b[:, :], lane_diag[:, :], start=False, stop=True)
                            last.then_inc(turned, 1)

                        regs = [pe.alloc_register(f"{name}_pe_window{i}") for i in range(MSGS * PART)]

                        def mix(g, p):
                            q = part(g, p)
                            if kind in ("score", "attend") and p % MSGS == 0:
                                pe.load(regs, off[0:1, bass.ds(g * PER_TURN + p * PART, MSGS * PART)])
                            at = [pe.snap(regs[p % MSGS * PART + k], min_val=0, max_val=(NW - 1) * PITCH) for k in range(PART)] if kind in ("score", "attend") else None
                            pe.wait_ge(turned_out, q + 3)
                            pe.wait_ge(used, q + PARTS - 1)
                            for k in range(PART):
                                lhs = lt[:, p % 2, k, :]
                                if kind == "mlp":
                                    last = nc.tensor.matmul(mixed_at(p, P, D)[:, k, :], lhs[0:A, :], W1b[:, :], start=True, stop=True)
                                elif kind == "rel":
                                    last = nc.tensor.matmul(mixed_at(p, P, D)[:, k, :], lhs[0:96, :], relS[:, :], start=True, stop=True)
                                elif kind == "gcn":
                                    last = nc.tensor.matmul(mixed_at(p, P, 2)[:, k, :], lhs,
                                                            pairs[:, bass.ds(g * PER_TURN + p * PART + k, 1), :].rearrange("e k c -> e (k c)"),
                                                            start=True, stop=True)
                                elif kind == "score":
                                    for i in range(3):
                                        last = nc.tensor.matmul(mixed_at(p, P, D)[:, k, :], lhs[0:WN, :],
                                                                QM3[:, i, bass.ds(at[k], D)], start=(i == 0), stop=(i == 2))
                                else:
                                    last = nc.tensor.matmul(mixed_at(p, P, 3 * HEADS)[:, k, :], lhs[0:WN, :],
                                                            QM3[:, :, bass.ds(at[k] + D, HEADS)], start=True, stop=True)
                            last.then_inc(mixed, 1)

                        def total(g, p):
                            q = part(g, p)
                            pe.wait_ge(s_ready, q + 1)
                            pe.wait_ge(added, q * 2 + 2)
                            if kind == "mlp":
                                pe.wait_ge(made, q + MSGS + 1)
                            elif kind == "rel":
                                pe.wait_ge(used, q + PARTS + 1)
                            else:
                                pe.wait_ge(msg_ready, q + PARTS + 1)
                            for k in range(PART):
                                rhs = hm[:, p % MSGS, k, 0:WIDTH]
                                last = nc.tensor.matmul(summed_at(p, WIDTH)[:, k, :], S[:, p, k, :], rhs, start=True, stop=True)
                            last.then_inc(released, 1)

                        def turn_scores(g, p):
                            if p % GROUP < GROUP - 1:
                                return
                            n, s = group(g, p), p // GROUP
                            pe.wait_ge(scanned, n + 1)
                            pe.sem_inc(pe_seen, 1)
                            pe.wait_ge(picked, n + 1)
                            pe.sem_inc(pe_seen, 1)
                            nc.tensor.transpose(bank(0, R, P), dsel[:, s, 0, :, :].rearrange("e t h -> e (t h)"), ident[:, :])
                            nc.tensor.transpose(bank(0, R, P, P), dsel[:, s, 1, :, :].rearrange("e t h -> e (t h)"),
                                                ident[:, :]).then_inc(lanes_turned, 1)

                        def turn_back(g, p):
                            if p % GROUP < GROUP - 1:
                                return
                            n, s = group(g, p), p // GROUP
                            pe.wait_ge(back_out, n + 1)
                            pe.sem_inc(pe_seen, 1)
                            pe.wait_ge(scanned, n + 2)
                            pe.sem_inc(pe_seen, 1)
                            nc.tensor.transpose(bank(1, P, R), best[:, s, :], ident[0:R, 0:R]).then_inc(back, 1)

                        def spread_maxima(g, p):
                            n, s = group(g, p), p // GROUP
                            pe.wait_ge(back_out, n + 2)
                            pe.wait_ge(kept, n + 1)
                            pe.wait_ge(runs_ready, part(g, p) + (1 + 2 * GROUP))
                            for i in range(p % GROUP * PART, (p % GROUP + 1) * PART):
                                last = nc.tensor.matmul(spread_at(p)[:, i * (HEADS + 1):(i + 1) * (HEADS + 1)], S8[:, s, i, :],
                                                        mrhs[:, s, i, :], start=True, stop=True)
                            last.then_inc(spread, 1)

                        if kind == "score":
                            pe.wait_ge(off_ready, 1)
                            nc.tensor.matmul(bank(7, WN, T), ones[0:1, 0:WN], off_f[:, :], start=True, stop=True).then_inc(off_spread, 1)

                        pipeline(pe, {"mlp": [(4, turn), (3, mix), (1, total)], "rel": [(4, turn), (3, mix), (1, total)],
                                      "gcn": [(4, spread_keys), (2, mix), (1, total)], "score": [(14, turn), (13, mix), (10, turn_scores), (7, turn_back), (1, spread_maxima)],
                                      "attend": [(6, turn), (5, mix), (1, total)]}[kind])

                    @block.vector
                    def _(dve):
                        v = nc.vector
                        if kind not in ("mlp", "attend"):
                            v.tensor_scalar(index[:, :], meta[:, :, 0], 2048.0 if meta is tmeta else 0.0, None,
                                            ALU.add).then_inc(index_made, 1)
                        if kind == "gcn":
                            v.tensor_scalar(pairs[:, :, 0], meta[:, 0:T, 0], -2048.0, None, ALU.add).then_inc(pairs_made, 1)
                            v.tensor_copy(pairs[:, :, 1], meta[:, 0:T, 1]).then_inc(pairs_made, 1)
                        if kind == "score":
                            v.memset(first[:, :, :], 1.0).then_inc(cleared, 1)
                            v.memset(mrhs[:, :, :, :], 1.0).then_inc(cleared, 1)
                            v.tensor_copy(off_f[:, :], off[:, :]).then_inc(off_ready, 1)
                            dve.wait_ge(off_spread, 1)
                            link = Chain(dve, link2)
                            link(v.tensor_copy(window_of[:, :], bank(7, WN, T)))
                            link(v.memset(window_reset[:, 0:1], 1.0))
                            link(v.tensor_tensor(window_reset[:, 1:T], window_of[:, 1:T], window_of[:, 0:T - 1], ALU.not_equal))
                            link(v.tensor_scalar(window_reset[:, :], window_reset[:, :], -BIG, None, ALU.mult))
                            dve.sem_inc(kept, 2)
                            dve.sem_inc(runs_ready, 2 * GROUP)
                            dve.sem_inc(scanned, 1)
                        else:
                            v.memset(hm[:, :, :, :], 1.0).then_inc(cleared, 1)
                            v.memset(acc[:, :, :], 0.0).then_inc(cleared, 1)
                            dve.sem_inc(added, 4)
                        dve.wait_ge(cleared, 2)
                        if kind != "gcn":
                            dve.sem_inc(used, PARTS)
                        if kind == "gcn":
                            dve.sem_inc(turned_out, 2)
                        if kind == "score":
                            dve.sem_inc(released, PARTS)
                        if kind == "attend":
                            dve.sem_inc(msg_ready, PARTS)

                        def one_hot(g, p):
                            q = part(g, p)
                            dve.wait_ge(released, q + 1)
                            dve.wait_ge(meta_ready, q + (1 + AHEAD))
                            if kind == "mlp":
                                v.tensor_copy(dmeta[:, tile(g, p), :], mslot[:, p, :, :])
                            last = v.tensor_tensor((Sb if kind == "score" else S)[:, p, :, :], iota1[:, 0:WN].unsqueeze(1).broadcast_to([P, PART, WN]),
                                                   dl(p).unsqueeze(2).broadcast_to([P, PART, WN]), ALU.is_equal)
                            if kind == "rel":
                                last = v.tensor_tensor(toh[:, p, :, :].rearrange("e k (c r) -> e k c r", c=3),
                                                       iota[:, 0:32].unsqueeze(1).unsqueeze(1).broadcast_to([P, PART, 3, 32]),
                                                       mslot[:, p, :, 1:2].unsqueeze(2).broadcast_to([P, PART, 3, 32]), ALU.is_equal)
                            last.then_inc(s_ready, 1)

                        def sort_tile(g, p):
                            q = part(g, p)
                            dve.wait_ge(turned, q + 1)
                            for k in range(PART):
                                last = v.tensor_scalar(below[:, p, k, :], turned_at(p, P)[:, k, :], mslot[:, p, k, 3:4], 0.0,
                                                       ALU.is_lt, ALU.add, accum_out=rank[:, p % 2, k:k + 1])
                            last.then_inc(rank_written, 1)
                            dve.wait_ge(rank_written, q + 1)
                            dve.wait_ge(mixed, q + 1)
                            v.tensor_tensor(lt[:, p % 2, :, :], iota[:, :].unsqueeze(1).broadcast_to([P, PART, P]),
                                            rank[:, p % 2, :].unsqueeze(2).broadcast_to([P, PART, P]),
                                            ALU.is_equal).then_inc(turned_out, 1)

                        def add_gathered(g, p):
                            q = part(g, p)
                            dve.wait_ge(mixed, q + 3)
                            dve.wait_ge(landed[p], (g + 1) * landing)
                            dve.wait_ge(made, q + 1)
                            v.tensor_tensor(tmp[:, p % MSGS, :, :], mixed_at(p, P, D), gbuf[:, p, :, :], ALU.add).then_inc(used, 1)

                        def times_relation(g, p):
                            q = part(g, p)
                            dve.wait_ge(mixed, q + 3)
                            dve.wait_ge(landed[p], (g + 1) * landing)
                            dve.wait_ge(released, q + PARTS - MSGS + 1)
                            v.tensor_tensor(hm[:, p % MSGS, :, 0:D], mixed_at(p, P, D), gbuf[:, p, :, 0:D], ALU.mult).then_inc(used, 1)

                        def score(g, p):
                            q = part(g, p)
                            dve.wait_ge(mixed, q + 3)
                            dve.wait_ge(landed[p], (g + 1) * landing)
                            v.tensor_tensor(tmp[:, p % MSGS, :, :], mixed_at(p, P, D), gbuf[:, p, :, 0:D], ALU.mult).then_inc(used, 1)
                            dve.wait_ge(used, q + PARTS + 1)
                            dve.sem_inc(product_seen, 1)
                            v.tensor_reduce(scores[:, tile(g, p), :],
                                            tmp[:, p % MSGS, :, :].rearrange("e k (h d) -> e k h d", h=HEADS),
                                            AX.X, ALU.add).then_inc(released, 1)

                        def join_greatest(g, p):
                            dve.wait_ge(mixed, part(g, p) + 3)
                            v.tensor_reduce(dmax[:, p % MSGS, :, :], mixed_at(p, P, 3 * HEADS).rearrange("e k (i h) -> e k h i", i=3),
                                            AX.X, ALU.add).then_inc(used, 1)

                        regs = [dve.alloc_register(f"{name}_dve_window{i}") for i in range(MSGS * PART)]
                        at = []

                        def add_up(g, p):
                            q = part(g, p)
                            if p % MSGS == 0:
                                dve.load(regs, off[0:1, bass.ds(g * PER_TURN + p * PART, MSGS * PART)])
                                at[:] = [dve.snap(r, min_val=0, max_val=(NW - 1) * PITCH) for r in regs]
                            dve.wait_ge(released, q + PARTS + 1)
                            for k in range(PART):
                                dve.wait_ge(added, q * 2 + (k + 3))
                                a = acc[:, k, bass.ds(at[p % MSGS * PART + k], WIDTH)]
                                v.tensor_tensor(a, summed_at(p, WIDTH)[:, k, :], a, ALU.add).then_inc(added, 1)

                        def scan(g, p):
                            if p % GROUP < GROUP - 1:
                                return
                            n, s = group(g, p), p // GROUP
                            dve.wait_ge(dl_out, n + 1)
                            v.tensor_tensor(first[:, s, 1:P], dlT[:, s, 1:P], dlT[:, s, 0:P - 1], ALU.not_equal).then_inc(link2, 1)
                            dve.wait_ge(link2, n * 3 + 5)
                            v.tensor_scalar(reset[:, s, :], first[:, s, 0:P], -BIG, None, ALU.mult).then_inc(link2, 1)
                            dve.wait_ge(link2, n * 3 + 6)
                            v.tensor_tensor_scan(best[:, s, :], reset[:, s, :], bank(0, R, P), 0.0, ALU.add,
                                                 ALU.max).then_inc(link2, 1)
                            dve.wait_ge(link2, n * 3 + 7)
                            v.tensor_tensor(best[:, s, :], best[:, s, :], first[:, s, 1:P + 1], ALU.mult).then_inc(scanned, 1)

                        def run_nodes(g, p):
                            s, t = p // GROUP, slice(p % GROUP * PART, (p % GROUP + 1) * PART)
                            v.tensor_tensor(S8[:, s, t, :], iota1[:, 0:WN].unsqueeze(1).broadcast_to([P, PART, WN]),
                                            dsel[:, s, 1, t, 0].unsqueeze(2).broadcast_to([P, PART, WN]),
                                            ALU.is_equal).then_inc(runs_ready, 1)

                        def keep_best(g, p):
                            if p % GROUP < GROUP - 1:
                                return
                            n, s = group(g, p), p // GROUP
                            dve.wait_ge(spread, (n + 1) * GROUP)
                            m = spread_at(p).rearrange("n (t c) -> n c t", t=G)
                            v.tensor_scalar(gap[:, s, :], m[:, HEADS, :], 1.0, -1.0, ALU.min, ALU.add).then_inc(gap_ready, 1)
                            dve.wait_ge(gap_ready, n + 1)
                            v.scalar_tensor_tensor(out=cand[:, :, bass.ds(n * G, G)],
                                                   in0=gap[:, s, :].unsqueeze(1).broadcast_to([WN, HEADS, G]),
                                                   scalar=BIG, in1=m[:, 0:HEADS, :], op0=ALU.mult, op1=ALU.add).then_inc(kept, 1)

                        pipeline(dve, {"mlp": [(5, one_hot), (2, add_gathered), (0, add_up)],
                                       "gcn": [(5, one_hot), (3, sort_tile), (0, add_up)],
                                       "rel": [(5, one_hot), (2, times_relation), (0, add_up)],
                                       "score": [(15, one_hot), (12, score), (8, scan), (3, run_nodes), (0, keep_best)],
                                       "attend": [(8, one_hot), (4, join_greatest), (0, add_up)]}[kind])

                        if kind == "score":
                            dve.wait_ge(kept, GROUPS + 2)
                            greatest = Chain(dve, cleared)
                            greatest.n = 2
                            for h in range(HEADS):
                                greatest(v.tensor_tensor_scan(cand[:, h, :], window_reset[:, :], cand[:, h, :], 0.0, ALU.add, ALU.max))
                            with dve.Fori(0, NW // 5) as g:
                                dve.load(regs[0:5], last_tile[0:1, bass.ds(g * 5, 5)])
                                ends = [dve.snap(r, min_val=0, max_val=T - 1) for r in regs[0:5]]
                                for i in range(5):
                                    v.tensor_copy(qmw[:, bass.ds(g * 5 + i, 1), D:D + HEADS],
                                                  cand[:, :, bass.ds(ends[i], 1)].rearrange("p h t -> p t h")).then_inc(gap_ready, 1)
                            dve.wait_ge(gap_ready, GROUPS + NW)
                            split_columns(greatest, slice(0, NW), D, D + HEADS, aux[:, :, 0:HEADS])

        def first_norm(dve, link, squared, rooted):
            layernorm_relu(dve, link, squared, rooted, 1)

        product("rows0", H, W1a[:, :], D, first_norm, lambda act, s, r: (squares(act, s, r), root(act, s, r, 1)),
                lambda g, rows, _: nc.vector.tensor_tensor(
                    aux[:, bass.ds(g * BATCH, BATCH), :], rows,
                    vecs[:, 6, :].unsqueeze(1).broadcast_to([WN, BATCH, D]), ALU.add),
                lambda w, _: [(by_window(tab_p)[:, w, :], aux[:, w, :])])
        edge_pass("mlp", tab_p, None, off_d, "layer0")

        with stage("update0") as (sb, sem):
            agg = sb("agg", [WN, BATCH, D + 2])
            st = sb("st", [WN, BATCH, D])
            aT, hT, uT = (sb(n, [D, BATCH, WN]) for n in ("aT", "hT", "uT"))
            cT = sb("cT", [1, BATCH, WN])
            agg_ready, st_ready, turned, a_out, h_out = (sem("agg_ready"), sem("st_ready"), sem("turned"), sem("a_out"),
                                                         sem("h_out"))
            mixed1, relu_out, mixed0, added = sem("mixed1"), sem("relu_out"), sem("mixed0"), sem("added")
            keyed, deg_kept = sem("keyed"), sem("deg_kept")
            with nc.Block() as block:
                @block.vector
                def _(dve):
                    v = nc.vector
                    v.tensor_scalar(dmeta[:, 0:T, 3], dmeta[:, 0:T, 1], float(P), lane[:, 0:1], ALU.mult, ALU.add).then_inc(keyed, 1)
                    v.tensor_tensor(X[:, :, :], X[:, :, :], over_nodes(vecs[:, 7, :]), ALU.add).then_inc(added, 1)

                    def add_halves(g):
                        w = bass.ds(g * BATCH, BATCH)
                        v.tensor_tensor(agg[:, :, :], accw[0][:, w, 0:D + 2], accw[1][:, w, 0:D + 2], ALU.add).then_inc(agg_ready, 1)
                        dve.wait_ge(agg_ready, g + 1)
                        v.tensor_copy(deg[:, w], agg[:, :, D]).then_inc(deg_kept, 1)

                    def evacuate_h(g):
                        dve.wait_ge(turned, g + 1)
                        v.tensor_copy(hT[:, :, :], banks(3, 256, BATCH, D, WN)).then_inc(h_out, 1)

                    def add_update(g):
                        w = bass.ds(g * BATCH, BATCH)
                        dve.wait_ge(mixed0, g + 1)
                        dve.wait_ge(added, g + 1)
                        v.tensor_tensor(X[:, w, :], X[:, w, :], banks(0, 256, BATCH, WN, D), ALU.add).then_inc(added, 1)

                    add_halves(0)
                    with dve.Fori(0, NW // BATCH - 1) as g:
                        evacuate_h(g)
                        dve.wait_ge(deg_kept, g + 1)
                        add_halves(g + 1)
                        add_update(g)
                    evacuate_h(NW // BATCH - 1)
                    add_update(NW // BATCH - 1)

                @block.scalar
                def _(act):
                    def pick_h(g):
                        act.copy(st[:, :, :], H[:, bass.ds(g * BATCH, BATCH), :]).then_inc(st_ready, 1)

                    def evacuate_sums(g):
                        act.wait_ge(turned, g + 1)
                        act.copy(aT[:, :, :], banks(0, 256, BATCH, D, WN)).then_inc(a_out, 1)
                        act.copy(cT[:, :, :], banks(6, 128, BATCH, 1, WN)).then_inc(a_out, 1)

                    def relu_out_of_psum(g):
                        act.wait_ge(mixed1, g + 1)
                        nc.scalar.activation(uT[:, :, :], banks(3, 256, BATCH, D, WN), ACT.Relu, bias=c1col[:, 0:1]).then_inc(relu_out, 1)

                    pick_h(0)
                    with act.Fori(0, NW // BATCH - 1) as g:
                        evacuate_sums(g)
                        pick_h(g + 1)
                        relu_out_of_psum(g)
                    evacuate_sums(NW // BATCH - 1)
                    relu_out_of_psum(NW // BATCH - 1)

                @block.tensor
                def _(pe):
                    with pe.Fori(0, NW // BATCH) as g:
                        pe.wait_ge(agg_ready, g + 1)
                        pe.wait_ge(st_ready, g + 1)
                        pe.wait_ge(added, g + 1)
                        for i in range(BATCH):
                            nc.tensor.transpose(bank(0, D, WN, i * 256), agg[:, i, 0:D], ident[0:WN, 0:WN])
                            nc.tensor.transpose(bank(3, D, WN, i * 256), st[:, i, :], ident[0:WN, 0:WN])
                            last = nc.tensor.transpose(bank(6, 1, WN, i * 128), agg[:, i, D + 1:D + 2], ident[0:WN, 0:WN])
                        last.then_inc(turned, 1)
                        pe.wait_ge(a_out, g * 2 + 2)
                        pe.wait_ge(h_out, g + 1)
                        for i in range(BATCH):
                            o = bank(3, D, WN, i * 256)
                            nc.tensor.matmul(o, U1a[:, :], hT[:, i, :], start=True, stop=False)
                            nc.tensor.matmul(o, W2U[:, :], aT[:, i, :], start=False, stop=False)
                            last = nc.tensor.matmul(o, b2U[:, :], cT[:, i, :], start=False, stop=True)
                        last.then_inc(mixed1, 1)
                        pe.wait_ge(relu_out, g + 1)
                        for i in range(BATCH):
                            last = nc.tensor.matmul(bank(0, WN, D, i * 256), uT[:, i, :], U2s[:, :], start=True, stop=True)
                        last.then_inc(mixed0, 1)

        def second_norm(dve, link, squared, rooted):
            v = nc.vector
            layernorm_relu(dve, link, squared, rooted, 1)
            link(v.tensor_scalar(deg, deg, 1.0, None, ALU.add))
            v.tensor_scalar(var, deg, 1.0e-30, None, ALU.max).then_inc(squared[0], 1)
            dve.wait_ge(rooted[0], 2)
            link(v.reciprocal(rstd, std))
            link(v.scalar_tensor_tensor(out=dinv, in0=deg, scalar=0.0, in1=rstd, op0=ALU.is_gt, op1=ALU.mult))

        product("rows1", H, gWs[:, :], D, second_norm, lambda act, s, r: (squares(act, s, r), root(act, s, r, 1), root(act, s, r, 2)),
                lambda g, rows, _: nc.vector.tensor_tensor(
                    aux[:, bass.ds(g * BATCH, BATCH), :], rows,
                    dinv[:, bass.ds(g * BATCH, BATCH)].unsqueeze(2).broadcast_to([WN, BATCH, D]), ALU.mult),
                lambda w, _: [(by_window(tab_h)[:, w, :], aux[:, w, :])])
        edge_pass("gcn", tab_h, dmeta, off_d, "layer1")

        with stage("update1") as (sb, sem):
            link_sem, squared, rooted, summed = sem("link"), (sem("squared"), sem("centred")), (sem("rooted"), sem("squares")), sem("summed")
            elu_in, elu_out, col_in, stored, done = sem("elu_in"), sem("elu_out"), sem("col_in"), sem("stored"), sem("done")
            brow = sb("brow", [WN, 4, D])
            with nc.Block() as block:
                @block.vector
                def _(dve):
                    link = Chain(dve, link_sem)
                    v = nc.vector
                    h, a = H[:, :, :], aux[:, :, :]
                    link(v.tensor_tensor(h, accw[0][:, :, 0:D], accw[1][:, :, 0:D], ALU.add))
                    link(v.tensor_tensor(h, h, a, ALU.add))
                    link(v.tensor_tensor(h, h, over_windows(dinv), ALU.mult))
                    link(v.tensor_tensor(h, h, over_nodes(vecs[:, 0, :]), ALU.add))
                    v.tensor_scalar(a, h, 0.0, None, ALU.min).then_inc(elu_in, 1)
                    dve.wait_ge(elu_out, 1)
                    link(v.scalar_tensor_tensor(out=h, in0=h, scalar=0.0, in1=a, op0=ALU.max, op1=ALU.add))
                    v.tensor_scalar(h, h, -1.0, None, ALU.add).then_inc(col_in, 1)
                    dve.wait_ge(summed, 1)
                    link(v.tensor_scalar(brow[:, 0, :], bank(0, WN, D), 1.0 / N, None, ALU.mult))
                    link(v.tensor_tensor(a, h, over_nodes(brow[:, 0, :]), ALU.subtract))
                    v.tensor_tensor(h, a, a, ALU.mult).then_inc(col_in, 1)
                    dve.wait_ge(summed, 2)
                    v.tensor_scalar(brow[:, 1, :], bank(1, WN, D), 1.0 / N, 1e-5, ALU.mult, ALU.add).then_inc(squared[0], 1)
                    dve.wait_ge(rooted[0], 1)
                    link(v.reciprocal(brow[:, 3, :], brow[:, 2, :]))
                    link(v.tensor_tensor(brow[:, 3, :], brow[:, 3, :], vecs[:, 1, :], ALU.mult))
                    link(v.tensor_tensor(a, a, over_nodes(brow[:, 3, :]), ALU.mult))
                    link(v.tensor_tensor(a, a, over_nodes(vecs[:, 2, :]), ALU.add))
                    normalise(dve, link, squared, rooted, 2, a)
                    link(v.tensor_tensor(a, a, over_windows(rstd), ALU.mult))
                    link(v.tensor_tensor(a, a, over_nodes(vecs[:, 3, :]), ALU.mult))
                    link(v.tensor_tensor(a, a, over_nodes(vecs[:, 4, :]), ALU.add))
                    link(v.tensor_tensor(X[:, :, :], X[:, :, :], a, ALU.add))
                    layernorm_relu(dve, link, squared, rooted, 3, 1)
                    link(v.tensor_tensor(X[:, :, :], X[:, :, :], H[:, :, :], ALU.add))
                    dve.sem_inc(done, 1)

                @block.scalar
                def _(act):
                    act.wait_ge(elu_in, 1)
                    nc.scalar.activation(aux[:, :, :], aux[:, :, :], ACT.Exp).then_inc(elu_out, 1)
                    act.wait_ge(squared[0], 1)
                    nc.scalar.activation(brow[:, 2, :], brow[:, 1, :], ACT.Sqrt).then_inc(rooted[0], 1)
                    for m in range(2):
                        squares(act, squared, rooted, m)
                        root(act, squared, rooted, m + 2)

                @block.tensor
                def _(pe):
                    for k in range(2):
                        pe.wait_ge(col_in, k + 1)
                        for w in range(NW):
                            last = nc.tensor.matmul(bank(k, WN, D), ones[0:WN, 0:WN], H[:, w, :], start=(w == 0), stop=(w == NW - 1))
                        last.then_inc(summed, 1)

                @block.sync
                def _(sp):
                    sp.wait_ge(done, 1)
                    sp.dma_start(by_window(tab_x0), H[:, :, :]).then_inc(stored, 16)
                    sp.wait_ge(stored, 16)

        def hop_end(title, last_hop, table_out):
            with stage(title) as (sb, sem):
                link_sem, squared, rooted, stored, done = sem("link"), (sem("squared"), sem("centred")), (sem("rooted"), sem("squares")), sem("stored"), sem("done")
                with nc.Block() as block:
                    @block.vector
                    def _(dve):
                        link = Chain(dve, link_sem)
                        v = nc.vector
                        a = aux[:, :, :]
                        for h in HALVES:
                            v.tensor_tensor(aux[:, h, :], accw[0][:, h, 0:D], accw[1][:, h, 0:D], ALU.add).then_inc(squared[1], 1)
                        link(v.tensor_tensor(denom, accw[0][:, :, D], accw[1][:, :, D], ALU.add))
                        link(v.tensor_scalar(denom, denom, 1.0, None, ALU.max))
                        link(v.reciprocal(rstd, denom))
                        for i, h in enumerate(HALVES):
                            dve.wait_ge(rooted[1], i + 1)
                            last = v.tensor_reduce(var[:, h], H[:, h, :], AX.X, ALU.add)
                        last.then_inc(squared[0], 1)
                        dve.wait_ge(rooted[0], 1)
                        link(v.tensor_tensor(std, std, rstd, ALU.mult))
                        link(v.tensor_scalar(std, std, 1e-12, None, ALU.max))
                        link(v.reciprocal(std, std))
                        link(v.tensor_tensor(rstd, rstd, std, ALU.mult))
                        link(v.tensor_tensor(a, a, over_windows(rstd), ALU.mult))
                        dve.sem_inc(done, 1)
                        v.tensor_tensor(X[:, :, :], X[:, :, :], a, ALU.add)

                    @block.scalar
                    def _(act):
                        squares(act, squared, rooted)
                        root(act, squared, rooted, 1)

                    @block.sync
                    def _(sp):
                        if not last_hop:
                            sp.wait_ge(done, 1)
                            sp.dma_start(by_window(table_out), aux[:, :, :]).then_inc(stored, 16)
                            sp.wait_ge(stored, 16)

        for i, (t_in, t_out) in enumerate(((tab_x0, tab_x1), (tab_x1, tab_x2), (tab_x2, None))):
            edge_pass("rel", t_in, smeta, off_s, f"hop{i}")
            hop_end(f"end{i}", i == 2, t_out)

        def split_qkv(g, rows, spare):
            w = bass.ds(g * BATCH, BATCH)
            for i, o in enumerate((qmw[:, w, 0:D], aux[:, w, :], spare[:, w, :])):
                last = nc.vector.tensor_tensor(o, rows[:, :, i * D:(i + 1) * D],
                                               qkvb[:, i * D:(i + 1) * D].unsqueeze(1).broadcast_to([WN, BATCH, D]), ALU.add)
            return last

        def split_columns(link, w, lo, hi, rest):
            v = nc.vector
            link(v.tensor_copy(qm3w[0][:, w, lo:hi], qmw[:, w, lo:hi]))
            link(v.tensor_tensor(rest, qmw[:, w, lo:hi], qm3w[0][:, w, lo:hi], ALU.subtract))
            link(v.tensor_copy(qm3w[1][:, w, lo:hi], rest))
            link(v.tensor_tensor(rest, rest, qm3w[1][:, w, lo:hi], ALU.subtract))
            link(v.tensor_copy(qm3w[2][:, w, lo:hi], rest))

        def split_queries(dve, g, finished, after_sem):
            dve.wait_ge(finished, g + 2)
            done = [0]

            def link(ins):
                done[0] += 1
                ins.then_inc(after_sem, 1)
                dve.wait_ge(after_sem, g * 5 + done[0])
            w = bass.ds(g * BATCH, BATCH)
            split_columns(link, w, 0, D, H[:, w, :])

        product("qkv", H, qkvT[:, :], 3 * D, first_norm, lambda act, s, r: (squares(act, s, r), root(act, s, r, 1)), split_qkv,
                lambda w, spare: [(by_window(tab_kv)[:, w, 0:D], aux[:, w, :]),
                                  (by_window(tab_kv)[:, w, D:2 * D], spare[:, w, :])],
                split_queries)
        edge_pass("score", tab_kv, tmeta, off_d, "scores")
        edge_pass("attend", None, tmeta, off_d, "attend")

        def last_rows(dve, link, squared, rooted):
            v = nc.vector
            link(v.tensor_tensor(aux[:, :, :], accw[0][:, :, 0:D], accw[1][:, :, 0:D], ALU.add))
            den = H[:, :, 0:HEADS]
            link(v.tensor_tensor(den, accw[0][:, :, D:D + HEADS], accw[1][:, :, D:D + HEADS], ALU.add))
            link(v.tensor_scalar(den, den, 1.0e-30, None, ALU.max))
            link(v.reciprocal(den, den))
            for h in range(HEADS):
                a = aux[:, :, h * HD:(h + 1) * HD]
                link(v.tensor_tensor(a, a, den[:, :, h:h + 1].broadcast_to([WN, NW, HD]), ALU.mult))
            link(v.tensor_tensor(X[:, :, :], X[:, :, :], over_nodes(vecs[:, 5, :]), ALU.add))

        def add_rows(g, rows, _):
            w = bass.ds(g * BATCH, BATCH)
            return nc.vector.tensor_tensor(X[:, w, :], X[:, w, :], rows, ALU.add)

        product("output", aux, outT[:, :], D, last_rows, lambda act, s, r: None, add_rows,
                lambda w, _: [(by_window(out)[:, w, :], X[:, w, :])])


_INS = ['x', 'src', 'dst', 'edge_attr_64', 'edge_type_20', 'edge_weight', 'L0_gnn_W1', 'L0_gnn_b1', 'L0_gnn_W2',
        'L0_gnn_b2', 'L0_gnn_U1', 'L0_gnn_c1', 'L0_gnn_U2', 'L0_gnn_c2', 'L1_gnn_W', 'L1_gnn_b', 'L1_gnn_bn_gamma',
        'L1_gnn_bn_beta', 'L1_gnn_ln_gamma', 'L1_gnn_ln_beta', 'L2_gnn_relation_embed', 'L3_gnn_qkv_w',
        'L3_gnn_qkv_b', 'L3_gnn_out_w', 'L3_gnn_out_b']


def kernel(**inputs):
    import numpy as _np
    import concourse.bacc as _bacc
    from concourse import mybir as _mybir
    from concourse.bass_utils import run_bass_kernel_spmd as _run

    nc = _bacc.Bacc("TRN2", target_bir_lowering=False, num_devices=1)
    arrays, args = {}, []
    for name in _INS:
        a = _np.ascontiguousarray(inputs[name])
        arrays[f"in_{name}_dram"] = a
        args.append(nc.dram_tensor(f"in_{name}_dram", a.shape, _mybir.dt.from_np(a.dtype), kind="ExternalInput").ap())
    args.append(nc.dram_tensor("out_0_dram", (3125, 128), _mybir.dt.float32, kind="ExternalOutput").ap())
    program(nc, *args)
    r = _run(nc, [arrays], core_ids=[0])
    return r.results[0]["out_0_dram"]
```
